# Optimizing a Trainium2 kernel written in Bass

```python
import numpy as np
import jax
import jax.numpy as jnp

def _softmax(x, axis=-1):
    return jax.nn.softmax(x, axis=axis)

def _gelu(x):
    return jax.nn.gelu(x, approximate=True)

def _silu(x):
    return jax.nn.silu(x)

def _sigmoid(x):
    return jax.nn.sigmoid(x)

def _layernorm(x, axis=-1, eps=1e-05):
    m = jnp.mean(x, axis=axis, keepdims=True)
    v = jnp.var(x, axis=axis, keepdims=True)
    return (x - m) / jnp.sqrt(v + eps)

def _scatter_add(tgt, idx, src, axis=0):
    return tgt.at[idx].add(src)

def _segment_sum(src, seg, n):
    return jax.ops.segment_sum(src, seg, n)
kernel_name = 'mk_seq_postln_d1_jaxref_r8_d9f477'

def setup_inputs(seed: int=0):
    np.random.seed(seed)
    _w = jnp.asarray

    def _L0_attn_setup():
        import jax, jax.numpy as jnp
        from jax import lax
        import numpy as np
        D_MODEL = 256
        D_STATE = 128
        D_CONV = 4
        EXPAND = 2
        HEADDIM = 64
        NGROUPS = 1
        D_INNER = EXPAND * D_MODEL
        D_SSM = D_INNER
        NHEADS = D_SSM // HEADDIM
        CONV_DIM = D_SSM + 2 * NGROUPS * D_STATE
        D_IN_PROJ = 2 * D_INNER + 2 * NGROUPS * D_STATE + NHEADS
        BATCH = 2
        SEQLEN = 256
        EPS = 1e-05

        def _silu(x):
            return x * jax.nn.sigmoid(x)
        key = jax.random.key(seed)
        ks = jax.random.split(key, 8)
        u = jax.random.normal(ks[0], (BATCH, SEQLEN, D_MODEL), jnp.float32)
        W_in = jax.random.normal(ks[1], (D_IN_PROJ, D_MODEL), jnp.float32) * 0.02
        conv_w = jax.random.normal(ks[2], (CONV_DIM, 1, D_CONV), jnp.float32) * 0.2
        conv_b = jax.random.normal(ks[3], (CONV_DIM,), jnp.float32) * 0.02
        dt = jnp.exp(jax.random.uniform(ks[4], (NHEADS,)) * (jnp.log(0.1) - jnp.log(0.001)) + jnp.log(0.001))
        dt_bias = dt + jnp.log(-jnp.expm1(-dt))
        A_log = jnp.log(jax.random.uniform(ks[5], (NHEADS,), minval=1.0, maxval=16.0))
        D = jnp.ones((NHEADS,), jnp.float32)
        norm_w = jnp.ones((D_SSM,), jnp.float32)
        W_out = jax.random.normal(ks[6], (D_MODEL, D_INNER), jnp.float32) * 0.02
        return dict(u=u, W_in=W_in, conv_w=conv_w, conv_b=conv_b, dt_bias=dt_bias, A_log=A_log, D=D, norm_w=norm_w, W_out=W_out)
    _L0_attn_in = _L0_attn_setup()

    def _L0_ffn_setup():
        import jax, jax.numpy as jnp
        import numpy as np
        TOP_K = 4

        def _silu_and_mul(gu):
            g, u = jnp.split(gu, 2, axis=-1)
            return jax.nn.silu(g) * u
        key = jax.random.key(seed)
        ks = jax.random.split(key, 7)
        H, E, I, Is = (256, 16, 176, 704)
        s = 0.02
        return {'hidden_states': jax.random.normal(ks[0], (4, 128, H), dtype=jnp.float32), 'gate_w': jax.random.normal(ks[1], (E, H), dtype=jnp.float32) * s, 'sgate_w': jax.random.normal(ks[2], (1, H), dtype=jnp.float32) * s, 'w13': jax.random.normal(ks[3], (E, 2 * I, H), dtype=jnp.float32) * s, 'w2': jax.random.normal(ks[4], (E, H, I), dtype=jnp.float32) * s, 'shared_gate_up_w': jax.random.normal(ks[5], (2 * Is, H), dtype=jnp.float32) * s, 'shared_down_w': jax.random.normal(ks[6], (H, Is), dtype=jnp.float32) * s}
    _L0_ffn_in = _L0_ffn_setup()
    _d = {'L0_attn_u': _L0_attn_in['u'], 'L0_attn_W_in': _L0_attn_in['W_in'], 'L0_attn_conv_w': _L0_attn_in['conv_w'], 'L0_attn_conv_b': _L0_attn_in['conv_b'], 'L0_attn_dt_bias': _L0_attn_in['dt_bias'], 'L0_attn_A_log': _L0_attn_in['A_log'], 'L0_attn_D': _L0_attn_in['D'], 'L0_attn_norm_w': _L0_attn_in['norm_w'], 'L0_attn_W_out': _L0_attn_in['W_out'], 'L0_ffn_gate_w': _L0_ffn_in['gate_w'], 'L0_ffn_sgate_w': _L0_ffn_in['sgate_w'], 'L0_ffn_w13': _L0_ffn_in['w13'], 'L0_ffn_w2': _L0_ffn_in['w2'], 'L0_ffn_shared_gate_up_w': _L0_ffn_in['shared_gate_up_w'], 'L0_ffn_shared_down_w': _L0_ffn_in['shared_down_w']}
    _x0 = _d['L0_attn_u']
    _d['L0_attn_u'] = jax.random.normal(jax.random.fold_in(jax.random.key(seed), 1), (4, 1024, 256), dtype=_x0.dtype)
    del _x0
    return _d

def reference(L0_attn_u, L0_attn_W_in, L0_attn_conv_w, L0_attn_conv_b, L0_attn_dt_bias, L0_attn_A_log, L0_attn_D, L0_attn_norm_w, L0_attn_W_out, L0_ffn_gate_w, L0_ffn_sgate_w, L0_ffn_w13, L0_ffn_w2, L0_ffn_shared_gate_up_w, L0_ffn_shared_down_w):

    def _L0_attn_ref(u, W_in, conv_w, conv_b, dt_bias, A_log, D, norm_w, W_out):
        import jax, jax.numpy as jnp
        from jax import lax
        import numpy as np
        D_MODEL = 256
        D_STATE = 128
        D_CONV = 4
        EXPAND = 2
        HEADDIM = 64
        NGROUPS = 1
        D_INNER = EXPAND * D_MODEL
        D_SSM = D_INNER
        NHEADS = D_SSM // HEADDIM
        CONV_DIM = D_SSM + 2 * NGROUPS * D_STATE
        D_IN_PROJ = 2 * D_INNER + 2 * NGROUPS * D_STATE + NHEADS
        BATCH = 2
        SEQLEN = 256
        EPS = 1e-05

        def _silu(x):
            return x * jax.nn.sigmoid(x)
        batch, seqlen, _ = u.shape
        zxbcdt = jnp.einsum('bld,ed->ble', u, W_in)
        z = zxbcdt[..., :D_SSM]
        xBC = zxbcdt[..., D_SSM:D_SSM + CONV_DIM]
        dt = zxbcdt[..., D_SSM + CONV_DIM:]
        xc = lax.conv_general_dilated(xBC.transpose(0, 2, 1), conv_w, window_strides=(1,), padding=[(D_CONV - 1, 0)], feature_group_count=CONV_DIM, dimension_numbers=('NCH', 'OIH', 'NCH'))
        xBC = _silu((xc + conv_b[None, :, None]).transpose(0, 2, 1))
        x = xBC[..., :D_SSM]
        Bm = xBC[..., D_SSM:D_SSM + NGROUPS * D_STATE]
        Cm = xBC[..., D_SSM + NGROUPS * D_STATE:]
        A = -jnp.exp(A_log)
        dt_s = jax.nn.softplus(dt + dt_bias)
        dA = jnp.exp(dt_s * A)
        xh = x.reshape(batch, seqlen, NHEADS, HEADDIM)

        def step(state, inp):
            dA_t, dt_t, B_t, C_t, x_t = inp
            dB = dt_t[:, :, None] * B_t[:, None, :]
            state = dA_t[:, :, None, None] * state + x_t[..., None] * dB[:, :, None, :]
            y = jnp.einsum('bn,bhpn->bhp', C_t, state)
            return (state, y)
        state0 = jnp.zeros((batch, NHEADS, HEADDIM, D_STATE), u.dtype)
        xs = (dA.transpose(1, 0, 2), dt_s.transpose(1, 0, 2), Bm.transpose(1, 0, 2), Cm.transpose(1, 0, 2), xh.transpose(1, 0, 2, 3))
        _, ys = lax.scan(step, state0, xs)
        y = ys.transpose(1, 0, 2, 3) + xh * D[None, None, :, None]
        y = y.reshape(batch, seqlen, D_SSM)
        yg = y * _silu(z)
        yn = yg * lax.rsqrt(jnp.mean(yg * yg, axis=-1, keepdims=True) + EPS) * norm_w
        return jnp.einsum('bld,ed->ble', yn, W_out)

    def _L0_ffn_ref(hidden_states, gate_w, sgate_w, w13, w2, shared_gate_up_w, shared_down_w):
        import jax, jax.numpy as jnp
        import numpy as np
        TOP_K = 4

        def _silu_and_mul(gu):
            g, u = jnp.split(gu, 2, axis=-1)
            return jax.nn.silu(g) * u
        B, S, H = hidden_states.shape
        x = hidden_states.reshape(-1, H)
        E = gate_w.shape[0]
        shared = _silu_and_mul(x @ shared_gate_up_w.T) @ shared_down_w.T
        shared = shared * jax.nn.sigmoid(x @ sgate_w.T)
        router_logits = x @ gate_w.T
        routing_weights = jax.nn.softmax(router_logits.astype(jnp.float32), axis=-1)
        topk_w, topk_ids = jax.lax.top_k(routing_weights, TOP_K)

        def body(acc, ew):
            w13_e, w2_e, e = ew
            coef = jnp.sum(jnp.where(topk_ids == e, topk_w, 0.0), axis=-1)
            h = _silu_and_mul(x @ w13_e.T)
            acc = acc + (h @ w2_e.T).astype(jnp.float32) * coef[:, None]
            return (acc, None)
        init = jnp.zeros((x.shape[0], H), dtype=jnp.float32)
        sparse_out, _ = jax.lax.scan(body, init, (w13, w2, jnp.arange(E)))
        out = shared + sparse_out.astype(x.dtype)
        return out.reshape(B, S, H)
    x = L0_attn_u
    x = _layernorm(x + _L0_attn_ref(x, L0_attn_W_in, L0_attn_conv_w, L0_attn_conv_b, L0_attn_dt_bias, L0_attn_A_log, L0_attn_D, L0_attn_norm_w, L0_attn_W_out), axis=-1)
    x = _layernorm(x + _L0_ffn_ref(x, L0_ffn_gate_w, L0_ffn_sgate_w, L0_ffn_w13, L0_ffn_w2, L0_ffn_shared_gate_up_w, L0_ffn_shared_down_w), axis=-1)
    return x

_drawn_inputs = setup_inputs


def setup_inputs(seed=0):
    import zlib

    import numpy as np

    out = dict(_drawn_inputs(seed))
    spreads = {'L0_attn_D': (1.0, 0.2), 'L0_attn_norm_w': (1.0, 0.2)}
    factors = {'L0_attn_dt_bias': 8.0,
     'L0_attn_A_log': 8.0,
     'L0_ffn_gate_w': 8.0,
     'L0_ffn_sgate_w': 8.0,
     'L0_ffn_w13': 8.0,
     'L0_ffn_w2': 8.0,
     'L0_ffn_shared_gate_up_w': 4.03,
     'L0_ffn_shared_down_w': 4.035}
    for name, (base, spread) in spreads.items():
        noise = np.random.default_rng([zlib.crc32(name.encode()), seed]).standard_normal(out[name].shape)
        drawn = base * np.exp(spread * noise) if base else spread * noise
        out[name] = jnp.asarray(drawn.astype(out[name].dtype))
    for name, factor in factors.items():
        out[name] = (out[name] * factor).astype(out[name].dtype)
    return out
```

```python
from contextlib import ExitStack

import concourse.bass as bass
from concourse import mybir

F32 = mybir.dt.float32
I32 = mybir.dt.int32
U32 = mybir.dt.uint32
ALU = mybir.AluOpType
ACT = mybir.ActivationFunctionType
AX = mybir.AxisListType

P = 128
DM = 256
KD = DM // P
DI = 512
KI = DI // P
NS = 128
NH = 8
HD = DI // NH
CONV = DI + 2 * NS
NG = CONV // P
GB, GC = KI, KI + 1
TAPS = 4
HALO = TAPS - 1
PROJ = 2 * DI + 2 * NS + NH
BATCH, SEQ = 4, 1024
CH = SEQ // P
NC = BATCH * CH
BLK = 512
QB = BLK // P
NE = 16
TOPK = 4
FI = 176
HF = FI // 2
NSL = 704 // FI
REGION = NC * P + P
TILES = NC * TOPK + NE
ROWS = 2 * P
EPS = 1e-5
RANK = DM
TOT = RANK + NE


START = 1


def met(count):
    return START + count


def primed(count):
    return 16 + count


def prime(pool, kept, sems):
    for j, s in enumerate(sems):
        pool.dma_start(kept.spare[j:j + 1, :], kept.zrow[0:1, 0:1]).then_inc(s, 16)


def start(nc, sems):
    with nc.Block() as block:
        @block.sync
        def _(sp):
            for s in sems:
                sp.sem_inc(s, START)


class Steps:

    def __init__(self, eng, sem, base=0):
        self.eng, self.sem, self.base, self.n = eng, sem, base, 0

    def done(self, ins, apart=False):
        self.n += 1
        ins.then_inc(self.sem, 1)
        self.eng.wait_ge(self.sem, self.base + self.n)
        if apart:
            waits_end(self.eng)


def waits_end(eng):
    eng.nop(nofuse=True)


class Kept:

    def __init__(self, x_rows, y_rows, tile_dram, spare, ident, ones, half, zrow, iota_e, reg0, place,
                 acc, prob, chosen, slot, banks):
        self.x_rows, self.y_rows, self.tile_dram, self.spare = x_rows, y_rows, tile_dram, spare
        self.ident, self.ones, self.half, self.zrow, self.iota_e = ident, ones, half, zrow, iota_e
        self.reg0, self.place = reg0, place
        self.acc, self.prob, self.chosen, self.slot, self.banks = acc, prob, chosen, slot, banks


def bc(ap, where, shape):
    return ap.unsqueeze(where).to_broadcast(shape)


def build(nc, uT, u, w_in, conv_w, conv_b, dt_bias, a_log, d_skip, norm_w, w_out, gate, up, down, out):
    with ExitStack() as whole:
        def keep(name, shape, dt=F32):
            return whole.enter_context(nc.sbuf_tensor(name, shape, dt))

        kept = Kept(
            x_rows=nc.dram_tensor("x_rows", (NE * REGION, DM), F32, kind="Internal").ap(),
            y_rows=nc.dram_tensor("y_rows", (TILES * P, DM), F32, kind="Internal").ap(),
            tile_dram=nc.dram_tensor("tile_dram", (ROWS, 2), I32, kind="Internal").ap(),
            spare=nc.dram_tensor("spare", (2, 1), F32, kind="Internal").ap(),
            ident=keep("ident", [P, P]),
            ones=keep("ones", [P, P]),
            half=keep("half", [P, 1]),
            zrow=keep("zrow", [P, DM]),
            iota_e=keep("iota_e", [P, NE]),
            reg0=keep("reg0", [P, NE]),
            place=keep("place", [P, NE]),
            acc=keep("acc", [P, NC, DM]),
            prob=keep("prob", [P, NC, TOPK]),
            chosen=keep("chosen", [P, NC, TOPK]),
            slot=keep("slot", [P, NC, TOPK]),
            banks=[whole.enter_context(nc.psum_tensor(f"bank{i}", [P, 512], F32)) for i in range(8)],
        )
        mamba(nc, kept, uT, u, w_in, conv_w, conv_b, dt_bias, a_log, d_skip, norm_w, w_out, gate, up, down)
        experts(nc, kept, up, down)
        combine(nc, kept, out)


def mamba(nc, kept, uT, u, w_in, conv_w, conv_b, dt_bias, a_log, d_skip, norm_w, w_out, gate, up, down):
    ident, ones, half, place = kept.ident, kept.ones, kept.half, kept.place
    PA, PX, PG, PD, PY, PO = kept.banks[0:2], kept.banks[2], kept.banks[3], kept.banks[4:6], kept.banks[6], kept.banks[7]

    with ExitStack() as ctx:
        def sb(name, shape, dt=F32):
            return ctx.enter_context(nc.sbuf_tensor(name, shape, dt))

        looped = []

        def sem(name):
            looped.append(once(name))
            return looped[-1]

        def once(name):
            return ctx.enter_context(nc.semaphore(name))

        win = sb("win", [P, KD, PROJ])
        wout = sb("wout", [P, KI, DM])
        gw = sb("gw", [P, KD, NE + 1])
        sup = sb("sup", [P, NSL, KD, 2 * FI])
        sdn = sb("sdn", [HF, NSL, 2, DM])
        cw = sb("cw", [P, NG, TAPS])
        cb = sb("cb", [P, NG])
        dtb = sb("dtb", [P, NH])
        ah = sb("ah", [P, NH])
        dsk = sb("dsk", [P, NH])
        nw = sb("nw", [P, KI])
        incl = sb("incl", [P, P])
        later = sb("later", [P, P])
        before = sb("before", [P, P])
        uTb = sb("uTb", [P, 2, KD, BLK])
        ut = sb("ut", [P, 2, DM])
        raw = sb("raw", [P, 2, NG, HALO + BLK])
        xc = sb("xc", [P, 2, NG, BLK])
        dtw = sb("dtw", [P, 8, CH * NH])
        dts = sb("dts", [P, CH * NH])
        dA = sb("dA", [P, CH * NH])
        dec = sb("dec", [P, 3, CH * NH])
        din = sb("din", [P, CH * NH])
        xtok = sb("xtok", [P, 2, DI])
        btok = sb("btok", [P, 2, NS])
        dAw = sb("dAw", [P, NH, P])
        gm = sb("gm", [P, P])
        E = sb("E", [P, NH, P])
        M = sb("M", [P, NH, P])
        xs = sb("xs", [P, DI])
        xD = sb("xD", [P, DI])
        zs = sb("zs", [P, DI])
        y1 = sb("y1", [P, DI])
        y2 = sb("y2", [P, DI])
        yg = sb("yg", [P, DI])
        ysq = sb("ysq", [P, DI])
        ygT = sb("ygT", [P, DI])
        state = sb("state", [P, DI])
        ss = sb("ss", [P, 1])
        msq = sb("msq", [P, 1])
        rms = sb("rms", [P, 1])
        res = sb("res", [P, DM])
        bst = sb("bst", [P, 6])
        mv = sb("mv", [P, 2])
        vare = sb("vare", [P, 1])
        rstd = sb("rstd", [P, 1])
        x1 = sb("x1", [P, 2, DM])
        x1T = sb("x1T", [P, 2, KD, P])
        lg = sb("lg", [P, NE + 1])
        top = sb("top", [P, 8])
        topi = sb("topi", [P, 8], U32)
        chf = sb("chf", [P, TOPK])
        negm = sb("negm", [P, 1])
        ex = sb("ex", [P, NE])
        ez = sb("ez", [P, 1])
        e4 = sb("e4", [P, TOPK])
        eg = sb("eg", [P, 1])
        rz = sb("rz", [P, 1])
        sg = sb("sg", [P, 2])
        oh = sb("oh", [P, TOPK, NE])
        mask = sb("mask", [P, NE])
        rs = sb("rs", [P, NE])
        osl = sb("osl", [P, TOPK, NE])
        slf = sb("slf", [P, TOPK])
        sloti = sb("sloti", [P, 2, TOPK], I32)
        gs = sb("gs", [P, 2, FI])
        hb = sb("hb", [P, 2, FI])
        hT = sb("hT", [HF, 2, 2, P])

        loaded = once("loaded")
        consts = once("consts")
        setup = once("setup")
        uT_in = [sem("uT_in0"), sem("uT_in1")]
        u_in = [sem("u_in0"), sem("u_in1")]
        scattered = [once("scattered0"), once("scattered1")]
        pa_made = sem("pa_made")
        raw_in = sem("raw_in")
        conv_made = sem("conv_made")
        xc_ready = sem("xc_ready")
        dt_proj = sem("dt_proj")
        dt_abs = sem("dt_abs")
        dt_exp = sem("dt_exp")
        dA_ready = sem("dA_ready")
        sums_made = sem("sums_made")
        dec_ready = sem("dec_ready")
        din_ready = sem("din_ready")
        xT_made = sem("xT_made")
        xtok_ready = sem("xtok_ready")
        btok_ready = sem("btok_ready")
        g_made = sem("g_made")
        gm_ready = sem("gm_ready")
        dAw_ready = sem("dAw_ready")
        diff_made = sem("diff_made")
        E_ready = sem("E_ready")
        M_ready = sem("M_ready")
        xs_ready = sem("xs_ready")
        zs_ready = sem("zs_ready")
        y_made = sem("y_made")
        st_made = sem("st_made")
        state_ready = sem("state_ready")
        y1_ready = sem("y1_ready")
        yg_ready = sem("yg_ready")
        ss_ready = sem("ss_ready")
        rms_ready = sem("rms_ready")
        ygT_made = sem("ygT_made")
        ygT_ready = sem("ygT_ready")
        o_made = sem("o_made")
        res_ready = sem("res_ready")
        var_ready = sem("var_ready")
        std_ready = sem("std_ready")
        x1_ready = sem("x1_ready")
        x1T_made = sem("x1T_made")
        x1T_ready = sem("x1T_ready")
        lg_made = sem("lg_made")
        lg_ready = sem("lg_ready")
        rex_ready = sem("rex_ready")
        mask_ready = sem("mask_ready")
        rank_made = sem("rank_made")
        rank_read = sem("rank_read")
        slot_ready = sem("slot_ready")
        gs_ready = sem("gs_ready")
        h_ready = sem("h_ready")
        hT_made = sem("hT_made")
        hT_ready = sem("hT_ready")
        dn_made = sem("dn_made")
        acc_ready = sem("acc_ready")
        dve_own = once("dve_own")
        pool_own = once("pool_own")

        LOADS = 14
        CONSTS = 8
        DVE_BASE, DVE_TURN = 1, 15 + 2 * NG * (TAPS - 1) + CH * (11 + 2) + (CH - 1) * 2
        POOL_BASE = 4
        POOL_TURN = 3 * CH

        def at(c, w=P):
            return slice(c * w, c * w + w)

        def heads(ap):
            return ap.rearrange("p (h d) -> p h d", h=NH)

        def over(ap):
            return bc(ap, 2, [P, NH, HD])

        plan = [("raw", 0, k) for k in range(NG)]
        for c in range(CH + 1):
            if c < CH:
                plan.append(("z", c, 0))
            if c:
                plan += [("up", c - 1, s) for s in range(NSL)]
            if c < QB - 1:
                plan += [("raw", 1, 2 * c), ("raw", 1, 2 * c + 1)]
        use = {key: n for n, key in enumerate(plan)}
        PA_TURN = len(plan)
        assert PA_TURN % 2 == 0
        kinds = {"raw": (raw_in, 2 * NG), "z": (zs_ready, CH), "up": (h_ready, CH * NSL)}

        def bank_of(key):
            return PA[use[key] % 2]

        def wait_pa(pe, b, key):
            n = use[key] - 2
            kind = plan[n][0]
            signal, per = kinds[kind]
            if n >= 0:
                pe.wait_ge(signal, met(b * per + sum(k[0] == kind for k in plan[:n + 1])))
            else:
                pe.wait_ge(signal, met(b * per))

        start(nc, looped)
        with nc.Block() as block:
            @block.sync
            def _(sp):
                for t, src in ((win, w_in), (cw, conv_w), (cb, conv_b), (dtb, dt_bias), (ah, a_log),
                               (dsk, d_skip), (nw, norm_w), (wout, w_out), (gw, gate), (sdn, down[:, NE:])):
                    sp.dma_start(t[:], src).then_inc(loaded, 16)
                for s in range(NSL):
                    sp.dma_start(sup[:, s], up[:, NE + s]).then_inc(loaded, 16)
                with sp.Fori(0, BATCH) as b:
                    for k in range(2):
                        sp.wait_ge(zs_ready, met(b * CH))
                        sp.dma_start(uTb[:, k], uT[:, :, bass.ds(b * SEQ + k * BLK, BLK)]).then_inc(uT_in[k], 16)
                    for c in range(CH):
                        sp.wait_ge(res_ready, met(b * CH + max(c - 1, 0)))
                        sp.dma_start(ut[:, c % 2], u[bass.ds(b * SEQ + c * P, P), :]).then_inc(u_in[c % 2], 16)

            @block.gpsimd
            def _(pool):
                pool.memset(ident[:], 0.0).then_inc(pool_own, 1)
                pool.memset(incl[:], 1.0).then_inc(pool_own, 1)
                pool.memset(later[:], 1.0).then_inc(pool_own, 1)
                pool.memset(before[:], 1.0).then_inc(pool_own, 1)
                pool.memset(ones[:], 1.0).then_inc(consts, 1)
                pool.memset(half[:], -0.5).then_inc(consts, 1)
                pool.memset(kept.zrow[:], 0.0).then_inc(consts, 1)
                pool.iota(kept.iota_e[:], [[1, NE]], base=0, channel_multiplier=0,
                          allow_small_or_imprecise_dtypes=True).then_inc(consts, 1)
                pool.wait_ge(pool_own, POOL_BASE)
                pool.affine_select(out=ident[:], in_=ident[:], compare_op=ALU.not_equal, fill=1.0, base=0,
                                   pattern=[[-1, P]], channel_multiplier=1).then_inc(consts, 1)
                pool.affine_select(out=incl[:], in_=incl[:], compare_op=ALU.is_ge, fill=0.0, base=0,
                                   pattern=[[1, P]], channel_multiplier=-1).then_inc(consts, 1)
                pool.affine_select(out=later[:], in_=later[:], compare_op=ALU.is_ge, fill=0.0, base=-1,
                                   pattern=[[-1, P]], channel_multiplier=1).then_inc(consts, 1)
                pool.affine_select(out=before[:], in_=before[:], compare_op=ALU.is_ge, fill=0.0, base=-1,
                                   pattern=[[1, P]], channel_multiplier=-1).then_inc(consts, 1)
                pool.wait_ge(consts, CONSTS)
                pool.wait_ge(loaded, 16 * LOADS)
                prime(pool, kept, scattered)

                with pool.Fori(0, BATCH) as b:
                    own = Steps(pool, pool_own, POOL_BASE + b * POOL_TURN)

                    def spread(c):
                        pool.wait_ge(dA_ready, met(b + 1))
                        pool.wait_ge(diff_made, met((b * CH + c) * 2))
                        pool.tensor_tensor(dAw[:], bc(incl[:], 1, [P, NH, P]),
                                           bc(dA[:, at(c, NH)], 2, [P, NH, P]), ALU.mult).then_inc(dAw_ready, 1)

                    spread(0)
                    for c in range(CH + 1):
                        if c < CH:
                            pool.wait_ge(xtok_ready, met(b * CH + c + 1))
                            pool.wait_ge(din_ready, met(b + 1))
                            pool.wait_ge(st_made, met(b * CH + c))
                            pool.tensor_tensor(heads(xs[:]), heads(xtok[:, c % 2]), over(din[:, at(c, NH)]),
                                               ALU.mult).then_inc(xs_ready, 1)
                            own.done(pool.tensor_tensor(heads(xD[:]), heads(xtok[:, c % 2]), over(dsk[:]), ALU.mult))
                        if c < CH - 1:
                            spread(c + 1)
                        if c:
                            pool.wait_ge(slot_ready, met(b * CH + c))
                            waits_end(pool)
                            for j in range(TOPK):
                                pool.indirect_dma_start(
                                    kept.x_rows,
                                    bass.IndirectOffsetOnAxis(ap=sloti[:, (c - 1) % 2, j:j + 1].bitcast(U32), axis=0),
                                    x1[:, (c - 1) % 2], None).then_inc(scattered[(c - 1) % 2], 16)
                        if c < CH:
                            pool.wait_ge(y1_ready, met(b * CH + c + 1))
                            own.done(pool.tensor_tensor(y2[:], y1[:], xD[:], ALU.add))
                            pool.wait_ge(zs_ready, met(b * CH + c + 1))
                            pool.wait_ge(ygT_made, met(b * CH + c))
                            pool.wait_ge(ss_ready, met(b * CH + c))
                            pool.tensor_tensor(yg[:], y2[:], zs[:], ALU.mult).then_inc(yg_ready, 1)
                            pool.wait_ge(ss_ready, met(b * CH + c + 1))
                            waits_end(pool)
                            own.done(pool.tensor_scalar(msq[:], ss[:], 1.0 / DI, EPS, ALU.mult, ALU.add))
                            pool.tensor_tensor(rms[:], msq[:], half[:], ALU.pow).then_inc(rms_ready, 1)
                            pool.wait_ge(var_ready, met(b * CH + c + 1))
                            pool.tensor_tensor(rstd[:], vare[:], half[:], ALU.pow).then_inc(std_ready, 1)

            @block.tensor
            def _(pe):
                pe.wait_ge(consts, CONSTS)
                pe.wait_ge(loaded, 16 * LOADS)
                pe.wait_ge(setup, 4)
                with pe.Fori(0, BATCH) as b:
                    def project(k, g):
                        wait_pa(pe, b, ("raw", k, g))
                        for d in range(KD):
                            mm = pe.matmul(bank_of(("raw", k, g))[:], win[:, d, at(NG - 2 + g)], uTb[:, k, d, :],
                                           start=d == 0, stop=d == KD - 1)
                        mm.then_inc(pa_made, 1)

                    def slice_up(c, s):
                        wait_pa(pe, b, ("up", c, s))
                        for d in range(KD):
                            mm = pe.matmul(bank_of(("up", c, s))[:, 0:2 * FI], x1T[:, c % 2, d], sup[:, s, d],
                                           start=d == 0, stop=d == KD - 1)
                        mm.then_inc(pa_made, 1)

                    def slice_turn(c, s):
                        n = (b * CH + c) * NSL + s
                        pe.wait_ge(h_ready, met(n + 1))
                        pe.wait_ge(hT_ready, met(n))
                        for j in range(2):
                            mm = pe.transpose(PG[0:HF, DM + j * P:DM + (j + 1) * P], hb[:, s % 2, at(j, HF)], ident[:])
                        mm.then_inc(hT_made, 1)

                    def slice_down(c, s):
                        pe.wait_ge(hT_ready, met((b * CH + c) * NSL + s + 1))
                        if s == 0:
                            pe.wait_ge(acc_ready, met(b * CH + c))
                        for j in range(2):
                            mm = pe.matmul(PO[:, 0:DM], hT[:, s % 2, j], sdn[:, s, j],
                                           start=s == 0 and j == 0, stop=s == NSL - 1 and j == 1)
                        if s == NSL - 1:
                            mm.then_inc(dn_made, 1)

                    def rank(c):
                        pe.wait_ge(mask_ready, met(b * CH + c + 1))
                        pe.matmul(PY[:, RANK:RANK + NE], before[:], mask[:], start=True, stop=True)
                        pe.matmul(PY[:, TOT:TOT + NE], ones[:], mask[:], start=True, stop=True).then_inc(rank_made, 1)

                    pe.wait_ge(uT_in[0], met(b * 16 + 16))
                    pe.wait_ge(uT_in[1], met(b * 16 + 16))
                    pe.wait_ge(rank_read, met(b * CH))
                    for c in range(CH):
                        for d in range(KD):
                            mm = pe.matmul(PY[:, at(c, NH)], uTb[:, c // QB, d, at(c % QB)], win[:, d, PROJ - NH:PROJ],
                                           start=d == 0, stop=d == KD - 1)
                    mm.then_inc(dt_proj, 1)
                    for g in range(NG):
                        project(0, g)
                    pe.wait_ge(dA_ready, met(b + 1))
                    for j, m in enumerate((incl, later, ones)):
                        mm = pe.matmul(PY[:, at(1 + j, CH * NH)], m[:], dA[:], start=True, stop=True)
                    mm.then_inc(sums_made, 1)

                    for c in range(CH + 1):
                        n = b * CH + c
                        k, q = c // QB, c % QB
                        if c < CH:
                            pe.wait_ge(xc_ready, met((b * 2 + k + 1) * NG))
                            pe.wait_ge(ygT_ready, met(n))
                            for j in range(KI):
                                mm = pe.transpose(PX[:, at(j)], xc[:, k, j, at(q)], ident[:])
                            mm.then_inc(xT_made, 1)
                            pe.wait_ge(hT_ready, met((b * CH + max(c - 1, 0)) * NSL))
                            pe.wait_ge(gm_ready, met(n))
                            pe.transpose(PG[:, P:2 * P], xc[:, k, GB, at(q)], ident[:])
                            pe.matmul(PG[:, 0:P], xc[:, k, GB, at(q)], xc[:, k, GC, at(q)],
                                      start=True, stop=True).then_inc(g_made, 1)
                            wait_pa(pe, b, ("z", c, 0))
                            for d in range(KD):
                                mm = pe.matmul(bank_of(("z", c, 0))[:], uTb[:, k, d, at(q)], win[:, d, 0:DI],
                                               start=d == 0, stop=d == KD - 1)
                            mm.then_inc(pa_made, 1)
                            pe.wait_ge(dAw_ready, met(n + 1))
                            pe.wait_ge(y1_ready, met(n))
                            pe.wait_ge(state_ready, met(n))
                            for j in range(2):
                                pe.matmul(PD[j][:], later[:], dAw[:, 4 * j:4 * j + 4],
                                          start=True, stop=True).then_inc(diff_made, 1)
                        if c:
                            rank(c - 1)
                            slice_up(c - 1, 0)
                            slice_up(c - 1, 1)
                            if c < CH:
                                pe.wait_ge(gm_ready, met(n + 1))
                                pe.wait_ge(btok_ready, met(n + 1))
                            slice_turn(c - 1, 0)
                            slice_down(c - 1, 0)
                            slice_turn(c - 1, 1)
                        if c < CH:
                            pe.wait_ge(rank_read, met(n))
                            pe.wait_ge(dec_ready, met(b + 1))
                            pe.wait_ge(xtok_ready, met(n + 1))
                            for h in range(NH):
                                if h % 4 == 0:
                                    pe.wait_ge(M_ready, met(2 * n + 1 + h // 4))
                                mm = pe.matmul(PY[:, at(h, HD)], M[:, h], xtok[:, c % 2, at(h, HD)],
                                               start=True, stop=True)
                            if c:
                                mm = pe.matmul(PD[0][:], xc[:, k, GC, at(q)], state[:], start=True, stop=True)
                            mm.then_inc(y_made, 1)
                            pe.wait_ge(xs_ready, met(n + 1))
                            pe.wait_ge(btok_ready, met(n + 1))
                            pe.matmul(PD[1][:], btok[:, c % 2], xs[:], start=True, stop=True).then_inc(st_made, 1)
                        if c:
                            slice_up(c - 1, 2)
                            slice_down(c - 1, 1)
                            slice_turn(c - 1, 2)
                        if c < CH:
                            pe.wait_ge(yg_ready, met(n + 1))
                            for j in range(KI):
                                mm = pe.transpose(PX[:, at(j)], yg[:, at(j)], ident[:])
                            mm.then_inc(ygT_made, 1)
                        if c:
                            slice_up(c - 1, 3)
                            slice_down(c - 1, 2)
                        if c < CH:
                            pe.wait_ge(ygT_ready, met(n + 1))
                            for j in range(KI):
                                mm = pe.matmul(PY[:, 0:DM], ygT[:, at(j)], wout[:, j], start=j == 0, stop=j == KI - 1)
                            mm.then_inc(o_made, 1)
                        if c:
                            slice_turn(c - 1, 3)
                            slice_down(c - 1, 3)
                        if c < QB - 1:
                            project(1, 2 * c)
                            project(1, 2 * c + 1)
                        if c < CH:
                            pe.wait_ge(x1_ready, met(n + 1))
                            for d in range(KD):
                                mm = pe.transpose(PY[:, DM + d * P:DM + (d + 1) * P], x1[:, c % 2, at(d)], ident[:])
                            mm.then_inc(x1T_made, 1)
                            pe.wait_ge(x1T_ready, met(n + 1))
                            for d in range(KD):
                                mm = pe.matmul(PY[:, 0:NE + 1], x1T[:, c % 2, d], gw[:, d], start=d == 0, stop=d == KD - 1)
                            mm.then_inc(lg_made, 1)

            @block.scalar
            def _(act):
                act.wait_ge(loaded, 16 * LOADS)
                act.activation(E[:, 0, 0:NH], ah[:], ACT.Exp).then_inc(setup, 1)
                with act.Fori(0, BATCH) as b:
                    def wait_pa_made(key):
                        act.wait_ge(pa_made, met(b * PA_TURN + use[key] + 1))

                    def raw_copy(k, g):
                        wait_pa_made(("raw", k, g))
                        act.wait_ge(conv_made, met(b * 2 * NG + k * NG))
                        bank = bank_of(("raw", k, g))
                        if k == 0:
                            act.copy(raw[:, 1, g, 0:HALO], bank[:, BLK - HALO:BLK])
                        act.copy(raw[:, k, g, HALO:HALO + BLK], bank[:]).then_inc(raw_in, 1)

                    def conv_silu(k, g):
                        act.wait_ge(conv_made, met((b * 2 + k) * NG + g + 1))
                        act.activation(xc[:, k, g], xc[:, k, g], ACT.Silu).then_inc(xc_ready, 1)

                    def slice_silu(c, s):
                        wait_pa_made(("up", c, s))
                        act.wait_ge(h_ready, met(b * CH * NSL + max(c * NSL + s - 1, 0)))
                        act.activation(gs[:, s % 2], bank_of(("up", c, s))[:, 0:FI], ACT.Silu).then_inc(gs_ready, 1)

                    def slice_copy(c, s):
                        n = (b * CH + c) * NSL + s
                        act.wait_ge(hT_made, met(n + 1))
                        if s == 0:
                            act.wait_ge(dn_made, met(b * CH + c))
                        act.copy(hT[:, s % 2].rearrange("p j t -> p (j t)"), PG[0:HF, DM:2 * DM]).then_inc(hT_ready, 1)

                    act.wait_ge(dt_abs, met(b + 1))
                    act.activation(dtw[:, 2], dtw[:, 1], ACT.Exp).then_inc(dt_exp, 1)
                    for g in range(NG):
                        raw_copy(0, g)
                    act.wait_ge(sums_made, met(b + 1))
                    act.activation(dec[:].rearrange("p a n -> p (a n)"), PY[:, CH * NH:4 * CH * NH],
                                   ACT.Exp).then_inc(dec_ready, 1)
                    for g in range(NG):
                        conv_silu(0, g)

                    for c in range(CH + 1):
                        n = b * CH + c
                        if c < CH:
                            act.wait_ge(xT_made, met(n + 1))
                            act.wait_ge(y_made, met(b * CH + max(c - 1, 0)))
                            act.wait_ge(yg_ready, met(b * CH + max(c - 1, 0)))
                            act.copy(xtok[:, c % 2], PX[:]).then_inc(xtok_ready, 1)
                            act.wait_ge(g_made, met(n + 1))
                            act.wait_ge(st_made, met(b * CH + max(c - 1, 0)))
                            act.wait_ge(gm_ready, met(n + 1))
                            act.copy(btok[:, c % 2], PG[:, P:2 * P]).then_inc(btok_ready, 1)
                            act.wait_ge(M_ready, met(2 * n))
                            for j in range(2):
                                act.wait_ge(diff_made, met(2 * n + j + 1))
                                act.activation(E[:, 4 * j:4 * j + 4].rearrange("p h t -> p (h t)"), PD[j][:],
                                               ACT.Exp).then_inc(E_ready, 1)
                        if c:
                            act.wait_ge(lg_ready, met(n))
                            act.activation(ex[:], lg[:, 0:NE], ACT.Exp, bias=negm[:], accum_out=ez[:])
                            act.activation(e4[:], top[:, 0:TOPK], ACT.Exp, bias=negm[:])
                            act.activation(eg[:], lg[:, NE:NE + 1], ACT.Exp, scale=-1.0).then_inc(rex_ready, 1)
                        if c < CH:
                            wait_pa_made(("z", c, 0))
                            act.wait_ge(yg_ready, met(n))
                            act.activation(zs[:], bank_of(("z", c, 0))[:], ACT.Silu).then_inc(zs_ready, 1)
                        if c:
                            slice_silu(c - 1, 0)
                            slice_silu(c - 1, 1)
                            slice_copy(c - 1, 0)
                            slice_copy(c - 1, 1)
                            slice_silu(c - 1, 2)
                            if c == CH:
                                slice_copy(c - 1, 2)
                        if c < CH:
                            if c:
                                slice_copy(c - 1, 2)
                            act.wait_ge(yg_ready, met(n + 1))
                            act.wait_ge(rms_ready, met(n))
                            act.activation(ysq[:], yg[:], ACT.Square, accum_out=ss[:]).then_inc(ss_ready, 1)
                            act.wait_ge(ygT_made, met(n + 1))
                            act.wait_ge(o_made, met(n))
                            act.copy(ygT[:], PX[:]).then_inc(ygT_ready, 1)
                        if c:
                            slice_silu(c - 1, 3)
                            slice_copy(c - 1, 3)
                        if c < QB - 1:
                            raw_copy(1, 2 * c)
                            raw_copy(1, 2 * c + 1)
                        if c < CH:
                            act.wait_ge(x1T_made, met(n + 1))
                            act.wait_ge(dn_made, met(b * CH + max(c - 1, 0)))
                            act.copy(x1T[:, c % 2].rearrange("p k t -> p (k t)"), PY[:, DM:2 * DM]).then_inc(x1T_ready, 1)
                        if c < QB - 1:
                            conv_silu(1, 2 * c)
                            conv_silu(1, 2 * c + 1)

            @block.vector
            def _(dve):
                dve.memset(raw[:, 0, :, 0:HALO], 0.0).then_inc(dve_own, 1)
                dve.wait_ge(loaded, 16 * LOADS)
                dve.wait_ge(consts, CONSTS)
                dve.wait_ge(setup, 1)
                dve.tensor_scalar(ah[:], E[:, 0, 0:NH], -1.0, None, ALU.mult).then_inc(setup, 1)
                for j in range(KI):
                    w = dve.tensor_scalar(wout[:, j], wout[:, j], nw[:, j:j + 1], None, ALU.mult)
                w.then_inc(setup, 1)
                dve.tensor_scalar(kept.reg0[:], kept.iota_e[:], float(REGION), None, ALU.mult)
                dve.tensor_scalar(place[:], kept.iota_e[:], float(REGION), None, ALU.mult).then_inc(setup, 1)
                dve.wait_ge(setup, 4)

                with dve.Fori(0, BATCH) as b:
                    own = Steps(dve, dve_own, DVE_BASE + b * DVE_TURN)

                    def conv(k, g):
                        dve.wait_ge(raw_in, met((b * 2 + k) * NG + g + 1))
                        if g == 0:
                            dve.wait_ge(y_made, met(b * CH))
                            dve.wait_ge(g_made, met(b * CH))
                        x = xc[:, k, g]
                        own.done(dve.tensor_scalar(x, raw[:, k, g, 0:BLK], cw[:, g, 0:1], cb[:, g:g + 1], ALU.mult, ALU.add))
                        for j in range(1, TAPS):
                            ins = dve.scalar_tensor_tensor(x, raw[:, k, g, j:j + BLK], cw[:, g, j:j + 1], x, ALU.mult, ALU.add)
                            if j < TAPS - 1:
                                own.done(ins)
                        ins.then_inc(conv_made, 1)

                    def route(c):
                        dve.wait_ge(lg_made, met(b * CH + c + 1))
                        dve.wait_ge(rex_ready, met(b * CH + c))
                        own.done(dve.tensor_copy(lg[:], PY[:, 0:NE + 1]), apart=True)
                        own.done(dve.max(top[:], lg[:, 0:NE]))
                        dve.tensor_scalar(negm[:], top[:, 0:1], -1.0, None, ALU.mult).then_inc(lg_ready, 1)
                        own.done(dve.max_index(topi[:], top[:], lg[:, 0:NE]))
                        own.done(dve.tensor_copy(chf[:], topi[:, 0:TOPK]))
                        dve.tensor_copy(kept.chosen[:, bass.ds(b * CH + c, 1), :].rearrange("p a k -> p (a k)"), chf[:])
                        own.done(dve.tensor_tensor(oh[:], bc(kept.iota_e[:], 1, [P, TOPK, NE]),
                                                   bc(chf[:], 2, [P, TOPK, NE]), ALU.is_equal))
                        dve.tensor_reduce(mask[:], oh[:].rearrange("p k e -> p e k"), AX.X, ALU.add).then_inc(mask_ready, 1)

                    def weigh(c):
                        dve.wait_ge(rex_ready, met(b * CH + c + 1))
                        own.done(dve.reciprocal(rz[:], ez[:]))
                        dve.tensor_scalar(kept.prob[:, bass.ds(b * CH + c, 1), :].rearrange("p a k -> p (a k)"), e4[:],
                                          rz[:], None, ALU.mult)
                        own.done(dve.tensor_scalar(sg[:, 0:1], eg[:], 1.0, None, ALU.add))
                        own.done(dve.reciprocal(sg[:, 1:2], sg[:, 0:1]))

                    def give_slots(c):
                        dve.wait_ge(rank_made, met(b * CH + c + 1))
                        dve.wait_ge(rank_read, met(b * CH + c))
                        own.done(dve.tensor_tensor(rs[:], PY[:, RANK:RANK + NE], place[:], ALU.add))
                        own.done(dve.tensor_tensor(osl[:], oh[:], bc(rs[:], 1, [P, TOPK, NE]), ALU.mult))
                        dve.tensor_tensor(place[:], PY[:, TOT:TOT + NE], place[:], ALU.add).then_inc(rank_read, 1)
                        own.done(dve.tensor_reduce(slf[:], osl[:], AX.X, ALU.add))
                        dve.tensor_copy(kept.slot[:, bass.ds(b * CH + c, 1), :].rearrange("p a k -> p (a k)"), slf[:])
                        dve.wait_ge(scattered[c % 2], primed((b * (CH // 2) + c // 2) * 16 * TOPK))
                        dve.tensor_copy(sloti[:, c % 2], slf[:]).then_inc(slot_ready, 1)

                    def hidden(c, s):
                        n = (b * CH + c) * NSL + s
                        dve.wait_ge(gs_ready, met(n + 1))
                        dve.wait_ge(hT_made, met(b * CH * NSL + max(c * NSL + s - 1, 0)))
                        dve.tensor_tensor(hb[:, s % 2], gs[:, s % 2], bank_of(("up", c, s))[:, FI:2 * FI],
                                          ALU.mult).then_inc(h_ready, 1)

                    v, na, e, r, r2, pl, m0, t0 = (dtw[:, j] for j in range(8))
                    dve.wait_ge(dt_proj, met(b + 1))
                    own.done(dve.tensor_tensor(v.rearrange("p (c h) -> p c h", c=CH),
                                               PY[:, 0:CH * NH].rearrange("p (c h) -> p c h", c=CH),
                                               bc(dtb[:], 1, [P, CH, NH]), ALU.add))
                    dve.scalar_tensor_tensor(na, v, -1.0, v, ALU.mult, ALU.min).then_inc(dt_abs, 1)
                    dve.tensor_scalar(m0, v, 0.0, None, ALU.max)
                    dve.wait_ge(dt_exp, met(b + 1))
                    own.done(dve.tensor_scalar(t0, e, 2.0, None, ALU.add))
                    own.done(dve.reciprocal(t0, t0))
                    own.done(dve.tensor_tensor(r, e, t0, ALU.mult))
                    own.done(dve.tensor_tensor(r2, r, r, ALU.mult))
                    own.done(dve.tensor_scalar(pl, r2, 1.0 / 17, None, ALU.mult))
                    for odd in (15, 13, 11, 9, 7, 5, 3):
                        own.done(dve.scalar_tensor_tensor(pl, pl, 1.0 / odd, r2, ALU.add, ALU.mult))
                    own.done(dve.scalar_tensor_tensor(pl, pl, 1.0, r, ALU.add, ALU.mult))
                    own.done(dve.scalar_tensor_tensor(dts[:], pl, 2.0, m0, ALU.mult, ALU.add))
                    dve.tensor_tensor(dA[:].rearrange("p (c h) -> p c h", c=CH),
                                      dts[:].rearrange("p (c h) -> p c h", c=CH),
                                      bc(ah[:], 1, [P, CH, NH]), ALU.mult).then_inc(dA_ready, 1)
                    for g in range(NG):
                        conv(0, g)
                    dve.wait_ge(dec_ready, met(b + 1))
                    dve.wait_ge(xs_ready, met(b * CH))
                    dve.tensor_tensor(din[:], dec[:, 1], dts[:], ALU.mult).then_inc(din_ready, 1)

                    for c in range(CH + 1):
                        n = b * CH + c
                        if c:
                            route(c - 1)
                        if c < CH:
                            dve.wait_ge(g_made, met(n + 1))
                            dve.tensor_tensor(gm[:], PG[:, 0:P], incl[:], ALU.mult).then_inc(gm_ready, 1)
                            dve.wait_ge(gm_ready, met(n + 1))
                            dve.wait_ge(y_made, met(n))
                            for h in range(NH):
                                if h % 4 == 0:
                                    dve.wait_ge(E_ready, met(2 * n + 1 + h // 4))
                                ins = dve.scalar_tensor_tensor(M[:, h], E[:, h], dts[:, c * NH + h:c * NH + h + 1], gm[:],
                                                               ALU.mult, ALU.mult)
                                if h % 4 == 3:
                                    ins.then_inc(M_ready, 1)
                        if c:
                            weigh(c - 1)
                            give_slots(c - 1)
                            hidden(c - 1, 0)
                            hidden(c - 1, 1)
                        if c < CH:
                            dve.wait_ge(y_made, met(n + 1))
                            if c:
                                own.done(dve.tensor_tensor(heads(y1[:]), heads(PD[0][:]), over(dec[:, 0, at(c, NH)]), ALU.mult))
                                dve.tensor_tensor(y1[:], PY[:], y1[:], ALU.add).then_inc(y1_ready, 1)
                                dve.wait_ge(state_ready, met(n))
                                own.done(dve.tensor_tensor(heads(state[:]), heads(state[:]), over(dec[:, 2, at(c, NH)]), ALU.mult))
                                dve.wait_ge(st_made, met(n + 1))
                                dve.tensor_tensor(state[:], PD[1][:], state[:], ALU.add).then_inc(state_ready, 1)
                            else:
                                dve.tensor_copy(y1[:], PY[:]).then_inc(y1_ready, 1)
                                dve.wait_ge(st_made, met(n + 1))
                                dve.tensor_copy(state[:], PD[1][:]).then_inc(state_ready, 1)
                        if c:
                            hidden(c - 1, 2)
                        if c < CH:
                            dve.wait_ge(o_made, met(n + 1))
                            dve.wait_ge(rms_ready, met(n + 1))
                            dve.wait_ge(u_in[c % 2], met((b * (CH // 2) + c // 2 + 1) * 16))
                            dve.scalar_tensor_tensor(res[:], PY[:, 0:DM], rms[:], ut[:, c % 2], ALU.mult,
                                                     ALU.add).then_inc(res_ready, 1)
                            dve.wait_ge(res_ready, met(n + 1))
                            own.done(dve.bn_stats(bst[:], res[:]), apart=True)
                            own.done(dve.bn_aggr(mv[:], bst[:]))
                            dve.tensor_scalar(vare[:], mv[:, 1:2], EPS, None, ALU.add).then_inc(var_ready, 1)
                        if c:
                            hidden(c - 1, 3)
                        if c < CH:
                            dve.wait_ge(std_ready, met(n + 1))
                            dve.wait_ge(scattered[c % 2], primed((b * (CH // 2) + c // 2) * 16 * TOPK))
                            dve.tensor_scalar(x1[:, c % 2], res[:], mv[:, 0:1], rstd[:], ALU.subtract,
                                              ALU.mult).then_inc(x1_ready, 1)
                        if c:
                            dve.wait_ge(dn_made, met(n))
                            dve.wait_ge(x1_ready, met(n))
                            dve.scalar_tensor_tensor(kept.acc[:, bass.ds(n - 1, 1), :].rearrange("p a d -> p (a d)"),
                                                     PO[:, 0:DM], sg[:, 1:2], x1[:, (c - 1) % 2], ALU.mult,
                                                     ALU.add).then_inc(acc_ready, 1)
                        if c < QB - 1:
                            conv(1, 2 * c)
                            conv(1, 2 * c + 1)
                    assert own.n == DVE_TURN, own.n
                dve.wait_ge(scattered[0], primed(NC // 2 * TOPK * 16))
                dve.wait_ge(scattered[1], primed(NC // 2 * TOPK * 16))


def experts(nc, kept, up, down):
    pX, pU, pH, pO = (kept.banks[2 * j:2 * j + 2] for j in range(4))

    with ExitStack() as ctx:
        def sb(name, shape, dt=F32):
            return ctx.enter_context(nc.sbuf_tensor(name, shape, dt))

        def sem(name):
            return ctx.enter_context(nc.semaphore(name))

        w13 = sb("w13", [P, NE * KD * 2 * FI])
        w2 = sb("w2", [HF, NE * 2 * DM])
        pad = sb("pad", [P, NE])
        padi = sb("padi", [P, NE], I32)
        row_i = sb("row_i", [P, 1])
        cnt = sb("cnt", [P, NE])
        cnti = sb("cnti", [P, NE], I32)
        tiles = sb("tiles", [P, NE])
        ones_e = sb("ones_e", [P, NE])
        ends = sb("ends", [P, NE])
        starts = sb("starts", [P, NE])
        jump = sb("jump", [P, NE])
        shift = sb("shift", [P, NE])
        tile_no = sb("tile_no", [P, 2])
        last = sb("last", [P, 1])
        past = sb("past", [P, 2, NE])
        pastj = sb("pastj", [P, 2, NE])
        tabf = sb("tabf", [P, 2, 2])
        tabx = sb("tabx", [P, 2])
        tabi = sb("tabi", [P, 2, 2], I32)
        table = sb("table", [1, ROWS * 2], I32)
        isk = sb("isk", [P, NC * TOPK, NE])
        sh = sb("sh", [P, NC * TOPK])
        xr = sb("xr", [P, 2, DM])
        xT = sb("xT", [P, 2, KD, P])
        gs = sb("gse", [P, 2, FI])
        hb = sb("hbe", [P, 2, FI])
        hT = sb("hTe", [HF, 2, 2, P])
        yo = sb("yo", [P, 2, DM])

        w_in = sem("w_in")
        nums = sem("nums")
        own_sem = sem("layout_own")
        pads_ready = sem("pads_ready")
        padded = sem("padded")
        tab_ready = sem("tab_ready")
        tab_out = sem("tab_out")
        tab_in = sem("tab_in")
        x_in = [sem("x_in0"), sem("x_in1")]
        xT_made = sem("xT_made_e")
        xT_ready = sem("xT_ready_e")
        u_made = sem("u_made")
        gs_ready = sem("gs_ready_e")
        h_ready = sem("h_ready_e")
        hT_made = sem("hT_made_e")
        hT_ready = sem("hT_ready_e")
        d_made = sem("d_made")
        yo_ready = sem("yo_ready")
        stored = [sem("stored0"), sem("stored1")]

        def turns(eng, step):
            step(0, 0, True)
            step(1, 1, True)
            with eng.Fori(1, TILES // 2) as i:
                for par in range(2):
                    step(2 * i + par, par, False)

        with nc.Block() as block:
            @block.sync
            def _(sp):
                for e in range(NE):
                    sp.dma_start(w13[:, e * KD * 2 * FI:(e + 1) * KD * 2 * FI], up[:, e].rearrange("p k n -> p (k n)")).then_inc(w_in, 16)
                    sp.dma_start(w2[:, e * 2 * DM:(e + 1) * 2 * DM], down[:, e].rearrange("p k n -> p (k n)")).then_inc(w_in, 16)
                sp.wait_ge(tab_ready, 1)
                sp.dma_start(kept.tile_dram.rearrange("(a p) c -> p a c", a=2), tabi[:]).then_inc(tab_out, 16)
                sp.wait_ge(tab_out, 16)
                sp.dma_start(table[:], kept.tile_dram.rearrange("t c -> (t c)").unsqueeze(0)).then_inc(tab_in, 16)
                sp.wait_ge(tab_in, 16)
                sp.wait_ge(padded, NE * 16)

                def load(t, par, first):
                    row = sp.value_load(table[0:1, bass.ds(2 * t + 1, 1)], min_val=0, max_val=NE * REGION - P)
                    if not first:
                        sp.wait_ge(xT_made, t - 1)
                    sp.dma_start(xr[:, par], kept.x_rows[bass.ds(row, P), :]).then_inc(x_in[par], 16)

                turns(sp, load)

            @block.gpsimd
            def _(pool):
                pool.iota(row_i[:], [[0, 1]], base=0, channel_multiplier=1,
                          allow_small_or_imprecise_dtypes=True).then_inc(nums, 1)
                pool.iota(tile_no[:], [[P, 2]], base=0, channel_multiplier=1,
                          allow_small_or_imprecise_dtypes=True).then_inc(nums, 1)
                pool.memset(ones_e[:], 1.0).then_inc(nums, 1)
                prime(pool, kept, stored)
                pool.wait_ge(pads_ready, 1)
                for e in range(NE):
                    pool.indirect_dma_start(
                        kept.x_rows, bass.IndirectOffsetOnAxis(ap=padi[:, e:e + 1].bitcast(U32), axis=0),
                        kept.zrow[:], None).then_inc(padded, 16)

                def store(t, par, first):
                    pool.wait_ge(yo_ready, t + 1)
                    pool.dma_start(kept.y_rows[bass.ds(t * P, P), :], yo[:, par]).then_inc(stored[par], 16)

                turns(pool, store)
                pool.wait_ge(stored[0], primed(TILES // 2 * 16))
                pool.wait_ge(stored[1], primed(TILES // 2 * 16))

            @block.tensor
            def _(pe):
                pe.wait_ge(tab_in, 16)
                pe.wait_ge(w_in, 2 * NE * 16)

                def rows_turn(t, par, pairs):
                    pe.wait_ge(x_in[par], pairs * 16 + 16)
                    for d in range(KD):
                        mm = pe.transpose(pX[par][:, d * P:(d + 1) * P], xr[:, par, d * P:(d + 1) * P], kept.ident[:])
                    mm.then_inc(xT_made, 1)

                def go_down(t, par, e):
                    pe.wait_ge(hT_ready, t + 1)
                    for j in range(2):
                        mm = pe.matmul(pO[par][:, 0:DM], hT[:, par, j], w2[:, bass.ds(e * 2 * DM + j * DM, DM)],
                                       start=j == 0, stop=j == 1)
                    mm.then_inc(d_made, 1)

                def expert_of(t):
                    return pe.value_load(table[0:1, bass.ds(2 * t, 1)], min_val=0, max_val=NE - 1)

                def step(t, par, first):
                    e = expert_of(t)
                    pe.wait_ge(xT_ready, t + 1)
                    if not first:
                        pe.wait_ge(h_ready, t - 1)
                    for d in range(KD):
                        mm = pe.matmul(pU[par][:, 0:2 * FI], xT[:, par, d], w13[:, bass.ds(e * KD * 2 * FI + d * 2 * FI, 2 * FI)],
                                       start=d == 0, stop=d == KD - 1)
                    mm.then_inc(u_made, 1)
                    if not (isinstance(t, int) and t == TILES - 1):
                        rows_turn(t + 1, 1 - par, (t + 1) // 2 if first else pairs_of(t, par))
                    if not (first and t == 0):
                        go_down(t - 1, 1 - par, expert_of(t - 1))
                    pe.wait_ge(h_ready, t + 1)
                    for j in range(2):
                        mm = pe.transpose(pH[par][0:HF, j * P:(j + 1) * P], hb[:, par, j * HF:(j + 1) * HF], kept.ident[:])
                    mm.then_inc(hT_made, 1)

                def pairs_of(t, par):
                    return turn + par

                rows_turn(0, 0, 0)
                step(0, 0, True)
                step(1, 1, True)
                with pe.Fori(1, TILES // 2 - 1) as turn:
                    for par in range(2):
                        step(2 * turn + par, par, False)
                turn = TILES // 2 - 1
                step(TILES - 2, 0, False)
                step(TILES - 1, 1, False)
                pe.wait_ge(yo_ready, TILES - 2)
                go_down(TILES - 1, 1, expert_of(TILES - 1))

            @block.scalar
            def _(act):
                def copy_rows(t, par):
                    act.wait_ge(xT_made, t + 1)
                    act.copy(xT[:, par].rearrange("p k t -> p (k t)"), pX[par][:, 0:DM]).then_inc(xT_ready, 1)

                def step(t, par, first, more=True):
                    act.wait_ge(u_made, t + 1)
                    if not first:
                        act.wait_ge(h_ready, t - 1)
                    act.activation(gs[:, par], pU[par][:, 0:FI], ACT.Silu).then_inc(gs_ready, 1)
                    if more:
                        copy_rows(t + 1, 1 - par)
                    act.wait_ge(hT_made, t + 1)
                    if not first:
                        act.wait_ge(d_made, t - 1)
                    act.copy(hT[:, par].rearrange("p k t -> p (k t)"), pH[par][0:HF, 0:2 * P]).then_inc(hT_ready, 1)

                copy_rows(0, 0)
                step(0, 0, True)
                step(1, 1, True)
                with act.Fori(1, TILES // 2 - 1) as i:
                    for par in range(2):
                        step(2 * i + par, par, False)
                step(TILES - 2, 0, False)
                step(TILES - 1, 1, False, more=False)

            @block.vector
            def _(dve):
                own = Steps(dve, own_sem)
                dve.wait_ge(nums, 3)
                own.done(dve.tensor_scalar(pad[:], kept.place[:], row_i[:], None, ALU.add))
                dve.tensor_copy(padi[:], pad[:]).then_inc(pads_ready, 1)
                own.done(dve.tensor_tensor(cnt[:], kept.place[:], kept.reg0[:], ALU.subtract))
                own.done(dve.tensor_scalar(cnti[:], cnt[:], float(P - 1), None, ALU.add))
                own.done(dve.tensor_scalar(cnti[:], cnti[:], 7, None, ALU.arith_shift_right))
                own.done(dve.tensor_copy(tiles[:], cnti[:]))
                own.done(dve.tensor_tensor_scan(ends[:], ones_e[:], tiles[:], 0.0, ALU.mult, ALU.add))
                own.done(dve.tensor_tensor(starts[:], ends[:], tiles[:], ALU.subtract))
                own.done(dve.tensor_scalar(jump[:], tiles[:], -float(P), float(REGION), ALU.mult, ALU.add))
                own.done(dve.tensor_scalar(last[:], ends[:, NE - 1:NE], -1.0, None, ALU.add))
                own.done(dve.tensor_scalar(tile_no[:], tile_no[:], last[:], None, ALU.min))
                own.done(dve.tensor_tensor(past[:], bc(tile_no[:], 2, [P, 2, NE]), bc(ends[:], 1, [P, 2, NE]), ALU.is_ge))
                own.done(dve.tensor_tensor(pastj[:], past[:], bc(jump[:], 1, [P, 2, NE]), ALU.mult))
                own.done(dve.tensor_reduce(tabf[:, :, 0], past[:], AX.X, ALU.add))
                own.done(dve.tensor_reduce(tabx[:], pastj[:], AX.X, ALU.add))
                own.done(dve.scalar_tensor_tensor(tabf[:, :, 1], tile_no[:], float(P), tabx[:], ALU.mult, ALU.add))
                dve.tensor_copy(tabi[:], tabf[:]).then_inc(tab_ready, 1)
                own.done(dve.scalar_tensor_tensor(shift[:], starts[:], float(P), kept.reg0[:], ALU.mult, ALU.subtract))
                own.done(dve.tensor_tensor(isk[:], bc(kept.chosen[:].rearrange("p c k -> p (c k)"), 2, [P, NC * TOPK, NE]),
                                           bc(kept.iota_e[:], 1, [P, NC * TOPK, NE]), ALU.is_equal))
                own.done(dve.tensor_tensor(isk[:], isk[:], bc(shift[:], 1, [P, NC * TOPK, NE]), ALU.mult))
                own.done(dve.tensor_reduce(sh[:], isk[:], AX.X, ALU.add))
                own.done(dve.tensor_tensor(kept.slot[:].rearrange("p c k -> p (c k)"),
                                           kept.slot[:].rearrange("p c k -> p (c k)"), sh[:], ALU.add))

                def emit(t, par, first, pairs):
                    dve.wait_ge(d_made, t + 1)
                    if not first:
                        dve.wait_ge(stored[par], primed(pairs * 16))
                    dve.tensor_copy(yo[:, par], pO[par][:, 0:DM]).then_inc(yo_ready, 1)

                def hide(t, par, first):
                    dve.wait_ge(gs_ready, t + 1)
                    if not first:
                        dve.wait_ge(hT_made, t - 1)
                    dve.tensor_tensor(hb[:, par], gs[:, par], pU[par][:, FI:2 * FI], ALU.mult).then_inc(h_ready, 1)

                hide(0, 0, True)
                hide(1, 1, True)
                emit(0, 0, True, 0)
                with dve.Fori(1, TILES // 2) as i:
                    hide(2 * i, 0, False)
                    emit(2 * i - 1, 1, False, i - 1)
                    hide(2 * i + 1, 1, False)
                    emit(2 * i, 0, False, i)
                emit(TILES - 1, 1, False, TILES // 2 - 1)


def combine(nc, kept, out):
    with ExitStack() as ctx:
        def sb(name, shape, dt=F32):
            return ctx.enter_context(nc.sbuf_tensor(name, shape, dt))

        def sem(name):
            return ctx.enter_context(nc.semaphore(name))

        ys = sb("ys", [P, 2, TOPK, DM])
        sloti = sb("sloti_c", [P, 2, TOPK], I32)
        pk = sb("pk", [P, 2, TOPK])
        sm = sb("sm", [P, 2, DM])
        bst = sb("bst_c", [P, 2, 6])
        mv = sb("mv_c", [P, 2, 2])
        vare = sb("vare_c", [P, 2, 1])
        rstd = sb("rstd_c", [P, 2, 1])
        res = sb("res_c", [P, 2, DM])

        slots_ready = sem("slots_ready")
        gathered = [sem("gathered0"), sem("gathered1")]
        summed = sem("summed")
        var_ready = sem("var_ready_c")
        std_ready = sem("std_ready_c")
        res_ready = sem("res_ready_c")
        written = [sem("written0"), sem("written1")]
        own_sem = sem("combine_own")
        TURN = 2 * 6

        start(nc, written)
        with nc.Block() as block:
            @block.gpsimd
            def _(pool):
                with pool.Fori(0, NC // 2) as i:
                    for par in range(2):
                        c = 2 * i + par
                        pool.wait_ge(slots_ready, c + 1)
                        waits_end(pool)
                        for j in range(TOPK):
                            pool.indirect_dma_start(
                                ys[:, par, j], None, kept.y_rows,
                                bass.IndirectOffsetOnAxis(ap=sloti[:, par, j:j + 1].bitcast(U32), axis=0)).then_inc(gathered[par], 16)
                    for par in range(2):
                        pool.wait_ge(var_ready, 2 * i + par + 1)
                        pool.tensor_tensor(rstd[:, par], vare[:, par], kept.half[:], ALU.pow).then_inc(std_ready, 1)

            @block.vector
            def _(dve):
                with dve.Fori(0, NC // 2) as i:
                    own = Steps(dve, own_sem, i * TURN)
                    for par in range(2):
                        c = 2 * i + par
                        dve.tensor_copy(pk[:, par], kept.prob[:, bass.ds(c, 1), :].rearrange("p a k -> p (a k)"))
                        dve.tensor_copy(sloti[:, par], kept.slot[:, bass.ds(c, 1), :].rearrange("p a k -> p (a k)")).then_inc(slots_ready, 1)
                    for par in range(2):
                        c = 2 * i + par
                        dve.wait_ge(gathered[par], (i + 1) * 16 * TOPK)
                        dve.wait_ge(slots_ready, c + 1)
                        own.done(dve.scalar_tensor_tensor(
                            sm[:, par], ys[:, par, 0], pk[:, par, 0:1],
                            kept.acc[:, bass.ds(c, 1), :].rearrange("p a d -> p (a d)"), ALU.mult, ALU.add))
                        for j in range(1, TOPK):
                            own.done(dve.scalar_tensor_tensor(sm[:, par], ys[:, par, j], pk[:, par, j:j + 1], sm[:, par],
                                                              ALU.mult, ALU.add))
                        own.done(dve.bn_stats(bst[:, par], sm[:, par]), apart=True)
                        own.done(dve.bn_aggr(mv[:, par], bst[:, par]))
                        dve.tensor_scalar(vare[:, par], mv[:, par, 1:2], EPS, None, ALU.add).then_inc(var_ready, 1)
                    for par in range(2):
                        c = 2 * i + par
                        dve.wait_ge(std_ready, c + 1)
                        dve.wait_ge(written[par], met(i * 16))
                        dve.tensor_scalar(res[:, par], sm[:, par], mv[:, par, 0:1], rstd[:, par], ALU.subtract,
                                          ALU.mult).then_inc(res_ready, 1)

            @block.sync
            def _(sp):
                with sp.Fori(0, NC // 2) as i:
                    for par in range(2):
                        c = 2 * i + par
                        sp.wait_ge(res_ready, c + 1)
                        sp.dma_start(out[bass.ds(c * P, P), :], res[:, par]).then_inc(written[par], 16)
                sp.wait_ge(written[0], met(NC // 2 * 16))
                sp.wait_ge(written[1], met(NC // 2 * 16))


def kernel(**inputs):
    import numpy as np
    from concourse import bacc
    from concourse.bass_utils import run_bass_kernel_spmd

    a = {k: np.asarray(v) for k, v in inputs.items()}

    def halves(w, p):
        return w.T.reshape(w.shape[1] // p, p, w.shape[0]).transpose(1, 0, 2)

    tokens = BATCH * SEQ
    u = a["L0_attn_u"].reshape(tokens, DM)
    f = NSL * FI
    sgu = a["L0_ffn_shared_gate_up_w"]
    ups = [*a["L0_ffn_w13"]] + [np.concatenate([sgu[s * FI:(s + 1) * FI], sgu[f + s * FI:f + (s + 1) * FI]]) for s in range(NSL)]
    downs = [*a["L0_ffn_w2"]] + [a["L0_ffn_shared_down_w"][:, s * FI:(s + 1) * FI] for s in range(NSL)]
    laid = {
        "uT": halves(u, P),
        "u": u,
        "w_in": halves(a["L0_attn_W_in"], P),
        "conv_w": a["L0_attn_conv_w"].reshape(NG, P, TAPS).transpose(1, 0, 2),
        "conv_b": a["L0_attn_conv_b"].reshape(NG, P).T,
        "dt_bias": np.broadcast_to(a["L0_attn_dt_bias"], (P, NH)),
        "a_log": np.broadcast_to(a["L0_attn_A_log"], (P, NH)),
        "d_skip": np.broadcast_to(a["L0_attn_D"], (P, NH)),
        "norm_w": a["L0_attn_norm_w"].reshape(KI, P).T,
        "w_out": halves(a["L0_attn_W_out"], P),
        "gate": halves(np.concatenate([a["L0_ffn_gate_w"], a["L0_ffn_sgate_w"]]), P),
        "up": np.stack([halves(w, P) for w in ups], axis=1),
        "down": np.stack([halves(w, HF) for w in downs], axis=1),
    }
    nc = bacc.Bacc("TRN2", target_bir_lowering=False, num_devices=1)
    arrays = {f"in_{k}": np.ascontiguousarray(v) for k, v in laid.items()}
    args = [nc.dram_tensor(k, v.shape, F32, kind="ExternalInput").ap() for k, v in arrays.items()]
    out = nc.dram_tensor("out_dram", (tokens, DM), F32, kind="ExternalOutput").ap()
    build(nc, *args, out)
    r = run_bass_kernel_spmd(nc, [arrays], core_ids=[0])
    return r.results[0]["out_dram"].reshape(BATCH, SEQ, DM)
```

```python
from contextlib import ExitStack

import concourse.bass as bass
from concourse import mybir

F32 = mybir.dt.float32
I32 = mybir.dt.int32
U32 = mybir.dt.uint32
ALU = mybir.AluOpType
ACT = mybir.ActivationFunctionType
AX = mybir.AxisListType

P = 128
DM = 256
KD = DM // P
DI = 512
KI = DI // P
NS = 128
NH = 8
HD = DI // NH
CONV = DI + 2 * NS
NG = CONV // P
GB, GC = KI, KI + 1
TAPS = 4
HALO = TAPS - 1
PROJ = 2 * DI + 2 * NS + NH
BATCH, SEQ = 4, 1024
CH = SEQ // P
NC = BATCH * CH
BLK = 512
QB = BLK // P
NE = 16
TOPK = 4
FI = 176
HF = FI // 2
NSL = 704 // FI
REGION = NC * P + P
TILES = NC * TOPK + NE
RING = 4
YROW = DM + 2 * TOPK
ODD = YROW + 1
XW = ODD + 1
EPS = 1e-5
RANK = DM
TOT = RANK + NE


START = 1


def met(count):
    return START + count


def primed(count):
    return 16 + count


def prime(pool, kept, sems):
    for j, s in enumerate(sems):
        pool.dma_start(kept.spare[j:j + 1, :], kept.padrow[0:1, 0:1]).then_inc(s, 16)


def start(nc, sems):
    with nc.Block() as block:
        @block.sync
        def _(sp):
            for s in sems:
                sp.sem_inc(s, START)


class Steps:

    def __init__(self, eng, sem, base=0):
        self.eng, self.sem, self.base, self.n = eng, sem, base, 0

    def done(self, ins, apart=False):
        self.n += 1
        ins.then_inc(self.sem, 1)
        self.eng.wait_ge(self.sem, self.base + self.n)
        if apart:
            waits_end(self.eng)


def waits_end(eng):
    eng.nop(nofuse=True)


class Kept:

    def __init__(self, x_rows, y_rows, base, spare, ident, ones, half, padrow, iota_e, reg0, place, w13, banks):
        self.x_rows, self.y_rows, self.base, self.spare = x_rows, y_rows, base, spare
        self.ident, self.ones, self.half, self.padrow, self.iota_e = ident, ones, half, padrow, iota_e
        self.reg0, self.place, self.w13, self.banks = reg0, place, w13, banks


def bc(ap, where, shape):
    return ap.unsqueeze(where).to_broadcast(shape)


def build(nc, uT, u, w_in, conv_w, conv_b, dt_bias, a_log, d_skip, norm_w, w_out, gate, up, down, out):
    with ExitStack() as whole:
        def keep(name, shape, dt=F32):
            return whole.enter_context(nc.sbuf_tensor(name, shape, dt))

        kept = Kept(
            x_rows=nc.dram_tensor("x_rows", (NE * REGION + P, XW), F32, kind="Internal").ap(),
            y_rows=nc.dram_tensor("y_rows", (NC * P * TOPK + 2 * P, DM), F32, kind="Internal").ap(),
            base=nc.dram_tensor("base", (NC * P, DM), F32, kind="Internal").ap(),
            spare=nc.dram_tensor("spare", (2, 1), F32, kind="Internal").ap(),
            ident=keep("ident", [P, P]),
            ones=keep("ones", [P, P]),
            half=keep("half", [P, 1]),
            padrow=keep("padrow", [P, XW]),
            iota_e=keep("iota_e", [P, NE]),
            reg0=keep("reg0", [P, NE]),
            place=keep("place", [P, NE]),
            w13=keep("w13", [P, NE * KD * 2 * FI]),
            banks=[whole.enter_context(nc.psum_tensor(f"bank{i}", [P, 512], F32)) for i in range(8)],
        )
        mamba(nc, kept, uT, u, w_in, conv_w, conv_b, dt_bias, a_log, d_skip, norm_w, w_out, gate, up, down)
        experts(nc, kept, down)
        combine(nc, kept, out)


def mamba(nc, kept, uT, u, w_in, conv_w, conv_b, dt_bias, a_log, d_skip, norm_w, w_out, gate, up, down):
    ident, ones, half, place = kept.ident, kept.ones, kept.half, kept.place
    PA, PX, PG, PD, PY, PO = kept.banks[0:2], kept.banks[2], kept.banks[3], kept.banks[4:6], kept.banks[6], kept.banks[7]

    with ExitStack() as ctx:
        def sb(name, shape, dt=F32):
            return ctx.enter_context(nc.sbuf_tensor(name, shape, dt))

        looped = []

        def sem(name):
            looped.append(once(name))
            return looped[-1]

        def once(name):
            return ctx.enter_context(nc.semaphore(name))

        win = sb("win", [P, KD, PROJ])
        wout = sb("wout", [P, KI, DM])
        gw = sb("gw", [P, KD, NE + 1])
        sup = sb("sup", [P, NSL, KD, 2 * FI])
        sdn = sb("sdn", [HF, NSL, 2, DM])
        cw = sb("cw", [P, NG, TAPS])
        cb = sb("cb", [P, NG])
        dtb = sb("dtb", [P, NH])
        ah = sb("ah", [P, NH])
        dsk = sb("dsk", [P, NH])
        nw = sb("nw", [P, KI])
        incl = sb("incl", [P, P])
        later = sb("later", [P, P])
        before = sb("before", [P, P])
        uTb = sb("uTb", [P, 2, KD, BLK])
        ut = sb("ut", [P, 2, DM])
        raw = sb("raw", [P, 2, NG, HALO + BLK])
        xc = sb("xc", [P, 2, NG, BLK])
        dtw = sb("dtw", [P, 8, CH * NH])
        dts = sb("dts", [P, CH * NH])
        dA = sb("dA", [P, CH * NH])
        dec = sb("dec", [P, 3, CH * NH])
        din = sb("din", [P, CH * NH])
        xtok = sb("xtok", [P, 2, DI])
        btok = sb("btok", [P, 2, NS])
        dAw = sb("dAw", [P, NH, P])
        gm = sb("gm", [P, P])
        E = sb("E", [P, NH, P])
        M = sb("M", [P, NH, P])
        xs = sb("xs", [P, DI])
        xD = sb("xD", [P, DI])
        zs = sb("zs", [P, DI])
        y1 = sb("y1", [P, DI])
        y2 = sb("y2", [P, DI])
        y3 = sb("y3", [P, DI])
        yg = sb("yg", [P, DI])
        ysq = sb("ysq", [P, DI])
        ygT = sb("ygT", [P, DI])
        state = sb("state", [P, DI])
        ss = sb("ss", [P, 1])
        msq = sb("msq", [P, 1])
        rms = sb("rms", [P, 1])
        res = sb("res", [P, DM])
        bst = sb("bst", [P, 6])
        mv = sb("mv", [P, 2])
        vare = sb("vare", [P, 1])
        rstd = sb("rstd", [P, 1])
        x1 = sb("x1", [P, 2, XW])
        acc = sb("acc", [P, 2, DM])
        x1T = sb("x1T", [P, 2, KD, P])
        tok_p = sb("tok_p", [P, 1])
        lg = sb("lg", [P, NE + 1])
        top = sb("top", [P, 8])
        topi = sb("topi", [P, 8], U32)
        chf = sb("chf", [P, TOPK])
        negm = sb("negm", [P, 1])
        ex = sb("ex", [P, NE])
        ez = sb("ez", [P, 1])
        e4 = sb("e4", [P, TOPK])
        eg = sb("eg", [P, 1])
        rz = sb("rz", [P, 1])
        sg = sb("sg", [P, 2])
        oh = sb("oh", [P, TOPK, NE])
        mask = sb("mask", [P, NE])
        rs = sb("rs", [P, NE])
        osl = sb("osl", [P, TOPK, NE])
        slf = sb("slf", [P, TOPK])
        sloti = sb("sloti", [P, 2, TOPK], I32)
        gs = sb("gs", [P, 2, FI])
        hb = sb("hb", [P, 2, FI])
        hT = sb("hT", [HF, 2, 2, P])

        loaded = once("loaded")
        consts = once("consts")
        setup = once("setup")
        uT_in = [sem("uT_in0"), sem("uT_in1")]
        u_in = [sem("u_in0"), sem("u_in1")]
        scattered = [once("scattered0"), once("scattered1")]
        acc_out = [sem("acc_out0"), sem("acc_out1")]
        w13_in = once("w13_in")
        padded = once("padded_end")
        pa_made = sem("pa_made")
        raw_in = sem("raw_in")
        conv_made = sem("conv_made")
        xc_ready = sem("xc_ready")
        dt_proj = sem("dt_proj")
        dt_abs = sem("dt_abs")
        dt_exp = sem("dt_exp")
        dA_ready = sem("dA_ready")
        sums_made = sem("sums_made")
        dec_ready = sem("dec_ready")
        din_ready = sem("din_ready")
        xT_made = sem("xT_made")
        xtok_ready = sem("xtok_ready")
        btok_ready = sem("btok_ready")
        g_made = sem("g_made")
        gm_ready = sem("gm_ready")
        dAw_ready = sem("dAw_ready")
        diff_made = sem("diff_made")
        E_ready = sem("E_ready")
        M_ready = sem("M_ready")
        xs_ready = sem("xs_ready")
        zs_ready = sem("zs_ready")
        z_made = sem("z_made")
        inter_made = sem("inter_made")
        y1_ready = sem("y1_ready")
        y_made = sem("y_made")
        st_made = sem("st_made")
        state_ready = sem("state_ready")
        y2_ready = sem("y2_ready")
        yg_ready = sem("yg_ready")
        ss_ready = sem("ss_ready")
        rms_ready = sem("rms_ready")
        ygT_made = sem("ygT_made")
        ygT_ready = sem("ygT_ready")
        o_made = sem("o_made")
        res_ready = sem("res_ready")
        var_ready = sem("var_ready")
        std_ready = sem("std_ready")
        x1_ready = sem("x1_ready")
        x1T_made = sem("x1T_made")
        x1T_ready = sem("x1T_ready")
        lg_made = sem("lg_made")
        lg_ready = sem("lg_ready")
        rex_ready = sem("rex_ready")
        mask_ready = sem("mask_ready")
        rank_made = sem("rank_made")
        rank_read = sem("rank_read")
        slot_ready = sem("slot_ready")
        gs_ready = sem("gs_ready")
        h_ready = sem("h_ready")
        hT_made = sem("hT_made")
        hT_ready = sem("hT_ready")
        dn_made = sem("dn_made")
        acc_ready = sem("acc_ready")
        dve_own = once("dve_own")
        pool_own = once("pool_own")

        LOADS = 14
        CONSTS = 11
        DVE_BASE = 1 + 15 + NG * (TAPS - 1)
        DVE_TURN = 15 + 2 * NG * (TAPS - 1) + CH * (11 + 3) + CH + CH - 1
        POOL_BASE = 5
        POOL_TURN = CH + CH - 1

        def at(c, w=P):
            return slice(c * w, c * w + w)

        def heads(ap):
            return ap.rearrange("p (h d) -> p h d", h=NH)

        def over(ap):
            return bc(ap, 2, [P, NH, HD])

        def uses(more):
            plan = []
            for c in range(CH + 1):
                if more and c == CH:
                    plan += [("raw", 0, NG - 2), ("raw", 0, NG - 1)]
                if c:
                    plan += [("up", c - 1, s) for s in range(NSL)]
                if c < QB - 1:
                    plan += [("raw", 1, 2 * c), ("raw", 1, 2 * c + 1)]
                if more and QB <= c < CH:
                    plan.append(("raw", 0, c - QB))
            return plan

        plans = {more: uses(more) for more in (True, False)}
        PA_TURN = len(plans[True])
        assert PA_TURN % 2 == 0 and NG % 2 == 0 and CH - QB == NG - 2
        kinds = {"raw": (raw_in, NG, 2 * NG), "up": (h_ready, 0, CH * NSL)}

        def bank_of(key, more):
            return PA[plans[more].index(key) % 2]

        def wait_pa(pe, b, key, more):
            plan = plans[more]
            n = plan.index(key) - 2
            if n >= 0:
                signal, first, per = kinds[plan[n][0]]
                pe.wait_ge(signal, met(first + b * per + sum(k[0] == plan[n][0] for k in plan[:n + 1])))
            else:
                for signal, first, per in kinds.values():
                    pe.wait_ge(signal, met(first + b * per))

        def turns(eng, turn):
            with eng.Fori(0, BATCH - 1) as b:
                turn(b, True)
            turn(BATCH - 1, False)

        start(nc, looped)
        with nc.Block() as block:
            @block.sync
            def _(sp):
                for t, src in ((win, w_in), (cw, conv_w), (cb, conv_b), (dtb, dt_bias), (ah, a_log),
                               (dsk, d_skip), (nw, norm_w), (wout, w_out), (gw, gate), (sdn, down[:, NE:])):
                    sp.dma_start(t[:], src).then_inc(loaded, 16)
                for s in range(NSL):
                    sp.dma_start(sup[:, s], up[:, NE + s]).then_inc(loaded, 16)
                for k in range(2):
                    sp.dma_start(uTb[:, k], uT[:, :, k * BLK:(k + 1) * BLK]).then_inc(uT_in[k], 16)

                def turn(b, more):
                    for c in range(CH + 1):
                        if c < CH:
                            sp.wait_ge(res_ready, met(b * CH + max(c - 1, 0)))
                            sp.dma_start(ut[:, c % 2], u[bass.ds(b * SEQ + c * P, P), :]).then_inc(u_in[c % 2], 16)
                        if more and c in (QB - 1, CH - 1):
                            k = c // QB
                            sp.wait_ge(z_made, met(b * CH + c + 1))
                            sp.dma_start(uTb[:, k], uT[:, :, bass.ds((b + 1) * SEQ + k * BLK, BLK)]).then_inc(uT_in[k], 16)
                        if c:
                            sp.wait_ge(acc_ready, met(b * CH + c))
                            sp.dma_start(kept.base[bass.ds(b * SEQ + (c - 1) * P, P), :],
                                         acc[:, (c - 1) % 2]).then_inc(acc_out[(c - 1) % 2], 16)
                    part = NE // BATCH * KD * 2 * FI
                    sp.dma_start(kept.w13[:, bass.ds(b * part, part)],
                                 up[:, bass.ds(b * (NE // BATCH), NE // BATCH)].rearrange("p e k n -> p (e k n)")).then_inc(w13_in, 16)
                sp.wait_ge(consts, CONSTS)

                turns(sp, turn)
                sp.dma_start(kept.x_rows[NE * REGION:NE * REGION + P, :], kept.padrow[:]).then_inc(padded, 16)
                for j in range(2):
                    sp.wait_ge(acc_out[j], met(NC // 2 * 16))
                sp.wait_ge(padded, 16)
                sp.wait_ge(w13_in, BATCH * 16)

            @block.gpsimd
            def _(pool):
                pool.memset(ident[:], 0.0).then_inc(pool_own, 1)
                pool.memset(incl[:], 1.0).then_inc(pool_own, 1)
                pool.memset(later[:], 1.0).then_inc(pool_own, 1)
                pool.memset(before[:], 1.0).then_inc(pool_own, 1)
                pool.memset(ones[:], 1.0).then_inc(consts, 1)
                pool.memset(half[:], -0.5).then_inc(consts, 1)
                pool.memset(kept.padrow[:], 0.0).then_inc(pool_own, 1)
                pool.iota(kept.iota_e[:], [[1, NE]], base=0, channel_multiplier=0,
                          allow_small_or_imprecise_dtypes=True).then_inc(consts, 1)
                pool.iota(tok_p[:], [[0, 1]], base=0, channel_multiplier=1,
                          allow_small_or_imprecise_dtypes=True).then_inc(consts, 1)
                pool.wait_ge(pool_own, POOL_BASE)
                pool.memset(kept.padrow[:, ODD:XW], float(P)).then_inc(consts, 1)
                pool.memset(kept.padrow[:, DM + TOPK:DM + 2 * TOPK], -1.0).then_inc(consts, 1)
                pool.iota(kept.padrow[:, YROW:ODD], [[0, 1]], base=NC * P * TOPK, channel_multiplier=1,
                          allow_small_or_imprecise_dtypes=True).then_inc(consts, 1)
                pool.affine_select(out=ident[:], in_=ident[:], compare_op=ALU.not_equal, fill=1.0, base=0,
                                   pattern=[[-1, P]], channel_multiplier=1).then_inc(consts, 1)
                pool.affine_select(out=incl[:], in_=incl[:], compare_op=ALU.is_ge, fill=0.0, base=0,
                                   pattern=[[1, P]], channel_multiplier=-1).then_inc(consts, 1)
                pool.affine_select(out=later[:], in_=later[:], compare_op=ALU.is_ge, fill=0.0, base=-1,
                                   pattern=[[-1, P]], channel_multiplier=1).then_inc(consts, 1)
                pool.affine_select(out=before[:], in_=before[:], compare_op=ALU.is_ge, fill=0.0, base=-1,
                                   pattern=[[1, P]], channel_multiplier=-1).then_inc(consts, 1)
                pool.wait_ge(consts, CONSTS)
                pool.wait_ge(loaded, 16 * LOADS)
                prime(pool, kept, scattered)

                def spread(b, c):
                    pool.wait_ge(dA_ready, met(b + 1))
                    pool.wait_ge(diff_made, met((b * CH + c) * 2))
                    pool.tensor_tensor(dAw[:], bc(incl[:], 1, [P, NH, P]),
                                       bc(dA[:, at(c, NH)], 2, [P, NH, P]), ALU.mult).then_inc(dAw_ready, 1)

                def turn(b, more):
                    own = Steps(pool, pool_own, POOL_BASE + b * POOL_TURN)
                    for c in range(CH + 1):
                        if c < CH:
                            pool.wait_ge(xtok_ready, met(b * CH + c + 1))
                            pool.wait_ge(din_ready, met(b + 1))
                            pool.wait_ge(st_made, met(b * CH + c))
                            pool.tensor_tensor(heads(xs[:]), heads(xtok[:, c % 2]), over(din[:, at(c, NH)]),
                                               ALU.mult).then_inc(xs_ready, 1)
                            if c:
                                own.done(pool.tensor_tensor(heads(xD[:]), heads(xtok[:, c % 2]), over(dsk[:]), ALU.mult))
                            else:
                                pool.wait_ge(yg_ready, met(b * CH))
                                pool.tensor_tensor(heads(y2[:]), heads(xtok[:, c % 2]), over(dsk[:]),
                                                   ALU.mult).then_inc(y2_ready, 1)
                        if c < CH - 1:
                            spread(b, c + 1)
                        if 0 < c < CH:
                            pool.wait_ge(y1_ready, met(b * (CH - 1) + c))
                            pool.wait_ge(yg_ready, met(b * CH + c))
                            pool.tensor_tensor(y2[:], y1[:], xD[:], ALU.add).then_inc(y2_ready, 1)
                        if c:
                            pool.wait_ge(slot_ready, met(b * CH + c))
                            waits_end(pool)
                            for j in range(TOPK):
                                pool.indirect_dma_start(
                                    kept.x_rows,
                                    bass.IndirectOffsetOnAxis(ap=sloti[:, (c - 1) % 2, j:j + 1].bitcast(U32), axis=0),
                                    x1[:, (c - 1) % 2], None).then_inc(scattered[(c - 1) % 2], 16)
                        if c < CH:
                            pool.wait_ge(ss_ready, met(b * CH + c + 1))
                            waits_end(pool)
                            own.done(pool.tensor_scalar(msq[:], ss[:], 1.0 / DI, EPS, ALU.mult, ALU.add))
                            pool.tensor_tensor(rms[:], msq[:], half[:], ALU.pow).then_inc(rms_ready, 1)
                            pool.wait_ge(var_ready, met(b * CH + c + 1))
                            pool.tensor_tensor(rstd[:], vare[:], half[:], ALU.pow).then_inc(std_ready, 1)
                    if more:
                        spread(b + 1, 0)

                spread(0, 0)
                turns(pool, turn)

            @block.tensor
            def _(pe):
                pe.wait_ge(consts, CONSTS)
                pe.wait_ge(loaded, 16 * LOADS)
                pe.wait_ge(setup, 5)

                def project(bank, k, g):
                    for d in range(KD):
                        mm = pe.matmul(bank[:], win[:, d, at(NG - 2 + g)], uTb[:, k, d, :], start=d == 0, stop=d == KD - 1)
                    mm.then_inc(pa_made, 1)

                def project_dt(b):
                    pe.wait_ge(uT_in[0], met(b * 16 + 16))
                    pe.wait_ge(uT_in[1], met(b * 16 + 16))
                    pe.wait_ge(ygT_ready, met(b * CH))
                    for c in range(CH):
                        for d in range(KD):
                            mm = pe.matmul(PX[:, at(c, NH)], uTb[:, c // QB, d, at(c % QB)], win[:, d, PROJ - NH:PROJ],
                                           start=d == 0, stop=d == KD - 1)
                    mm.then_inc(dt_proj, 1)

                def sum_decays(b):
                    pe.wait_ge(dA_ready, met(b + 1))
                    for j, m in enumerate((incl, later, ones)):
                        mm = pe.matmul(PX[:, at(1 + j, CH * NH)], m[:], dA[:], start=True, stop=True)
                    mm.then_inc(sums_made, 1)

                def turn(b, more):
                    def project_turn(k, g):
                        key = ("raw", k, g)
                        wait_pa(pe, b, key, more)
                        if k == 0:
                            pe.wait_ge(uT_in[0], met(b * 16 + 32))
                        project(bank_of(key, more), k, g)

                    def slice_up(c, s):
                        wait_pa(pe, b, ("up", c, s), more)
                        for d in range(KD):
                            mm = pe.matmul(bank_of(("up", c, s), more)[:, 0:2 * FI], x1T[:, c % 2, d], sup[:, s, d],
                                           start=d == 0, stop=d == KD - 1)
                        mm.then_inc(pa_made, 1)

                    def slice_turn(c, s):
                        n = (b * CH + c) * NSL + s
                        pe.wait_ge(h_ready, met(n + 1))
                        pe.wait_ge(hT_ready, met(n))
                        for j in range(2):
                            mm = pe.transpose(PG[0:HF, DM + j * P:DM + (j + 1) * P], hb[:, s % 2, at(j, HF)], ident[:])
                        mm.then_inc(hT_made, 1)

                    def slice_down(c, s):
                        pe.wait_ge(hT_ready, met((b * CH + c) * NSL + s + 1))
                        if s == 0:
                            pe.wait_ge(acc_ready, met(b * CH + c))
                        for j in range(2):
                            mm = pe.matmul(PO[:, 0:DM], hT[:, s % 2, j], sdn[:, s, j],
                                           start=s == 0 and j == 0, stop=s == NSL - 1 and j == 1)
                        if s == NSL - 1:
                            mm.then_inc(dn_made, 1)

                    def rank(c):
                        pe.wait_ge(mask_ready, met(b * CH + c + 1))
                        pe.matmul(PY[:, RANK:RANK + NE], before[:], mask[:], start=True, stop=True)
                        pe.matmul(PY[:, TOT:TOT + NE], ones[:], mask[:], start=True, stop=True).then_inc(rank_made, 1)

                    for c in range(CH + 1):
                        n = b * CH + c
                        k, q = c // QB, c % QB
                        if c < CH:
                            pe.wait_ge(xc_ready, met((b * 2 + k + 1) * NG))
                            pe.wait_ge(ygT_ready, met(n))
                            pe.wait_ge(dec_ready, met(b + 1))
                            for j in range(KI):
                                mm = pe.transpose(PX[:, at(j)], xc[:, k, j, at(q)], ident[:])
                            mm.then_inc(xT_made, 1)
                            pe.wait_ge(hT_ready, met((b * CH + max(c - 1, 0)) * NSL))
                            pe.wait_ge(gm_ready, met(n))
                            pe.transpose(PG[:, P:2 * P], xc[:, k, GB, at(q)], ident[:])
                            pe.matmul(PG[:, 0:P], xc[:, k, GB, at(q)], xc[:, k, GC, at(q)],
                                      start=True, stop=True).then_inc(g_made, 1)
                            pe.wait_ge(dAw_ready, met(n + 1))
                            if c:
                                pe.wait_ge(y1_ready, met(b * (CH - 1) + c - 1))
                            pe.wait_ge(state_ready, met(n))
                            for j in range(2):
                                pe.matmul(PD[j][:], later[:], dAw[:, 4 * j:4 * j + 4],
                                          start=True, stop=True).then_inc(diff_made, 1)
                        if more and c == CH:
                            project_dt(b + 1)
                            project_turn(0, NG - 2)
                            project_turn(0, NG - 1)
                        if c:
                            pe.wait_ge(x1_ready, met(n))
                            for d in range(KD):
                                mm = pe.transpose(PY[:, DM + d * P:DM + (d + 1) * P], x1[:, (c - 1) % 2, at(d)], ident[:])
                            mm.then_inc(x1T_made, 1)
                        if more and c == CH:
                            sum_decays(b + 1)
                        if c < CH:
                            pe.wait_ge(xtok_ready, met(n + 1))
                            for d in range(KD):
                                mm = pe.matmul(PX[:], uTb[:, k, d, at(q)], win[:, d, 0:DI], start=d == 0, stop=d == KD - 1)
                            mm.then_inc(z_made, 1)
                        if c:
                            pe.wait_ge(x1T_ready, met(n))
                            for d in range(KD):
                                mm = pe.matmul(PY[:, 0:NE + 1], x1T[:, (c - 1) % 2, d], gw[:, d], start=d == 0, stop=d == KD - 1)
                            mm.then_inc(lg_made, 1)
                            slice_up(c - 1, 0)
                            slice_up(c - 1, 1)
                            rank(c - 1)
                        if c < CH:
                            if c:
                                pe.wait_ge(E_ready, met(2 * n + 1))
                                pe.matmul(PD[0][:], xc[:, k, GC, at(q)], state[:], start=True, stop=True).then_inc(inter_made, 1)
                            pe.wait_ge(rank_read, met(n))
                            for h in range(NH):
                                if h % 4 == 0:
                                    pe.wait_ge(M_ready, met(2 * n + 1 + h // 4))
                                mm = pe.matmul(PY[:, at(h, HD)], M[:, h], xtok[:, c % 2, at(h, HD)],
                                               start=True, stop=True)
                            mm.then_inc(y_made, 1)
                            pe.wait_ge(xs_ready, met(n + 1))
                            pe.wait_ge(btok_ready, met(n + 1))
                            pe.matmul(PD[1][:], btok[:, c % 2], xs[:], start=True, stop=True).then_inc(st_made, 1)
                        if c:
                            if c < CH:
                                pe.wait_ge(gm_ready, met(n + 1))
                            slice_turn(c - 1, 0)
                            slice_up(c - 1, 2)
                            slice_down(c - 1, 0)
                            slice_turn(c - 1, 1)
                            slice_up(c - 1, 3)
                        if c < CH:
                            pe.wait_ge(yg_ready, met(n + 1))
                            for j in range(KI):
                                mm = pe.transpose(PX[:, at(j)], yg[:, at(j)], ident[:])
                            mm.then_inc(ygT_made, 1)
                        if c:
                            slice_down(c - 1, 1)
                            slice_turn(c - 1, 2)
                        if c < CH:
                            pe.wait_ge(ygT_ready, met(n + 1))
                            for j in range(KI):
                                mm = pe.matmul(PY[:, 0:DM], ygT[:, at(j)], wout[:, j], start=j == 0, stop=j == KI - 1)
                            mm.then_inc(o_made, 1)
                        if c:
                            slice_turn(c - 1, 3)
                            slice_down(c - 1, 2)
                        if c < QB - 1:
                            project_turn(1, 2 * c)
                            project_turn(1, 2 * c + 1)
                        if more and QB <= c < CH:
                            project_turn(0, c - QB)
                        if c:
                            slice_down(c - 1, 3)

                project_dt(0)
                for g in range(NG):
                    if g >= 2:
                        pe.wait_ge(raw_in, met(g - 1))
                    project(PA[g % 2], 0, g)
                sum_decays(0)
                turns(pe, turn)

            @block.scalar
            def _(act):
                act.wait_ge(loaded, 16 * LOADS)
                act.activation(E[:, 0, 0:NH], ah[:], ACT.Exp).then_inc(setup, 1)

                def raw_copy(bank, b, k, g, made):
                    act.wait_ge(pa_made, met(made))
                    act.wait_ge(conv_made, met(b * 2 * NG + k * NG))
                    if k == 0:
                        act.copy(raw[:, 1, g, 0:HALO], bank[:, BLK - HALO:BLK])
                    act.copy(raw[:, k, g, HALO:HALO + BLK], bank[:]).then_inc(raw_in, 1)

                def conv_silu(b, k, g):
                    act.wait_ge(conv_made, met((b * 2 + k) * NG + g + 1))
                    act.activation(xc[:, k, g], xc[:, k, g], ACT.Silu).then_inc(xc_ready, 1)

                def dt_exponent(b):
                    act.wait_ge(dt_abs, met(b + 1))
                    act.activation(dtw[:, 2], dtw[:, 1], ACT.Exp).then_inc(dt_exp, 1)

                def decays(b):
                    act.wait_ge(sums_made, met(b + 1))
                    act.activation(dec[:].rearrange("p a n -> p (a n)"), PX[:, CH * NH:4 * CH * NH], ACT.Exp).then_inc(dec_ready, 1)

                def turn(b, more):
                    def made(key):
                        return NG + b * PA_TURN + plans[more].index(key) + 1

                    def raw_turn(k, g):
                        key = ("raw", k, g)
                        raw_copy(bank_of(key, more), b + 1 - k, k, g, made(key))

                    def slice_silu(c, s):
                        act.wait_ge(pa_made, met(made(("up", c, s))))
                        act.wait_ge(h_ready, met(b * CH * NSL + max(c * NSL + s - 1, 0)))
                        act.activation(gs[:, s % 2], bank_of(("up", c, s), more)[:, 0:FI], ACT.Silu).then_inc(gs_ready, 1)

                    def slice_copy(c, s):
                        n = (b * CH + c) * NSL + s
                        act.wait_ge(hT_made, met(n + 1))
                        if s == 0:
                            act.wait_ge(dn_made, met(b * CH + c))
                        act.copy(hT[:, s % 2].rearrange("p j t -> p (j t)"), PG[0:HF, DM:2 * DM]).then_inc(hT_ready, 1)

                    for c in range(CH + 1):
                        n = b * CH + c
                        if c < CH:
                            act.wait_ge(xT_made, met(n + 1))
                            act.wait_ge(y_made, met(b * CH + max(c - 1, 0)))
                            act.wait_ge(yg_ready, met(b * CH + max(c - 1, 0)))
                            act.copy(xtok[:, c % 2], PX[:]).then_inc(xtok_ready, 1)
                            act.wait_ge(g_made, met(n + 1))
                            act.wait_ge(st_made, met(b * CH + max(c - 1, 0)))
                            act.wait_ge(gm_ready, met(n + 1))
                            act.copy(btok[:, c % 2], PG[:, P:2 * P]).then_inc(btok_ready, 1)
                            act.wait_ge(M_ready, met(2 * n))
                            for j in range(2):
                                act.wait_ge(diff_made, met(2 * n + j + 1))
                                act.activation(E[:, 4 * j:4 * j + 4].rearrange("p h t -> p (h t)"), PD[j][:],
                                               ACT.Exp).then_inc(E_ready, 1)
                        if more and c == CH:
                            dt_exponent(b + 1)
                            raw_turn(0, NG - 2)
                            raw_turn(0, NG - 1)
                        if c:
                            act.wait_ge(x1T_made, met(n))
                            act.wait_ge(dn_made, met(b * CH + max(c - 2, 0)))
                            act.copy(x1T[:, (c - 1) % 2].rearrange("p k t -> p (k t)"), PY[:, DM:2 * DM]).then_inc(x1T_ready, 1)
                            if more and c == CH:
                                decays(b + 1)
                            act.wait_ge(lg_ready, met(n))
                            act.activation(ex[:], lg[:, 0:NE], ACT.Exp, bias=negm[:], accum_out=ez[:])
                            act.activation(e4[:], top[:, 0:TOPK], ACT.Exp, bias=negm[:])
                            act.activation(eg[:], lg[:, NE:NE + 1], ACT.Exp, scale=-1.0).then_inc(rex_ready, 1)
                        if c < CH:
                            act.wait_ge(z_made, met(n + 1))
                            act.wait_ge(yg_ready, met(n))
                            act.activation(zs[:], PX[:], ACT.Silu).then_inc(zs_ready, 1)
                        if c:
                            slice_silu(c - 1, 0)
                            slice_silu(c - 1, 1)
                            slice_copy(c - 1, 0)
                            slice_silu(c - 1, 2)
                            slice_copy(c - 1, 1)
                            slice_silu(c - 1, 3)
                        if c < CH:
                            act.wait_ge(ygT_made, met(n + 1))
                            act.wait_ge(o_made, met(n))
                            act.copy(ygT[:], PX[:]).then_inc(ygT_ready, 1)
                        if c:
                            slice_copy(c - 1, 2)
                        if c < CH:
                            act.wait_ge(yg_ready, met(n + 1))
                            act.wait_ge(rms_ready, met(n))
                            act.activation(ysq[:], yg[:], ACT.Square, accum_out=ss[:]).then_inc(ss_ready, 1)
                        if c:
                            slice_copy(c - 1, 3)
                        if 0 < c < QB:
                            conv_silu(b, 1, 2 * c - 2)
                            conv_silu(b, 1, 2 * c - 1)
                        if more and c > QB:
                            conv_silu(b + 1, 0, c - QB - 1)
                        if c < QB - 1:
                            raw_turn(1, 2 * c)
                            raw_turn(1, 2 * c + 1)
                        if more and QB <= c < CH:
                            raw_turn(0, c - QB)
                        if more and c == CH:
                            conv_silu(b + 1, 0, NG - 2)
                            conv_silu(b + 1, 0, NG - 1)

                dt_exponent(0)
                for g in range(NG):
                    raw_copy(PA[g % 2], 0, 0, g, g + 1)
                for g in range(NG):
                    conv_silu(0, 0, g)
                decays(0)
                turns(act, turn)

            @block.vector
            def _(dve):
                dve.memset(raw[:, 0, :, 0:HALO], 0.0).then_inc(dve_own, 1)
                dve.wait_ge(loaded, 16 * LOADS)
                dve.wait_ge(consts, CONSTS)
                dve.wait_ge(setup, 1)
                dve.tensor_scalar(ah[:], E[:, 0, 0:NH], -1.0, None, ALU.mult).then_inc(setup, 1)
                for j in range(KI):
                    w = dve.tensor_scalar(wout[:, j], wout[:, j], nw[:, j:j + 1], None, ALU.mult)
                w.then_inc(setup, 1)
                dve.tensor_scalar(kept.reg0[:], kept.iota_e[:], float(REGION), None, ALU.mult)
                dve.tensor_scalar(place[:], kept.iota_e[:], float(REGION), None, ALU.mult).then_inc(setup, 1)
                dve.memset(x1[:, :, ODD:XW], 0.0)
                for j in range(2):
                    w = dve.tensor_scalar(x1[:, j, YROW:ODD], tok_p[:], float(TOPK), float((j - 2) * P * TOPK), ALU.mult, ALU.add)
                w.then_inc(setup, 1)
                dve.wait_ge(setup, 5)

                def conv(own, b, k, g):
                    dve.wait_ge(raw_in, met((b * 2 + k) * NG + g + 1))
                    if g == 0:
                        n = b * CH if k else (b - 1) * CH + QB
                        if not (isinstance(n, int) and n <= 0):
                            dve.wait_ge(y_made, met(n))
                            dve.wait_ge(g_made, met(n))
                    x = xc[:, k, g]
                    own.done(dve.tensor_scalar(x, raw[:, k, g, 0:BLK], cw[:, g, 0:1], cb[:, g:g + 1], ALU.mult, ALU.add))
                    for j in range(1, TAPS):
                        ins = dve.scalar_tensor_tensor(x, raw[:, k, g, j:j + BLK], cw[:, g, j:j + 1], x, ALU.mult, ALU.add)
                        if j < TAPS - 1:
                            own.done(ins)
                    ins.then_inc(conv_made, 1)

                v, na, e, r, r2, pl, m0, t0 = (dtw[:, j] for j in range(8))

                def dt_values(own, b):
                    dve.wait_ge(dt_proj, met(b + 1))
                    own.done(dve.tensor_tensor(v.rearrange("p (c h) -> p c h", c=CH),
                                               PX[:, 0:CH * NH].rearrange("p (c h) -> p c h", c=CH),
                                               bc(dtb[:], 1, [P, CH, NH]), ALU.add))
                    dve.scalar_tensor_tensor(na, v, -1.0, v, ALU.mult, ALU.min).then_inc(dt_abs, 1)
                    dve.tensor_scalar(m0, v, 0.0, None, ALU.max)

                def softplus(own, b):
                    dve.wait_ge(dt_exp, met(b + 1))
                    own.done(dve.tensor_scalar(t0, e, 2.0, None, ALU.add))
                    own.done(dve.reciprocal(t0, t0))
                    own.done(dve.tensor_tensor(r, e, t0, ALU.mult))
                    own.done(dve.tensor_tensor(r2, r, r, ALU.mult))
                    own.done(dve.tensor_scalar(pl, r2, 1.0 / 17, None, ALU.mult))
                    for odd in (15, 13, 11, 9, 7, 5, 3):
                        own.done(dve.scalar_tensor_tensor(pl, pl, 1.0 / odd, r2, ALU.add, ALU.mult))
                    own.done(dve.scalar_tensor_tensor(pl, pl, 1.0, r, ALU.add, ALU.mult))
                    own.done(dve.scalar_tensor_tensor(dts[:], pl, 2.0, m0, ALU.mult, ALU.add))
                    dve.tensor_tensor(dA[:].rearrange("p (c h) -> p c h", c=CH),
                                      dts[:].rearrange("p (c h) -> p c h", c=CH),
                                      bc(ah[:], 1, [P, CH, NH]), ALU.mult).then_inc(dA_ready, 1)

                def weigh_inputs(b):
                    dve.wait_ge(dec_ready, met(b + 1))
                    dve.wait_ge(xs_ready, met(b * CH))
                    dve.tensor_tensor(din[:], dec[:, 1], dts[:], ALU.mult).then_inc(din_ready, 1)

                def turn(b, more):
                    own = Steps(dve, dve_own, DVE_BASE + b * DVE_TURN)

                    def route(c):
                        dve.wait_ge(lg_made, met(b * CH + c + 1))
                        dve.wait_ge(rex_ready, met(b * CH + c))
                        own.done(dve.tensor_copy(lg[:], PY[:, 0:NE + 1]), apart=True)
                        own.done(dve.max(top[:], lg[:, 0:NE]))
                        dve.tensor_scalar(negm[:], top[:, 0:1], -1.0, None, ALU.mult).then_inc(lg_ready, 1)
                        own.done(dve.max_index(topi[:], top[:], lg[:, 0:NE]))
                        own.done(dve.tensor_copy(chf[:], topi[:, 0:TOPK]))
                        dve.tensor_copy(x1[:, c % 2, DM + TOPK:DM + 2 * TOPK], chf[:])
                        own.done(dve.tensor_tensor(oh[:], bc(kept.iota_e[:], 1, [P, TOPK, NE]),
                                                   bc(chf[:], 2, [P, TOPK, NE]), ALU.is_equal))
                        dve.tensor_reduce(mask[:], oh[:].rearrange("p k e -> p e k"), AX.X, ALU.add).then_inc(mask_ready, 1)

                    def weigh(c):
                        dve.wait_ge(rex_ready, met(b * CH + c + 1))
                        own.done(dve.reciprocal(rz[:], ez[:]))
                        dve.tensor_scalar(x1[:, c % 2, DM:DM + TOPK], e4[:], rz[:], None, ALU.mult)
                        own.done(dve.tensor_scalar(sg[:, 0:1], eg[:], 1.0, None, ALU.add))
                        own.done(dve.reciprocal(sg[:, 1:2], sg[:, 0:1]))

                    def give_slots(c):
                        dve.wait_ge(rank_made, met(b * CH + c + 1))
                        dve.wait_ge(rank_read, met(b * CH + c))
                        own.done(dve.tensor_tensor(rs[:], PY[:, RANK:RANK + NE], place[:], ALU.add))
                        own.done(dve.tensor_tensor(osl[:], oh[:], bc(rs[:], 1, [P, TOPK, NE]), ALU.mult))
                        dve.tensor_tensor(place[:], PY[:, TOT:TOT + NE], place[:], ALU.add).then_inc(rank_read, 1)
                        own.done(dve.tensor_reduce(slf[:], osl[:], AX.X, ALU.add))
                        dve.wait_ge(scattered[c % 2], primed((b * (CH // 2) + c // 2) * 16 * TOPK))
                        dve.tensor_copy(sloti[:, c % 2], slf[:]).then_inc(slot_ready, 1)

                    def hidden(c, s):
                        n = (b * CH + c) * NSL + s
                        dve.wait_ge(gs_ready, met(n + 1))
                        dve.wait_ge(hT_made, met(b * CH * NSL + max(c * NSL + s - 1, 0)))
                        dve.tensor_tensor(hb[:, s % 2], gs[:, s % 2], bank_of(("up", c, s), more)[:, FI:2 * FI],
                                          ALU.mult).then_inc(h_ready, 1)

                    for c in range(CH + 1):
                        n = b * CH + c
                        if c < CH:
                            dve.wait_ge(g_made, met(n + 1))
                            dve.tensor_tensor(gm[:], PG[:, 0:P], incl[:], ALU.mult).then_inc(gm_ready, 1)
                            dve.wait_ge(gm_ready, met(n + 1))
                            dve.wait_ge(y_made, met(n))
                            for h in range(NH):
                                if h % 4 == 0:
                                    dve.wait_ge(E_ready, met(2 * n + 1 + h // 4))
                                ins = dve.scalar_tensor_tensor(M[:, h], E[:, h], dts[:, c * NH + h:c * NH + h + 1], gm[:],
                                                               ALU.mult, ALU.mult)
                                if h % 4 == 3:
                                    ins.then_inc(M_ready, 1)
                        if more and c == CH:
                            dt_values(own, b + 1)
                            softplus(own, b + 1)
                            conv(own, b + 1, 0, c - QB - 1)
                        if c:
                            route(c - 1)
                            weigh(c - 1)
                            give_slots(c - 1)
                        if more and c == CH:
                            weigh_inputs(b + 1)
                        if 0 < c < CH:
                            dve.wait_ge(inter_made, met(b * (CH - 1) + c))
                            dve.tensor_tensor(heads(y1[:]), heads(PD[0][:]), over(dec[:, 0, at(c, NH)]),
                                              ALU.mult).then_inc(y1_ready, 1)
                        if c:
                            hidden(c - 1, 0)
                            hidden(c - 1, 1)
                        if c < CH:
                            dve.wait_ge(y_made, met(n + 1))
                            dve.wait_ge(y2_ready, met(n + 1))
                            own.done(dve.tensor_tensor(y3[:], PY[:], y2[:], ALU.add))
                            dve.wait_ge(zs_ready, met(n + 1))
                            dve.wait_ge(ygT_made, met(n))
                            dve.wait_ge(ss_ready, met(n))
                            dve.tensor_tensor(yg[:], y3[:], zs[:], ALU.mult).then_inc(yg_ready, 1)
                            if c:
                                dve.wait_ge(state_ready, met(n))
                                own.done(dve.tensor_tensor(heads(state[:]), heads(state[:]), over(dec[:, 2, at(c, NH)]), ALU.mult))
                                dve.wait_ge(st_made, met(n + 1))
                                dve.tensor_tensor(state[:], PD[1][:], state[:], ALU.add).then_inc(state_ready, 1)
                            else:
                                dve.wait_ge(st_made, met(n + 1))
                                dve.tensor_copy(state[:], PD[1][:]).then_inc(state_ready, 1)
                        if c:
                            if c < QB:
                                conv(own, b, 1, 2 * c - 2)
                            if more and c == CH:
                                conv(own, b + 1, 0, NG - 2)
                            hidden(c - 1, 2)
                            hidden(c - 1, 3)
                            if c < QB:
                                conv(own, b, 1, 2 * c - 1)
                            if more and QB < c < CH:
                                conv(own, b + 1, 0, c - QB - 1)
                            if more and c == CH:
                                conv(own, b + 1, 0, NG - 1)
                        if c < CH:
                            dve.wait_ge(o_made, met(n + 1))
                            dve.wait_ge(rms_ready, met(n + 1))
                            dve.wait_ge(u_in[c % 2], met((b * (CH // 2) + c // 2 + 1) * 16))
                            dve.scalar_tensor_tensor(res[:], PY[:, 0:DM], rms[:], ut[:, c % 2], ALU.mult,
                                                     ALU.add).then_inc(res_ready, 1)
                            dve.wait_ge(res_ready, met(n + 1))
                            own.done(dve.bn_stats(bst[:], res[:]), apart=True)
                            own.done(dve.bn_aggr(mv[:], bst[:]))
                            dve.tensor_scalar(vare[:], mv[:, 1:2], EPS, None, ALU.add).then_inc(var_ready, 1)
                            dve.wait_ge(std_ready, met(n + 1))
                            dve.wait_ge(scattered[c % 2], primed((b * (CH // 2) + c // 2) * 16 * TOPK))
                            dve.tensor_scalar(x1[:, c % 2, 0:DM], res[:], mv[:, 0:1], rstd[:], ALU.subtract,
                                              ALU.mult).then_inc(x1_ready, 1)
                            own.done(dve.tensor_scalar(x1[:, c % 2, YROW:ODD], x1[:, c % 2, YROW:ODD],
                                                       float(2 * P * TOPK), None, ALU.add))
                        if c:
                            dve.wait_ge(dn_made, met(n))
                            dve.wait_ge(x1_ready, met(n))
                            dve.wait_ge(acc_out[(c - 1) % 2], met((b * (CH // 2) + (c - 1) // 2) * 16))
                            dve.scalar_tensor_tensor(acc[:, (c - 1) % 2], PO[:, 0:DM], sg[:, 1:2], x1[:, (c - 1) % 2, 0:DM],
                                                     ALU.mult, ALU.add).then_inc(acc_ready, 1)
                    if more:
                        assert own.n == DVE_TURN, own.n

                front = Steps(dve, dve_own, 1)
                dt_values(front, 0)
                softplus(front, 0)
                for g in range(NG):
                    conv(front, 0, 0, g)
                weigh_inputs(0)
                assert 1 + front.n == DVE_BASE, front.n
                turns(dve, turn)
                dve.wait_ge(scattered[0], primed(NC // 2 * TOPK * 16))
                dve.wait_ge(scattered[1], primed(NC // 2 * TOPK * 16))


def experts(nc, kept, down):
    pX, pU, pH, pO = (kept.banks[2 * j:2 * j + 2] for j in range(4))
    w13 = kept.w13

    with ExitStack() as ctx:
        def sb(name, shape, dt=F32):
            return ctx.enter_context(nc.sbuf_tensor(name, shape, dt))

        def sem(name):
            return ctx.enter_context(nc.semaphore(name))

        w2 = sb("w2", [HF, NE * 2 * DM])
        free = sb("free", [P, NE], I32)
        cnt = sb("cnt", [P, NE])
        cnti = sb("cnti", [P, NE], I32)
        tiles = sb("tiles", [P, NE])
        ones_e = sb("ones_e", [P, NE])
        ends = sb("ends", [P, NE])
        jump = sb("jump", [P, NE])
        tile_no = sb("tile_no", [P, TILES])
        past = sb("past", [P, TILES, NE])
        pastj = sb("pastj", [P, TILES, NE])
        expert = sb("expert", [P, TILES])
        jumped = sb("jumped", [P, TILES])
        row = sb("row", [P, TILES])
        table = sb("table", [P, 3, TILES], I32)
        xr = sb("xr", [P, RING, XW])
        hit = sb("hit", [P, RING, TOPK])
        nth = sb("nth", [P, TOPK])
        pair = sb("pair", [P, RING, 2, TOPK])
        chosen = sb("chosen", [P, RING, 2])
        y_row = sb("y_row", [P, RING], I32)
        xT = sb("xT", [P, 2, KD, P])
        gs = sb("gse", [P, 2, FI])
        hb = sb("hbe", [P, 2, FI])
        hT = sb("hTe", [HF, 2, 2, P])
        yo = sb("yo", [P, 2, DM])

        w2_in = sem("w2_in")
        nums = sem("nums")
        own_sem = sem("layout_own")
        free_ready = sem("free_ready")
        padded = sem("padded")
        table_ready = sem("table_ready")
        x_in = [sem(f"x_in{j}") for j in range(RING)]
        picked = sem("picked")
        xT_made = sem("xT_made_e")
        xT_ready = sem("xT_ready_e")
        u_made = sem("u_made")
        gs_ready = sem("gs_ready_e")
        h_ready = sem("h_ready_e")
        hT_made = sem("hT_made_e")
        hT_ready = sem("hT_ready_e")
        d_made = sem("d_made")
        yo_ready = sem("yo_ready")
        scattered = [sem("scattered0_e"), sem("scattered1_e")]
        LAYOUT = 10

        def pad(eng, experts_of):
            eng.wait_ge(free_ready, 1)
            for e in experts_of:
                at_row = eng.value_load(free[0:1, e:e + 1], min_val=0, max_val=NE * REGION - P)
                eng.dma_start(kept.x_rows[bass.ds(at_row, P), :], kept.padrow[:]).then_inc(padded, 16)

        def turns(eng, step):
            for k in range(RING):
                step(k, k, 0, True)
            with eng.Fori(1, TILES // RING) as i:
                for k in range(RING):
                    step(RING * i + k, k, i, False)

        with nc.Block() as block:
            @block.sync
            def _(sp):
                for e in range(0, NE, 4):
                    sp.dma_start(w2[:, e * 2 * DM:(e + 4) * 2 * DM],
                                 down[:, e:e + 4].rearrange("p e k n -> p (e k n)")).then_inc(w2_in, 16)
                pad(sp, range(0, NE, 2))
                sp.wait_ge(table_ready, 3)
                sp.wait_ge(padded, NE * 16)

                def load(t, k, turn, first):
                    at_row = sp.value_load(table[0:1, 2, bass.ds(t, 1)], min_val=0, max_val=NE * REGION)
                    if not first:
                        sp.wait_ge(xT_made, t - RING + 1)
                        sp.wait_ge(picked, t - RING + 1)
                    sp.dma_start(xr[:, k], kept.x_rows[bass.ds(at_row, P), :]).then_inc(x_in[k], 16)

                turns(sp, load)

            @block.gpsimd
            def _(pool):
                pool.iota(tile_no[:], [[1, TILES]], base=0, channel_multiplier=0,
                          allow_small_or_imprecise_dtypes=True).then_inc(nums, 1)
                pool.memset(ones_e[:], 1.0).then_inc(nums, 1)
                pool.iota(nth[:], [[1, TOPK]], base=0, channel_multiplier=0,
                          allow_small_or_imprecise_dtypes=True).then_inc(nums, 1)
                prime(pool, kept, scattered)
                def scatter(t, k, turn, first):
                    pool.wait_ge(yo_ready, t + 1)
                    waits_end(pool)
                    pool.indirect_dma_start(
                        kept.y_rows, bass.IndirectOffsetOnAxis(ap=y_row[:, k:k + 1].bitcast(U32), axis=0),
                        yo[:, k % 2], None).then_inc(scattered[k % 2], 16)

                turns(pool, scatter)
                pool.wait_ge(scattered[0], primed(TILES // 2 * 16))
                pool.wait_ge(scattered[1], primed(TILES // 2 * 16))

            @block.tensor
            def _(pe):
                pe.wait_ge(table_ready, 3)
                pe.wait_ge(w2_in, NE // 4 * 16)

                def up_column(t):
                    return pe.value_load(table[0:1, 0, bass.ds(t, 1)], min_val=0, max_val=(NE - 1) * KD * 2 * FI)

                def down_column(t):
                    return pe.value_load(table[0:1, 1, bass.ds(t, 1)], min_val=0, max_val=(NE - 1) * 2 * DM)

                def turn_rows(t, k, turn):
                    pe.wait_ge(x_in[k], turn * 16 + 16)
                    for d in range(KD):
                        mm = pe.transpose(pX[k % 2][:, d * P:(d + 1) * P], xr[:, k, d * P:(d + 1) * P], kept.ident[:])
                    mm.then_inc(xT_made, 1)

                def go_up(t, k, column):
                    pe.wait_ge(xT_ready, t + 1)
                    for d in range(KD):
                        mm = pe.matmul(pU[k % 2][:, 0:2 * FI], xT[:, k % 2, d],
                                       w13[:, bass.ds(column + d * 2 * FI, 2 * FI)], start=d == 0, stop=d == KD - 1)
                    mm.then_inc(u_made, 1)

                def turn_hidden(t, k):
                    pe.wait_ge(h_ready, t + 1)
                    for j in range(2):
                        mm = pe.transpose(pH[k % 2][0:HF, j * P:(j + 1) * P], hb[:, k % 2, j * HF:(j + 1) * HF], kept.ident[:])
                    mm.then_inc(hT_made, 1)

                def go_down(t, k, column, first=False):
                    pe.wait_ge(hT_ready, t + 1)
                    if not first:
                        pe.wait_ge(yo_ready, t - 1)
                    for j in range(2):
                        mm = pe.matmul(pO[k % 2][:, 0:DM], hT[:, k % 2, j], w2[:, bass.ds(column + j * DM, DM)],
                                       start=j == 0, stop=j == 1)
                    mm.then_inc(d_made, 1)

                turn_rows(0, 0, 0)
                for k in range(RING):
                    if k >= 2:
                        go_down(k - 2, k - 2, down_column(k - 2), first=True)
                    if k >= 1:
                        turn_hidden(k - 1, k - 1)
                    go_up(k, k, up_column(k))
                    turn_rows(k + 1, (k + 1) % RING, (k + 1) // RING)

                def four(turn, last):
                    down_at, up_at = down_column(RING * turn - 2), up_column(RING * turn)
                    for k in range(RING):
                        t = RING * turn + k
                        go_down(t - 2, (k - 2) % RING, down_at)
                        turn_hidden(t - 1, (k - 1) % RING)
                        go_up(t, k, up_at)
                        if k < RING - 1:
                            down_at, up_at = down_column(t - 1), up_column(t + 1)
                        if not (last and k == RING - 1):
                            turn_rows(t + 1, (k + 1) % RING, turn + (k + 1) // RING)

                with pe.Fori(1, TILES // RING - 1) as turn:
                    four(turn, False)
                four(TILES // RING - 1, True)
                go_down(TILES - 2, 2, down_column(TILES - 2))
                turn_hidden(TILES - 1, 3)
                go_down(TILES - 1, 3, down_column(TILES - 1))

            @block.scalar
            def _(act):
                def copy_rows(t, k):
                    act.wait_ge(xT_made, t + 1)
                    act.copy(xT[:, k % 2].rearrange("p k t -> p (k t)"), pX[k % 2][:, 0:DM]).then_inc(xT_ready, 1)

                def copy_hidden(t, k, first=False):
                    act.wait_ge(hT_made, t + 1)
                    if not first:
                        act.wait_ge(d_made, t - 1)
                    act.copy(hT[:, k % 2].rearrange("p k t -> p (k t)"), pH[k % 2][0:HF, 0:2 * P]).then_inc(hT_ready, 1)

                def gate(t, k):
                    act.wait_ge(u_made, t + 1)
                    act.activation(gs[:, k % 2], pU[k % 2][:, 0:FI], ACT.Silu).then_inc(gs_ready, 1)

                pad(act, range(1, NE, 2))
                copy_rows(0, 0)
                for k in range(RING):
                    if k >= 1:
                        copy_hidden(k - 1, k - 1, first=k < 3)
                    gate(k, k)
                    copy_rows(k + 1, (k + 1) % RING)

                def four(turn, last):
                    for k in range(RING):
                        t = RING * turn + k
                        copy_hidden(t - 1, (k - 1) % RING)
                        gate(t, k)
                        if not (last and k == RING - 1):
                            copy_rows(t + 1, (k + 1) % RING)

                with act.Fori(1, TILES // RING - 1) as turn:
                    four(turn, False)
                four(TILES // RING - 1, True)
                copy_hidden(TILES - 1, 3)

            @block.vector
            def _(dve):
                own = Steps(dve, own_sem)
                dve.wait_ge(nums, 3)
                dve.tensor_copy(free[:], kept.place[:]).then_inc(free_ready, 1)
                own.done(dve.tensor_tensor(cnt[:], kept.place[:], kept.reg0[:], ALU.subtract))
                own.done(dve.tensor_scalar(cnti[:], cnt[:], float(P - 1), None, ALU.add))
                own.done(dve.tensor_scalar(cnti[:], cnti[:], 7, None, ALU.arith_shift_right))
                own.done(dve.tensor_copy(tiles[:], cnti[:]))
                own.done(dve.tensor_tensor_scan(ends[:], ones_e[:], tiles[:], 0.0, ALU.mult, ALU.add))
                own.done(dve.tensor_scalar(jump[:], tiles[:], -float(P), float(REGION), ALU.mult, ALU.add))
                own.done(dve.tensor_tensor(past[:], bc(tile_no[:], 2, [P, TILES, NE]), bc(ends[:], 1, [P, TILES, NE]), ALU.is_ge))
                own.done(dve.tensor_tensor(pastj[:], past[:], bc(jump[:], 1, [P, TILES, NE]), ALU.mult))
                dve.tensor_reduce(expert[:], past[:], AX.X, ALU.add)
                own.done(dve.tensor_reduce(jumped[:], pastj[:], AX.X, ALU.add))
                own.done(dve.scalar_tensor_tensor(row[:], tile_no[:], float(P), jumped[:], ALU.mult, ALU.add))
                for j, width in enumerate((KD * 2 * FI, 2 * DM)):
                    dve.tensor_scalar(table[:, j], expert[:], float(NE - 1), float(width), ALU.min, ALU.mult).then_inc(table_ready, 1)
                dve.tensor_scalar(table[:, 2], row[:], float(NE * REGION), None, ALU.min).then_inc(table_ready, 1)
                assert own.n == LAYOUT, own.n

                def pick(t, k, turn, n):
                    dve.wait_ge(x_in[k], turn * 16 + 16)
                    dve.tensor_tensor(hit[:, k], xr[:, k, DM + TOPK:DM + 2 * TOPK],
                                      expert[:, bass.ds(t, 1)].to_broadcast([P, TOPK]), ALU.is_equal).then_inc(own_sem, 1)
                    dve.wait_ge(own_sem, n + 1)
                    dve.tensor_tensor(pair[:, k, 0], hit[:, k], xr[:, k, DM:DM + TOPK], ALU.mult)
                    dve.tensor_tensor(pair[:, k, 1], hit[:, k], nth[:], ALU.mult).then_inc(own_sem, 1)
                    dve.wait_ge(own_sem, n + 2)
                    dve.tensor_reduce(chosen[:, k], pair[:, k], AX.X, ALU.add).then_inc(own_sem, 1)

                def place_row(k):
                    if k % 2 == 0:
                        dve.tensor_tensor(y_row[:, k:k + 1], xr[:, k, YROW:ODD], chosen[:, k, 1:2], ALU.add).then_inc(picked, 1)
                    else:
                        dve.scalar_tensor_tensor(y_row[:, k:k + 1], xr[:, k, YROW:ODD], chosen[:, k, 1:2], xr[:, k, ODD:XW],
                                                 ALU.add, ALU.add).then_inc(picked, 1)

                def emit(t, k, n, before=None):
                    dve.wait_ge(own_sem, n)
                    dve.wait_ge(d_made, t + 1)
                    if before is not None:
                        dve.wait_ge(scattered[k % 2], primed(before * 16))
                    dve.tensor_scalar(yo[:, k % 2], pO[k % 2][:, 0:DM], chosen[:, k, 0:1], None,
                                      ALU.mult).then_inc(yo_ready, 1)

                def hide(t, k):
                    dve.wait_ge(gs_ready, t + 1)
                    dve.tensor_tensor(hb[:, k % 2], gs[:, k % 2], pU[k % 2][:, FI:2 * FI], ALU.mult).then_inc(h_ready, 1)

                for k in range(RING):
                    hide(k, k)
                    if k >= 2:
                        emit(k - 2, k - 2, LAYOUT + 3 * (k - 1))
                    pick(k, k, 0, LAYOUT + 3 * k)
                    dve.wait_ge(own_sem, LAYOUT + 3 * (k + 1))
                    place_row(k)
                with dve.Fori(1, TILES // RING) as turn:
                    for k in range(RING):
                        t = RING * turn + k
                        hide(t, k)
                        emit(t - 2, (k - 2) % RING, LAYOUT + 3 * (t - 1), 2 * turn - 1 + k // 2)
                        pick(t, k, turn, LAYOUT + 3 * t)
                        dve.wait_ge(own_sem, LAYOUT + 3 * (t + 1))
                        place_row(k)
                for k in (2, 3):
                    t = TILES - RING + k
                    emit(t, k, LAYOUT + 3 * (t + 1), TILES // 2 - 1)


def combine(nc, kept, out):
    TB = 4
    NB = NC // TB
    with ExitStack() as ctx:
        def sb(name, shape, dt=F32):
            return ctx.enter_context(nc.sbuf_tensor(name, shape, dt))

        def sem(name):
            return ctx.enter_context(nc.semaphore(name))

        IN = 3
        ys = sb("ys", [P, IN, TB, TOPK, DM])
        xb = sb("xb", [P, IN, TB, DM])
        sm = sb("sm", [P, 2, TB, DM])
        bst = sb("bst_c", [P, 2, TB, 6])
        mv = sb("mv_c", [P, 2, TB, 2])
        vare = sb("vare_c", [P, 2, TB])
        rstd = sb("rstd_c", [P, 2, TB])
        shift = sb("shift", [P, 2, TB])
        res = sb("res_c", [P, 2, TB, DM])

        ys_in = [sem(f"ys_in{j}") for j in range(IN)]
        xb_in = [sem(f"xb_in{j}") for j in range(IN)]
        pairs_ready = sem("pairs_ready")
        four_ready = sem("four_ready")
        sum_ready = sem("sum_ready")
        stats_ready = sem("stats_ready")
        var_ready = sem("var_ready_c")
        std_ready = sem("std_ready_c")
        shift_ready = sem("shift_ready")
        res_ready = sem("res_ready_c")
        written = [sem("written0"), sem("written1")]

        def block_rows(t, i, each):
            n = TB * P * each
            return t[i * n:(i + 1) * n, :].rearrange("(p j) d -> p j d", p=P)

        with nc.Block() as block:
            @block.sync
            def _(sp):
                for i in range(NB):
                    if i >= IN:
                        sp.wait_ge(sum_ready, i - IN + 1)
                    sp.dma_start(ys[:, i % IN].rearrange("p t k d -> p (t k) d"),
                                 block_rows(kept.y_rows, i, TOPK)).then_inc(ys_in[i % IN], 16)
                    sp.dma_start(xb[:, i % IN], block_rows(kept.base, i, 1)).then_inc(xb_in[i % IN], 16)
                for j in range(2):
                    sp.wait_ge(written[j], NB // 2 * 16)

            @block.vector
            def _(dve):
                def add_four(i):
                    y = ys[:, i % IN]
                    dve.wait_ge(ys_in[i % IN], (i // IN + 1) * 16)
                    dve.tensor_tensor(y[:, :, 0:2], y[:, :, 0:2], y[:, :, 2:4], ALU.add).then_inc(pairs_ready, 1)
                    dve.wait_ge(pairs_ready, i + 1)
                    dve.tensor_tensor(y[:, :, 0], y[:, :, 0], y[:, :, 1], ALU.add).then_inc(four_ready, 1)

                def stats(i):
                    dve.wait_ge(sum_ready, i + 1)
                    for j in range(TB):
                        s = dve.bn_stats(bst[:, i % 2, j], sm[:, i % 2, j])
                    s.then_inc(stats_ready, 1)
                    dve.wait_ge(stats_ready, 2 * i + 1)
                    for j in range(TB):
                        s = dve.bn_aggr(mv[:, i % 2, j], bst[:, i % 2, j])
                    s.then_inc(stats_ready, 1)
                    dve.wait_ge(stats_ready, 2 * i + 2)
                    dve.tensor_scalar(vare[:, i % 2], mv[:, i % 2, :, 1], EPS, None, ALU.add).then_inc(var_ready, 1)

                def finish(i):
                    dve.wait_ge(std_ready, i + 1)
                    if i >= 2:
                        dve.wait_ge(res_ready, i - 1)
                    dve.scalar_tensor_tensor(shift[:, i % 2], mv[:, i % 2, :, 0], -1.0, rstd[:, i % 2], ALU.mult,
                                             ALU.mult).then_inc(shift_ready, 1)

                for i in range(NB):
                    add_four(i)
                    if i:
                        stats(i - 1)
                        finish(i - 1)
                stats(NB - 1)
                finish(NB - 1)

            @block.gpsimd
            def _(pool):
                for i in range(NB):
                    pool.wait_ge(four_ready, i + 1)
                    pool.wait_ge(xb_in[i % IN], (i // IN + 1) * 16)
                    if i >= 2:
                        pool.wait_ge(res_ready, i - 1)
                    pool.tensor_tensor(sm[:, i % 2], ys[:, i % IN, :, 0], xb[:, i % IN], ALU.add).then_inc(sum_ready, 1)
                    pool.wait_ge(var_ready, i + 1)
                    pool.tensor_tensor(rstd[:, i % 2], vare[:, i % 2], kept.half[:].to_broadcast([P, TB]),
                                       ALU.pow).then_inc(std_ready, 1)

            @block.scalar
            def _(act):
                for i in range(NB):
                    act.wait_ge(shift_ready, i + 1)
                    if i >= 2:
                        act.wait_ge(written[i % 2], i // 2 * 16)
                    for j in range(TB):
                        r = act.activation(res[:, i % 2, j], sm[:, i % 2, j], ACT.Identity, bias=shift[:, i % 2, j:j + 1],
                                           scale=rstd[:, i % 2, j:j + 1])
                    r.then_inc(res_ready, 1)
                    act.wait_ge(res_ready, i + 1)
                    act.dma_start(block_rows(out, i, 1), res[:, i % 2]).then_inc(written[i % 2], 16)


def kernel(**inputs):
    import numpy as np
    from concourse import bacc
    from concourse.bass_utils import run_bass_kernel_spmd

    a = {k: np.asarray(v) for k, v in inputs.items()}

    def halves(w, p):
        return w.T.reshape(w.shape[1] // p, p, w.shape[0]).transpose(1, 0, 2)

    tokens = BATCH * SEQ
    u = a["L0_attn_u"].reshape(tokens, DM)
    f = NSL * FI
    sgu = a["L0_ffn_shared_gate_up_w"]
    ups = [*a["L0_ffn_w13"]] + [np.concatenate([sgu[s * FI:(s + 1) * FI], sgu[f + s * FI:f + (s + 1) * FI]]) for s in range(NSL)]
    downs = [*a["L0_ffn_w2"]] + [a["L0_ffn_shared_down_w"][:, s * FI:(s + 1) * FI] for s in range(NSL)]
    laid = {
        "uT": halves(u, P),
        "u": u,
        "w_in": halves(a["L0_attn_W_in"], P),
        "conv_w": a["L0_attn_conv_w"].reshape(NG, P, TAPS).transpose(1, 0, 2),
        "conv_b": a["L0_attn_conv_b"].reshape(NG, P).T,
        "dt_bias": np.broadcast_to(a["L0_attn_dt_bias"], (P, NH)),
        "a_log": np.broadcast_to(a["L0_attn_A_log"], (P, NH)),
        "d_skip": np.broadcast_to(a["L0_attn_D"], (P, NH)),
        "norm_w": a["L0_attn_norm_w"].reshape(KI, P).T,
        "w_out": halves(a["L0_attn_W_out"], P),
        "gate": halves(np.concatenate([a["L0_ffn_gate_w"], a["L0_ffn_sgate_w"]]), P),
        "up": np.stack([halves(w, P) for w in ups], axis=1),
        "down": np.stack([halves(w, HF) for w in downs], axis=1),
    }
    nc = bacc.Bacc("TRN2", target_bir_lowering=False, num_devices=1)
    arrays = {f"in_{k}": np.ascontiguousarray(v) for k, v in laid.items()}
    args = [nc.dram_tensor(k, v.shape, F32, kind="ExternalInput").ap() for k, v in arrays.items()]
    out = nc.dram_tensor("out_dram", (tokens, DM), F32, kind="ExternalOutput").ap()
    build(nc, *args, out)
    r = run_bass_kernel_spmd(nc, [arrays], core_ids=[0])
    return r.results[0]["out_dram"].reshape(BATCH, SEQ, DM)
```

```python
from contextlib import ExitStack

import concourse.bass as bass
from concourse import mybir

F32 = mybir.dt.float32
F32R = mybir.dt.float32r
I32 = mybir.dt.int32
U32 = mybir.dt.uint32
ALU = mybir.AluOpType
ACT = mybir.ActivationFunctionType
AX = mybir.AxisListType

P = 128
DM = 256
KD = DM // P
DI = 512
KI = DI // P
NS = 128
NH = 8
HD = DI // NH
CONV = DI + 2 * NS
NG = CONV // P
GB, GC = KI, KI + 1
TAPS = 4
HALO = TAPS - 1
WIDE = 2 * DI + 2 * NS
PROJ = WIDE + NH
BATCH, SEQ = 4, 1024
CH = SEQ // P
NC = BATCH * CH
BLK = 512
QB = BLK // P
NE = 16
GATES = NE + 2
TOPK = 4
FI = 176
HF = FI // 2
NSL = 704 // FI
REGION = NC * P + P
TILES = NC * TOPK + NE
RING = 8
TURN = 2 * RING
YROW = DM + 2 * TOPK
ODD = YROW + 1
XW = ODD + 1
EPS = 1e-5
RANK = DM
TOT = RANK + NE


START = 1


def met(count):
    return START + count


def primed(count):
    return 16 + count


def prime(pool, kept, sems):
    for j, s in enumerate(sems):
        pool.dma_start(kept.spare[j:j + 1, :], kept.padrow[0:1, 0:1]).then_inc(s, 16)


def start(nc, sems):
    with nc.Block() as block:
        @block.sync
        def _(sp):
            for s in sems:
                sp.sem_inc(s, START)


class Steps:

    def __init__(self, eng, sem, base=0):
        self.eng, self.sem, self.base, self.n = eng, sem, base, 0

    def done(self, ins, apart=False):
        self.n += 1
        ins.then_inc(self.sem, 1)
        self.eng.wait_ge(self.sem, self.base + self.n)
        if apart:
            waits_end(self.eng)


def waits_end(eng):
    eng.nop(nofuse=True)


class Kept:

    def __init__(self, x_rows, y_rows, base, spare, ident, ones, half, padrow, iota_e, reg0, place, banks):
        self.x_rows, self.y_rows, self.base, self.spare = x_rows, y_rows, base, spare
        self.ident, self.ones, self.half, self.padrow, self.iota_e = ident, ones, half, padrow, iota_e
        self.reg0, self.place, self.banks = reg0, place, banks


def bc(ap, where, shape):
    return ap.unsqueeze(where).to_broadcast(shape)


def build(nc, uT, u, w_in, conv_w, conv_b, dt_bias, a_log, d_skip, norm_w, w_out, gate, up, down, out):
    with ExitStack() as whole:
        def keep(name, shape, dt=F32):
            return whole.enter_context(nc.sbuf_tensor(name, shape, dt))

        kept = Kept(
            x_rows=nc.dram_tensor("x_rows", (NE * REGION + P, XW), F32, kind="Internal").ap(),
            y_rows=nc.dram_tensor("y_rows", (NC * P * TOPK + 2 * P, DM), F32, kind="Internal").ap(),
            base=nc.dram_tensor("base", (NC * P, DM), F32, kind="Internal").ap(),
            spare=nc.dram_tensor("spare", (2, 1), F32, kind="Internal").ap(),
            ident=keep("ident", [P, P]),
            ones=keep("ones", [P, P]),
            half=keep("half", [P, 1]),
            padrow=keep("padrow", [P, XW]),
            iota_e=keep("iota_e", [P, NE]),
            reg0=keep("reg0", [P, NE]),
            place=keep("place", [P, NE]),
            banks=[whole.enter_context(nc.psum_tensor(f"bank{i}", [P, 512], F32)) for i in range(8)],
        )
        mamba(nc, kept, uT, u, w_in, conv_w, conv_b, dt_bias, a_log, d_skip, norm_w, w_out, gate, up, down)
        experts(nc, kept, up, down)
        combine(nc, kept, out)


def mamba(nc, kept, uT, u, w_in, conv_w, conv_b, dt_bias, a_log, d_skip, norm_w, w_out, gate, up, down):
    ident, ones, half, place = kept.ident, kept.ones, kept.half, kept.place
    PA, PX, PG, PD, PY, PO = kept.banks[0:2], kept.banks[2], kept.banks[3], kept.banks[4:6], kept.banks[6], kept.banks[7]

    with ExitStack() as ctx:
        def sb(name, shape, dt=F32):
            return ctx.enter_context(nc.sbuf_tensor(name, shape, dt))

        looped = []

        def sem(name):
            looped.append(once(name))
            return looped[-1]

        def once(name):
            return ctx.enter_context(nc.semaphore(name))

        win = sb("win", [P, 2, KD, WIDE], F32R)
        wdt = sb("wdt", [P, KD, NH])
        wout = sb("wout", [P, KI, DM])
        gw = sb("gw", [P, 2, KD, GATES], F32R)
        graw = sb("graw", [P, KD, GATES])
        sup = sb("sup", [P, 2, NSL, KD, 2 * FI], F32R)
        sdn = sb("sdn", [HF, NSL, 2, DM])
        cw = sb("cw", [P, NG, TAPS])
        cb = sb("cb", [P, NG])
        dtb = sb("dtb", [P, NH])
        ah = sb("ah", [P, NH])
        dsk = sb("dsk", [P, NH])
        nw = sb("nw", [P, KI])
        incl = sb("incl", [P, P])
        later = sb("later", [P, P])
        laterr = sb("laterr", [P, P], F32R)
        before = sb("before", [P, P])
        uTb = sb("uTb", [P, 2, KD, BLK])
        us = sb("us", [P, 2, 2, KD, BLK], F32R)
        ut = sb("ut", [P, 2, DM])
        raw = sb("raw", [P, 2, NG, HALO + BLK])
        xc = sb("xc", [P, 2, NG, BLK])
        dtw = sb("dtw", [P, 8, CH * NH])
        dts = sb("dts", [P, CH * NH])
        dA = sb("dA", [P, CH * NH])
        dAs = sb("dAs", [P, 2, CH * NH], F32R)
        dec = sb("dec", [P, 3, CH * NH])
        din = sb("din", [P, CH * NH])
        xtok = sb("xtok", [P, 2, DI])
        btok = sb("btok", [P, 2, NS])
        dAw = sb("dAw", [P, 2, NH, P], F32R)
        gm = sb("gm", [P, P])
        E = sb("E", [P, NH, P])
        M = sb("M", [P, NH, P])
        xs = sb("xs", [P, DI])
        xD = sb("xD", [P, DI])
        zs = sb("zs", [P, DI])
        y1 = sb("y1", [P, DI])
        y2 = sb("y2", [P, DI])
        yg = sb("yg", [P, DI])
        ysq = sb("ysq", [P, DI])
        ygT = sb("ygT", [P, DI])
        state = sb("state", [P, DI])
        ss = sb("ss", [P, 1])
        warm = sb("warm", [P, 1])
        msq = sb("msq", [P, 1])
        rms = sb("rms", [P, 1])
        res = sb("res", [P, DM])
        bst = sb("bst", [P, 6])
        mv = sb("mv", [P, 2])
        vare = sb("vare", [P, 1])
        rstd = sb("rstd", [P, 1])
        x1 = sb("x1", [P, 2, XW])
        acc = sb("acc", [P, 2, DM])
        x1T = sb("x1T", [P, 2, 2, KD, P], F32R)
        tok_p = sb("tok_p", [P, 1])
        lg = sb("lg", [P, NE + 1])
        top = sb("top", [P, 8])
        topi = sb("topi", [P, 8], U32)
        chf = sb("chf", [P, TOPK])
        negm = sb("negm", [P, 1])
        ex = sb("ex", [P, NE])
        ez = sb("ez", [P, 1])
        e4 = sb("e4", [P, TOPK])
        eg = sb("eg", [P, 1])
        rz = sb("rz", [P, 1])
        sg = sb("sg", [P, 2])
        oh = sb("oh", [P, TOPK, NE])
        mask = sb("mask", [P, NE])
        rs = sb("rs", [P, NE])
        osl = sb("osl", [P, TOPK, NE])
        slf = sb("slf", [P, TOPK])
        sloti = sb("sloti", [P, 2, TOPK], I32)
        gs = sb("gs", [P, 2, FI])
        hb = sb("hb", [P, 2, FI])
        hT = sb("hT", [HF, 2, 2, P])

        loaded = once("loaded")
        consts = once("consts")
        setup = once("setup")
        whi_ready = once("whi_ready")
        wlo_ready = once("wlo_ready")
        uT_in = [sem("uT_in0"), sem("uT_in1")]
        u_in = [sem("u_in0"), sem("u_in1")]
        scattered = [once("scattered0"), once("scattered1")]
        acc_out = [sem("acc_out0"), sem("acc_out1")]
        padded = once("padded_end")
        pa_made = sem("pa_made")
        raw_in = sem("raw_in")
        conv_made = sem("conv_made")
        xc_ready = sem("xc_ready")
        dt_proj = sem("dt_proj")
        dt_abs = sem("dt_abs")
        dt_exp = sem("dt_exp")
        dA_ready = sem("dA_ready")
        sums_made = sem("sums_made")
        dec_ready = sem("dec_ready")
        din_ready = sem("din_ready")
        xT_made = sem("xT_made")
        xtok_ready = sem("xtok_ready")
        btok_ready = sem("btok_ready")
        g_made = sem("g_made")
        gm_ready = sem("gm_ready")
        dAw_ready = sem("dAw_ready")
        diff_made = sem("diff_made")
        E_ready = sem("E_ready")
        M_ready = sem("M_ready")
        xs_ready = sem("xs_ready")
        zs_ready = sem("zs_ready")
        z_made = sem("z_made")
        inter_made = sem("inter_made")
        y1_ready = sem("y1_ready")
        y_made = sem("y_made")
        st_made = sem("st_made")
        state_ready = sem("state_ready")
        y2_ready = sem("y2_ready")
        yg_ready = sem("yg_ready")
        ss_ready = sem("ss_ready")
        rms_ready = sem("rms_ready")
        ygT_made = sem("ygT_made")
        ygT_ready = sem("ygT_ready")
        o_made = sem("o_made")
        res_ready = sem("res_ready")
        var_ready = sem("var_ready")
        std_ready = sem("std_ready")
        x1_ready = sem("x1_ready")
        x1T_made = sem("x1T_made")
        x1hi_ready = sem("x1hi_ready")
        x1lo_ready = sem("x1lo_ready")
        uhi_ready = sem("uhi_ready")
        ulo_ready = sem("ulo_ready")
        lg_made = sem("lg_made")
        lg_ready = sem("lg_ready")
        rex_ready = sem("rex_ready")
        mask_ready = sem("mask_ready")
        rank_made = sem("rank_made")
        rank_read = sem("rank_read")
        slot_ready = sem("slot_ready")
        gs_ready = sem("gs_ready")
        h_ready = sem("h_ready")
        hT_made = sem("hT_made")
        hT_ready = sem("hT_ready")
        dn_made = sem("dn_made")
        acc_ready = sem("acc_ready")
        dve_own = once("dve_own")
        pool_own = once("pool_own")

        stage = raw[:].rearrange("p a g n -> p (a g n)")
        win_raw = stage[:, 0:KD * PROJ]
        sup_raw = stage[:, KD * PROJ:KD * PROJ + NSL * KD * 2 * FI]
        parted = ((win, win_raw.rearrange("p (k n) -> p k n", k=KD)[:, :, 0:WIDE]),
                  (sup, sup_raw.rearrange("p (s k n) -> p s k n", s=NSL, k=KD)), (gw, graw[:]))

        LOADS = 14
        CONSTS = 11
        DVE_BASE = 2 + 17 + NG * (TAPS - 1)
        DVE_TURN = 17 + 2 * NG * (TAPS - 1) + CH * (11 + 3) + CH + CH - 1
        POOL_BASE = 5
        POOL_TURN = CH + CH - 1

        def at(c, w=P):
            return slice(c * w, c * w + w)

        def heads(ap):
            return ap.rearrange("p (h d) -> p h d", h=NH)

        def over(ap):
            return bc(ap, 2, [P, NH, HD])

        def uses(more):
            plan = []
            for c in range(CH + 1):
                if more and c == CH:
                    plan += [("raw", 0, NG - 2), ("raw", 0, NG - 1)]
                if c:
                    plan += [("up", c - 1, s) for s in range(NSL)]
                if c < QB - 1:
                    plan += [("raw", 1, 2 * c), ("raw", 1, 2 * c + 1)]
                if more and QB <= c < CH:
                    plan.append(("raw", 0, c - QB))
            return plan

        plans = {more: uses(more) for more in (True, False)}
        PA_TURN = len(plans[True])
        assert PA_TURN % 2 == 0 and NG % 2 == 0 and CH - QB == NG - 2
        kinds = {"raw": (raw_in, NG, 2 * NG), "up": (h_ready, 0, CH * NSL)}

        def bank_of(key, more):
            return PA[plans[more].index(key) % 2]

        def wait_pa(pe, b, key, more):
            plan = plans[more]
            n = plan.index(key) - 2
            if n >= 0:
                signal, first, per = kinds[plan[n][0]]
                pe.wait_ge(signal, met(first + b * per + sum(k[0] == plan[n][0] for k in plan[:n + 1])))
            else:
                for signal, first, per in kinds.values():
                    pe.wait_ge(signal, met(first + b * per))

        def turns(eng, turn):
            with eng.Fori(0, BATCH - 1) as b:
                turn(b, True)
            turn(BATCH - 1, False)

        start(nc, looped)
        with nc.Block() as block:
            @block.sync
            def _(sp):
                sp.dma_start(win_raw, w_in.rearrange("p k n -> p (k n)")).then_inc(loaded, 16)
                for t, src in ((cw, conv_w), (cb, conv_b), (dtb, dt_bias), (ah, a_log),
                               (dsk, d_skip), (nw, norm_w), (wout, w_out), (graw, gate), (sdn, down[:, NE:])):
                    sp.dma_start(t[:], src).then_inc(loaded, 16)
                for s in range(NSL):
                    n = KD * 2 * FI
                    sp.dma_start(sup_raw[:, s * n:(s + 1) * n], up[:, NE + s].rearrange("p k n -> p (k n)")).then_inc(loaded, 16)
                for k in range(2):
                    sp.dma_start(uTb[:, k], uT[:, :, k * BLK:(k + 1) * BLK]).then_inc(uT_in[k], 16)

                def turn(b, more):
                    for c in range(CH + 1):
                        if c < CH:
                            sp.wait_ge(res_ready, met(b * CH + max(c - 1, 0)))
                            sp.dma_start(ut[:, c % 2], u[bass.ds(b * SEQ + c * P, P), :]).then_inc(u_in[c % 2], 16)
                        if more and c in (QB - 1, CH - 1):
                            k = c // QB
                            sp.wait_ge(z_made, met(b * CH + c + 1))
                            sp.dma_start(uTb[:, k], uT[:, :, bass.ds((b + 1) * SEQ + k * BLK, BLK)]).then_inc(uT_in[k], 16)
                        if c:
                            sp.wait_ge(acc_ready, met(b * CH + c))
                            sp.dma_start(kept.base[bass.ds(b * SEQ + (c - 1) * P, P), :],
                                         acc[:, (c - 1) % 2]).then_inc(acc_out[(c - 1) % 2], 16)

                turns(sp, turn)
                sp.dma_start(kept.x_rows[NE * REGION:NE * REGION + P, :], kept.padrow[:]).then_inc(padded, 16)
                for j in range(2):
                    sp.wait_ge(acc_out[j], met(NC // 2 * 16))
                sp.wait_ge(padded, 16)

            @block.gpsimd
            def _(pool):
                pool.memset(ident[:], 0.0).then_inc(pool_own, 1)
                pool.memset(incl[:], 1.0).then_inc(pool_own, 1)
                pool.memset(later[:], 1.0).then_inc(pool_own, 1)
                pool.memset(before[:], 1.0).then_inc(pool_own, 1)
                pool.memset(ones[:], 1.0).then_inc(consts, 1)
                pool.memset(half[:], -0.5).then_inc(consts, 1)
                pool.memset(kept.padrow[:], 0.0).then_inc(pool_own, 1)
                pool.iota(kept.iota_e[:], [[1, NE]], base=0, channel_multiplier=0,
                          allow_small_or_imprecise_dtypes=True).then_inc(consts, 1)
                pool.iota(tok_p[:], [[0, 1]], base=0, channel_multiplier=1,
                          allow_small_or_imprecise_dtypes=True).then_inc(consts, 1)
                pool.wait_ge(pool_own, POOL_BASE)
                pool.memset(kept.padrow[:, ODD:XW], float(P)).then_inc(consts, 1)
                pool.memset(kept.padrow[:, DM + TOPK:DM + 2 * TOPK], -1.0).then_inc(consts, 1)
                pool.iota(kept.padrow[:, YROW:ODD], [[0, 1]], base=NC * P * TOPK, channel_multiplier=1,
                          allow_small_or_imprecise_dtypes=True).then_inc(consts, 1)
                pool.affine_select(out=ident[:], in_=ident[:], compare_op=ALU.not_equal, fill=1.0, base=0,
                                   pattern=[[-1, P]], channel_multiplier=1).then_inc(consts, 1)
                pool.affine_select(out=incl[:], in_=incl[:], compare_op=ALU.is_ge, fill=0.0, base=0,
                                   pattern=[[1, P]], channel_multiplier=-1).then_inc(consts, 1)
                pool.affine_select(out=later[:], in_=later[:], compare_op=ALU.is_ge, fill=0.0, base=-1,
                                   pattern=[[-1, P]], channel_multiplier=1).then_inc(consts, 1)
                pool.affine_select(out=before[:], in_=before[:], compare_op=ALU.is_ge, fill=0.0, base=-1,
                                   pattern=[[1, P]], channel_multiplier=-1).then_inc(consts, 1)
                pool.wait_ge(consts, CONSTS)
                pool.wait_ge(loaded, 16 * LOADS)
                prime(pool, kept, scattered)

                def spread(b, c):
                    pool.wait_ge(dA_ready, met(b + 1))
                    pool.wait_ge(diff_made, met((b * CH + c) * 2))
                    for part in range(2):
                        pool.tensor_tensor(dAw[:, part], bc(incl[:], 1, [P, NH, P]),
                                           bc(dAs[:, part, at(c, NH)], 2, [P, NH, P]), ALU.mult).then_inc(dAw_ready, 1)

                def turn(b, more):
                    own = Steps(pool, pool_own, POOL_BASE + b * POOL_TURN)
                    for c in range(CH + 1):
                        if c < CH:
                            pool.wait_ge(xtok_ready, met(b * CH + c + 1))
                            pool.wait_ge(din_ready, met(b + 1))
                            pool.wait_ge(st_made, met(b * CH + c))
                            pool.tensor_tensor(heads(xs[:]), heads(xtok[:, c % 2]), over(din[:, at(c, NH)]),
                                               ALU.mult).then_inc(xs_ready, 1)
                            if c:
                                own.done(pool.tensor_tensor(heads(xD[:]), heads(xtok[:, c % 2]), over(dsk[:]), ALU.mult))
                            else:
                                pool.wait_ge(yg_ready, met(b * CH))
                                pool.tensor_tensor(heads(y2[:]), heads(xtok[:, c % 2]), over(dsk[:]),
                                                   ALU.mult).then_inc(y2_ready, 1)
                        if c < CH - 1:
                            spread(b, c + 1)
                        if 0 < c < CH:
                            pool.wait_ge(y1_ready, met(b * (CH - 1) + c))
                            pool.wait_ge(yg_ready, met(b * CH + c))
                            pool.tensor_tensor(y2[:], y1[:], xD[:], ALU.add).then_inc(y2_ready, 1)
                        if c:
                            pool.wait_ge(slot_ready, met(b * CH + c))
                            waits_end(pool)
                            for j in range(TOPK):
                                pool.indirect_dma_start(
                                    kept.x_rows,
                                    bass.IndirectOffsetOnAxis(ap=sloti[:, (c - 1) % 2, j:j + 1].bitcast(U32), axis=0),
                                    x1[:, (c - 1) % 2], None).then_inc(scattered[(c - 1) % 2], 16)
                        if c < CH:
                            pool.wait_ge(ss_ready, met(b * CH + c + 1))
                            waits_end(pool)
                            own.done(pool.tensor_scalar(msq[:], ss[:], 1.0 / DI, EPS, ALU.mult, ALU.add))
                            pool.tensor_tensor(rms[:], msq[:], half[:], ALU.pow).then_inc(rms_ready, 1)
                            pool.wait_ge(var_ready, met(b * CH + c + 1))
                            pool.tensor_tensor(rstd[:], vare[:], half[:], ALU.pow).then_inc(std_ready, 1)
                    if more:
                        spread(b + 1, 0)

                spread(0, 0)
                turns(pool, turn)

            @block.tensor
            def _(pe):
                pe.wait_ge(consts, CONSTS)
                pe.wait_ge(loaded, 16 * LOADS)
                pe.wait_ge(setup, 5)
                pe.wait_ge(wlo_ready, len(parted) + 1)

                def product(out, left, right):
                    for d in range(KD):
                        for a in range(2):
                            pe.matmul(out, left(0, d), right(a, d), start=d == 0 and a == 0, stop=False)
                    for d in range(KD):
                        mm = pe.matmul(out, left(1, d), right(0, d), start=False, stop=d == KD - 1)
                    return mm


                def project(bank, k, g):
                    product(bank[:], lambda a, d: win[:, a, d, at(NG - 2 + g)],
                            lambda a, d: us[:, k, a, d, :]).then_inc(pa_made, 1)

                def project_dt(b):
                    pe.wait_ge(uT_in[0], met(b * 16 + 16))
                    pe.wait_ge(uT_in[1], met(b * 16 + 16))
                    pe.wait_ge(ygT_ready, met(b * CH))
                    for c in range(CH):
                        for d in range(KD):
                            mm = pe.matmul(PX[:, at(c, NH)], uTb[:, c // QB, d, at(c % QB)], wdt[:, d],
                                           start=d == 0, stop=d == KD - 1)
                    mm.then_inc(dt_proj, 1)

                def sum_decays(b):
                    pe.wait_ge(dA_ready, met(b + 1))
                    for j, m in enumerate((incl, later, ones)):
                        mm = pe.matmul(PX[:, at(1 + j, CH * NH)], m[:], dA[:], start=True, stop=True)
                    mm.then_inc(sums_made, 1)

                def turn(b, more):
                    def project_turn(k, g):
                        key = ("raw", k, g)
                        wait_pa(pe, b, key, more)
                        pe.wait_ge(ulo_ready, met(b * 2 + (2 if k else 3)))
                        project(bank_of(key, more), k, g)

                    def slice_up(c, s):
                        wait_pa(pe, b, ("up", c, s), more)
                        product(bank_of(("up", c, s), more)[:, 0:2 * FI], lambda a, d: x1T[:, c % 2, a, d],
                                lambda a, d: sup[:, a, s, d]).then_inc(pa_made, 1)

                    def turn_x1(c):
                        pe.wait_ge(x1_ready, met(b * CH + c + 1))
                        for d in range(KD):
                            mm = pe.transpose(PY[:, DM + d * P:DM + (d + 1) * P], x1[:, c % 2, at(d)], ident[:])
                        mm.then_inc(x1T_made, 1)

                    def slice_turn(c, s):
                        n = (b * CH + c) * NSL + s
                        pe.wait_ge(h_ready, met(n + 1))
                        pe.wait_ge(hT_ready, met(n))
                        for j in range(2):
                            mm = pe.transpose(PG[0:HF, DM + j * P:DM + (j + 1) * P], hb[:, s % 2, at(j, HF)], ident[:])
                        mm.then_inc(hT_made, 1)

                    def slice_down(c, s):
                        pe.wait_ge(hT_ready, met((b * CH + c) * NSL + s + 1))
                        if s == 0:
                            pe.wait_ge(rank_read, met(b * CH + c + 1))
                        for j in range(2):
                            mm = pe.matmul(PO[:, 0:DM], hT[:, s % 2, j], sdn[:, s, j],
                                           start=s == 0 and j == 0, stop=s == NSL - 1 and j == 1)
                        if s == NSL - 1:
                            mm.then_inc(dn_made, 1)

                    def rank(c):
                        pe.wait_ge(mask_ready, met(b * CH + c + 1))
                        pe.wait_ge(acc_ready, met(b * CH + c))
                        pe.matmul(PO[:, RANK:RANK + NE], before[:], mask[:], start=True, stop=True)
                        pe.matmul(PO[:, TOT:TOT + NE], ones[:], mask[:], start=True, stop=True).then_inc(rank_made, 1)

                    for c in range(CH + 1):
                        n = b * CH + c
                        k, q = c // QB, c % QB
                        if c < CH:
                            pe.wait_ge(xc_ready, met((b * 2 + k + 1) * NG))
                            pe.wait_ge(ygT_ready, met(n))
                            pe.wait_ge(dec_ready, met(b + 1))
                            for j in range(KI):
                                mm = pe.transpose(PX[:, at(j)], xc[:, k, j, at(q)], ident[:])
                            mm.then_inc(xT_made, 1)
                            pe.wait_ge(hT_ready, met((b * CH + max(c - 1, 0)) * NSL))
                            pe.wait_ge(gm_ready, met(n))
                            pe.transpose(PG[:, P:2 * P], xc[:, k, GB, at(q)], ident[:])
                            pe.matmul(PG[:, 0:P], xc[:, k, GB, at(q)], xc[:, k, GC, at(q)],
                                      start=True, stop=True).then_inc(g_made, 1)
                            if c:
                                turn_x1(c - 1)
                            pe.wait_ge(dAw_ready, met(2 * n + 2))
                            if c:
                                pe.wait_ge(y1_ready, met(b * (CH - 1) + c - 1))
                            pe.wait_ge(state_ready, met(n))
                            for j in range(2):
                                for part in range(2):
                                    mm = pe.matmul(PD[j][:], laterr[:], dAw[:, part, 4 * j:4 * j + 4],
                                                   start=part == 0, stop=part == 1)
                                mm.then_inc(diff_made, 1)
                        if more and c == CH:
                            project_dt(b + 1)
                            project_turn(0, NG - 2)
                            project_turn(0, NG - 1)
                        if c == CH:
                            turn_x1(c - 1)
                        if more and c == CH:
                            sum_decays(b + 1)
                        if c < CH:
                            pe.wait_ge(xtok_ready, met(n + 1))
                            pe.wait_ge(ulo_ready, met(b * 2 + k + 1))
                            product(PX[:], lambda a, d: us[:, k, a, d, at(q)],
                                    lambda a, d: win[:, a, d, 0:DI]).then_inc(z_made, 1)
                        if c:
                            pe.wait_ge(x1lo_ready, met(n))
                            product(PY[:, 0:GATES], lambda a, d: x1T[:, (c - 1) % 2, a, d],
                                    lambda a, d: gw[:, a, d]).then_inc(lg_made, 1)
                            slice_up(c - 1, 0)
                            slice_up(c - 1, 1)
                        if c == CH:
                            rank(c - 1)
                        if c < CH:
                            if c:
                                pe.wait_ge(E_ready, met(2 * n + 1))
                                pe.matmul(PD[0][:], xc[:, k, GC, at(q)], state[:], start=True, stop=True).then_inc(inter_made, 1)
                            if c:
                                rank(c - 1)
                            for h in range(NH):
                                if h % 4 == 0:
                                    pe.wait_ge(M_ready, met(2 * n + 1 + h // 4))
                                mm = pe.matmul(PY[:, at(h, HD)], M[:, h], xtok[:, c % 2, at(h, HD)],
                                               start=True, stop=True)
                            mm.then_inc(y_made, 1)
                            pe.wait_ge(xs_ready, met(n + 1))
                            pe.wait_ge(btok_ready, met(n + 1))
                            pe.matmul(PD[1][:], btok[:, c % 2], xs[:], start=True, stop=True).then_inc(st_made, 1)
                        if c:
                            if c < CH:
                                pe.wait_ge(gm_ready, met(n + 1))
                            slice_turn(c - 1, 0)
                            slice_up(c - 1, 2)
                            slice_down(c - 1, 0)
                            slice_turn(c - 1, 1)
                            slice_up(c - 1, 3)
                        if c < CH:
                            pe.wait_ge(yg_ready, met(n + 1))
                            for j in range(KI):
                                mm = pe.transpose(PX[:, at(j)], yg[:, at(j)], ident[:])
                            mm.then_inc(ygT_made, 1)
                        if c:
                            slice_down(c - 1, 1)
                            slice_turn(c - 1, 2)
                        if c < CH:
                            pe.wait_ge(ygT_ready, met(n + 1))
                            for j in range(KI):
                                mm = pe.matmul(PY[:, 0:DM], ygT[:, at(j)], wout[:, j], start=j == 0, stop=j == KI - 1)
                            mm.then_inc(o_made, 1)
                        if c:
                            slice_turn(c - 1, 3)
                            slice_down(c - 1, 2)
                        if c < QB - 1:
                            project_turn(1, 2 * c)
                            project_turn(1, 2 * c + 1)
                        if more and QB <= c < CH:
                            project_turn(0, c - QB)
                        if c:
                            slice_down(c - 1, 3)

                pe.wait_ge(ulo_ready, met(1))
                for g in range(NG):
                    if g == 3:
                        project_dt(0)
                    if g >= 2:
                        pe.wait_ge(raw_in, met(g - 1))
                    project(PA[g % 2], 0, g)
                sum_decays(0)
                turns(pe, turn)

            @block.scalar
            def _(act):
                act.wait_ge(loaded, 16 * LOADS)
                act.wait_ge(consts, CONSTS)
                for part, whole in parted:
                    act.copy(part[:, 0], whole).then_inc(whi_ready, 1)
                act.activation(E[:, 0, 0:NH], ah[:], ACT.Exp).then_inc(setup, 1)

                def u_hi(b, k):
                    act.wait_ge(uT_in[k], met(b * 16 + 16))
                    act.copy(us[:, k, 0], uTb[:, k]).then_inc(uhi_ready, 1)

                u_hi(0, 0)
                u_hi(0, 1)
                act.wait_ge(dve_own, 2)


                def raw_copy(bank, b, k, g, made):
                    act.wait_ge(pa_made, met(made))
                    act.wait_ge(conv_made, met(b * 2 * NG + k * NG))
                    if k == 0:
                        act.copy(raw[:, 1, g, 0:HALO], bank[:, BLK - HALO:BLK])
                    act.copy(raw[:, k, g, HALO:HALO + BLK], bank[:]).then_inc(raw_in, 1)

                def conv_silu(b, k, g):
                    act.wait_ge(conv_made, met((b * 2 + k) * NG + g + 1))
                    act.activation(xc[:, k, g], xc[:, k, g], ACT.Silu).then_inc(xc_ready, 1)

                def dt_exponent(b):
                    act.wait_ge(dt_abs, met(b + 1))
                    act.activation(dtw[:, 2], dtw[:, 1], ACT.Exp).then_inc(dt_exp, 1)

                def decays(b):
                    act.wait_ge(sums_made, met(b + 1))
                    act.activation(dec[:].rearrange("p a n -> p (a n)"), PX[:, CH * NH:4 * CH * NH], ACT.Exp).then_inc(dec_ready, 1)

                def turn(b, more):
                    def made(key):
                        return NG + b * PA_TURN + plans[more].index(key) + 1

                    def raw_turn(k, g):
                        key = ("raw", k, g)
                        raw_copy(bank_of(key, more), b + 1 - k, k, g, made(key))

                    def x1_hi(c):
                        act.wait_ge(x1T_made, met(b * CH + c + 1))
                        act.wait_ge(dn_made, met(b * CH + max(c - 1, 0)))
                        act.copy(x1T[:, c % 2, 0].rearrange("p k t -> p (k t)"), PY[:, DM:2 * DM]).then_inc(x1hi_ready, 1)

                    def slice_silu(c, s):
                        act.wait_ge(pa_made, met(made(("up", c, s))))
                        act.wait_ge(h_ready, met(b * CH * NSL + max(c * NSL + s - 1, 0)))
                        act.activation(gs[:, s % 2], bank_of(("up", c, s), more)[:, 0:FI], ACT.Silu).then_inc(gs_ready, 1)

                    def slice_copy(c, s):
                        n = (b * CH + c) * NSL + s
                        act.wait_ge(hT_made, met(n + 1))
                        if s == 0:
                            act.wait_ge(dn_made, met(b * CH + c))
                        act.copy(hT[:, s % 2].rearrange("p j t -> p (j t)"), PG[0:HF, DM:2 * DM]).then_inc(hT_ready, 1)

                    for c in range(CH + 1):
                        n = b * CH + c
                        if c < CH:
                            act.wait_ge(xT_made, met(n + 1))
                            act.wait_ge(y_made, met(b * CH + max(c - 1, 0)))
                            act.wait_ge(yg_ready, met(b * CH + max(c - 1, 0)))
                            act.copy(xtok[:, c % 2], PX[:]).then_inc(xtok_ready, 1)
                            act.wait_ge(g_made, met(n + 1))
                            act.wait_ge(st_made, met(b * CH + max(c - 1, 0)))
                            act.wait_ge(gm_ready, met(n + 1))
                            act.copy(btok[:, c % 2], PG[:, P:2 * P]).then_inc(btok_ready, 1)
                            if c:
                                x1_hi(c - 1)
                            act.wait_ge(M_ready, met(2 * n))
                            for j in range(2):
                                act.wait_ge(diff_made, met(2 * n + j + 1))
                                act.activation(E[:, 4 * j:4 * j + 4].rearrange("p h t -> p (h t)"), PD[j][:],
                                               ACT.Exp).then_inc(E_ready, 1)
                        if more and c == CH:
                            dt_exponent(b + 1)
                            raw_turn(0, NG - 2)
                            raw_turn(0, NG - 1)
                        if c == CH:
                            x1_hi(c - 1)
                        if c:
                            if more and c == CH:
                                decays(b + 1)
                            act.wait_ge(lg_ready, met(n))
                            act.activation(ex[:], lg[:, 0:NE], ACT.Exp, bias=negm[:], accum_out=ez[:])
                            act.activation(e4[:], top[:, 0:TOPK], ACT.Exp, bias=negm[:])
                            act.activation(eg[:], lg[:, NE:NE + 1], ACT.Exp, scale=-1.0).then_inc(rex_ready, 1)
                        if c < CH:
                            act.wait_ge(z_made, met(n + 1))
                            act.wait_ge(yg_ready, met(n))
                            act.activation(zs[:], PX[:], ACT.Silu).then_inc(zs_ready, 1)
                        if more and c in (QB, CH):
                            act.wait_ge(z_made, met(b * CH + c))
                            u_hi(b + 1, c // QB - 1)
                        if c:
                            slice_silu(c - 1, 0)
                            slice_silu(c - 1, 1)
                            slice_copy(c - 1, 0)
                            slice_silu(c - 1, 2)
                            slice_copy(c - 1, 1)
                            slice_silu(c - 1, 3)
                        if c < CH:
                            act.wait_ge(ygT_made, met(n + 1))
                            act.wait_ge(o_made, met(n))
                            act.copy(ygT[:], PX[:]).then_inc(ygT_ready, 1)
                        if c:
                            slice_copy(c - 1, 2)
                        if c < CH:
                            act.wait_ge(yg_ready, met(n + 1))
                            act.wait_ge(rms_ready, met(n))
                            act.activation(ysq[:], yg[:], ACT.Square, accum_out=ss[:]).then_inc(ss_ready, 1)
                        if c:
                            slice_copy(c - 1, 3)
                        if 0 < c < QB:
                            conv_silu(b, 1, 2 * c - 2)
                            conv_silu(b, 1, 2 * c - 1)
                        if more and c > QB:
                            conv_silu(b + 1, 0, c - QB - 1)
                        if c < CH - 1:
                            act.activation(warm[:], ones[:, 0:1], ACT.Exp)
                        if c < QB - 1:
                            raw_turn(1, 2 * c)
                            raw_turn(1, 2 * c + 1)
                        if more and QB <= c < CH:
                            raw_turn(0, c - QB)
                        if more and c == CH:
                            conv_silu(b + 1, 0, NG - 2)
                            conv_silu(b + 1, 0, NG - 1)

                for g in range(NG):
                    if g == 3:
                        dt_exponent(0)
                    raw_copy(PA[g % 2], 0, 0, g, g + 1)
                for g in range(NG):
                    conv_silu(0, 0, g)
                decays(0)
                turns(act, turn)

            @block.vector
            def _(dve):
                dve.wait_ge(loaded, 16 * LOADS)
                dve.wait_ge(consts, CONSTS)
                for j, (part, whole) in enumerate(parted):
                    dve.wait_ge(whi_ready, j + 1)
                    dve.tensor_tensor(part[:, 1], whole, part[:, 0], ALU.subtract).then_inc(wlo_ready, 1)
                dve.tensor_copy(laterr[:], later[:]).then_inc(wlo_ready, 1)
                dve.tensor_copy(wdt[:], win_raw.rearrange("p (k n) -> p k n", k=KD)[:, :, WIDE:PROJ]).then_inc(dve_own, 1)
                dve.wait_ge(dve_own, 1)
                dve.wait_ge(wlo_ready, len(parted) + 1)
                dve.memset(raw[:, 0, :, 0:HALO], 0.0).then_inc(dve_own, 1)
                dve.wait_ge(dve_own, 2)
                dve.wait_ge(setup, 1)
                dve.tensor_scalar(ah[:], E[:, 0, 0:NH], -1.0, None, ALU.mult).then_inc(setup, 1)
                for j in range(KI):
                    w = dve.tensor_scalar(wout[:, j], wout[:, j], nw[:, j:j + 1], None, ALU.mult)
                w.then_inc(setup, 1)
                dve.tensor_scalar(kept.reg0[:], kept.iota_e[:], float(REGION), None, ALU.mult)
                dve.tensor_scalar(place[:], kept.iota_e[:], float(REGION), None, ALU.mult).then_inc(setup, 1)
                dve.memset(x1[:, :, ODD:XW], 0.0)
                for j in range(2):
                    w = dve.tensor_scalar(x1[:, j, YROW:ODD], tok_p[:], float(TOPK), float((j - 2) * P * TOPK), ALU.mult, ALU.add)
                w.then_inc(setup, 1)
                dve.wait_ge(setup, 5)

                def conv(own, b, k, g):
                    dve.wait_ge(raw_in, met((b * 2 + k) * NG + g + 1))
                    if g == 0:
                        n = b * CH if k else (b - 1) * CH + QB
                        if not (isinstance(n, int) and n <= 0):
                            dve.wait_ge(y_made, met(n))
                            dve.wait_ge(g_made, met(n))
                    x = xc[:, k, g]
                    own.done(dve.tensor_scalar(x, raw[:, k, g, 0:BLK], cw[:, g, 0:1], cb[:, g:g + 1], ALU.mult, ALU.add))
                    for j in range(1, TAPS):
                        ins = dve.scalar_tensor_tensor(x, raw[:, k, g, j:j + BLK], cw[:, g, j:j + 1], x, ALU.mult, ALU.add)
                        if j < TAPS - 1:
                            own.done(ins)
                    ins.then_inc(conv_made, 1)

                v, na, e, r, r2, pl, m0, t0 = (dtw[:, j] for j in range(8))

                def dt_values(own, b):
                    dve.wait_ge(dt_proj, met(b + 1))
                    own.done(dve.tensor_tensor(v.rearrange("p (c h) -> p c h", c=CH),
                                               PX[:, 0:CH * NH].rearrange("p (c h) -> p c h", c=CH),
                                               bc(dtb[:], 1, [P, CH, NH]), ALU.add))
                    dve.scalar_tensor_tensor(na, v, -1.0, v, ALU.mult, ALU.min).then_inc(dt_abs, 1)
                    dve.tensor_scalar(m0, v, 0.0, None, ALU.max)

                def softplus(own, b):
                    dve.wait_ge(dt_exp, met(b + 1))
                    own.done(dve.tensor_scalar(t0, e, 2.0, None, ALU.add))
                    own.done(dve.reciprocal(t0, t0))
                    own.done(dve.tensor_tensor(r, e, t0, ALU.mult))
                    own.done(dve.tensor_tensor(r2, r, r, ALU.mult))
                    own.done(dve.tensor_scalar(pl, r2, 1.0 / 17, None, ALU.mult))
                    for odd in (15, 13, 11, 9, 7, 5, 3):
                        own.done(dve.scalar_tensor_tensor(pl, pl, 1.0 / odd, r2, ALU.add, ALU.mult))
                    own.done(dve.scalar_tensor_tensor(pl, pl, 1.0, r, ALU.add, ALU.mult))
                    own.done(dve.scalar_tensor_tensor(dts[:], pl, 2.0, m0, ALU.mult, ALU.add))
                    own.done(dve.tensor_tensor(dA[:].rearrange("p (c h) -> p c h", c=CH),
                                               dts[:].rearrange("p (c h) -> p c h", c=CH),
                                               bc(ah[:], 1, [P, CH, NH]), ALU.mult))
                    own.done(dve.tensor_copy(dAs[:, 0], dA[:]))
                    dve.tensor_tensor(dAs[:, 1], dA[:], dAs[:, 0], ALU.subtract).then_inc(dA_ready, 1)

                def u_lo(b, k):
                    dve.wait_ge(uhi_ready, met(b * 2 + k + 1))
                    dve.tensor_tensor(us[:, k, 1], uTb[:, k], us[:, k, 0], ALU.subtract).then_inc(ulo_ready, 1)

                def weigh_inputs(b):
                    dve.wait_ge(dec_ready, met(b + 1))
                    dve.wait_ge(xs_ready, met(b * CH))
                    dve.tensor_tensor(din[:], dec[:, 1], dts[:], ALU.mult).then_inc(din_ready, 1)

                def turn(b, more):
                    own = Steps(dve, dve_own, DVE_BASE + b * DVE_TURN)

                    def x1_lo(c):
                        dve.wait_ge(x1hi_ready, met(b * CH + c + 1))
                        dve.tensor_tensor(x1T[:, c % 2, 1].rearrange("p k t -> p (k t)"), PY[:, DM:2 * DM],
                                          x1T[:, c % 2, 0].rearrange("p k t -> p (k t)"), ALU.subtract).then_inc(x1lo_ready, 1)

                    def route(c):
                        dve.wait_ge(lg_made, met(b * CH + c + 1))
                        dve.wait_ge(rex_ready, met(b * CH + c))
                        own.done(dve.tensor_copy(lg[:], PY[:, 0:NE + 1]), apart=True)
                        own.done(dve.max(top[:], lg[:, 0:NE]))
                        dve.tensor_scalar(negm[:], top[:, 0:1], -1.0, None, ALU.mult).then_inc(lg_ready, 1)
                        own.done(dve.max_index(topi[:], top[:], lg[:, 0:NE]))
                        own.done(dve.tensor_copy(chf[:], topi[:, 0:TOPK]))
                        dve.tensor_copy(x1[:, c % 2, DM + TOPK:DM + 2 * TOPK], chf[:])
                        own.done(dve.tensor_tensor(oh[:], bc(kept.iota_e[:], 1, [P, TOPK, NE]),
                                                   bc(chf[:], 2, [P, TOPK, NE]), ALU.is_equal))
                        dve.tensor_reduce(mask[:], oh[:].rearrange("p k e -> p e k"), AX.X, ALU.add).then_inc(mask_ready, 1)

                    def weigh(c):
                        dve.wait_ge(rex_ready, met(b * CH + c + 1))
                        own.done(dve.reciprocal(rz[:], ez[:]))
                        dve.tensor_scalar(x1[:, c % 2, DM:DM + TOPK], e4[:], rz[:], None, ALU.mult)
                        own.done(dve.tensor_scalar(sg[:, 0:1], eg[:], 1.0, None, ALU.add))
                        own.done(dve.reciprocal(sg[:, 1:2], sg[:, 0:1]))

                    def give_slots(c):
                        dve.wait_ge(rank_made, met(b * CH + c + 1))
                        dve.wait_ge(rank_read, met(b * CH + c))
                        own.done(dve.tensor_tensor(rs[:], PO[:, RANK:RANK + NE], place[:], ALU.add))
                        own.done(dve.tensor_tensor(osl[:], oh[:], bc(rs[:], 1, [P, TOPK, NE]), ALU.mult))
                        dve.tensor_tensor(place[:], PO[:, TOT:TOT + NE], place[:], ALU.add).then_inc(rank_read, 1)
                        own.done(dve.tensor_reduce(slf[:], osl[:], AX.X, ALU.add))
                        dve.wait_ge(scattered[c % 2], primed((b * (CH // 2) + c // 2) * 16 * TOPK))
                        dve.tensor_copy(sloti[:, c % 2], slf[:]).then_inc(slot_ready, 1)

                    def hidden(c, s):
                        n = (b * CH + c) * NSL + s
                        dve.wait_ge(gs_ready, met(n + 1))
                        dve.wait_ge(hT_made, met(b * CH * NSL + max(c * NSL + s - 1, 0)))
                        dve.tensor_tensor(hb[:, s % 2], gs[:, s % 2], bank_of(("up", c, s), more)[:, FI:2 * FI],
                                          ALU.mult).then_inc(h_ready, 1)

                    for c in range(CH + 1):
                        n = b * CH + c
                        if c < CH:
                            dve.wait_ge(g_made, met(n + 1))
                            dve.tensor_tensor(gm[:], PG[:, 0:P], incl[:], ALU.mult).then_inc(gm_ready, 1)
                            if c:
                                x1_lo(c - 1)
                            dve.wait_ge(gm_ready, met(n + 1))
                            dve.wait_ge(y_made, met(n))
                            for h in range(NH):
                                if h % 4 == 0:
                                    dve.wait_ge(E_ready, met(2 * n + 1 + h // 4))
                                ins = dve.scalar_tensor_tensor(M[:, h], E[:, h], dts[:, c * NH + h:c * NH + h + 1], gm[:],
                                                               ALU.mult, ALU.mult)
                                if h % 4 == 3:
                                    ins.then_inc(M_ready, 1)
                        if more and c == CH:
                            dt_values(own, b + 1)
                            softplus(own, b + 1)
                        if c == CH:
                            x1_lo(c - 1)
                        if more and c == CH:
                            conv(own, b + 1, 0, c - QB - 1)
                        if c:
                            route(c - 1)
                            weigh(c - 1)
                            give_slots(c - 1)
                        if more and c == CH:
                            weigh_inputs(b + 1)
                        if more and c in (QB, CH):
                            u_lo(b + 1, c // QB - 1)
                        if 0 < c < CH:
                            dve.wait_ge(inter_made, met(b * (CH - 1) + c))
                            dve.tensor_tensor(heads(y1[:]), heads(PD[0][:]), over(dec[:, 0, at(c, NH)]),
                                              ALU.mult).then_inc(y1_ready, 1)
                        if c:
                            hidden(c - 1, 0)
                            hidden(c - 1, 1)
                        if c < CH:
                            dve.wait_ge(y_made, met(n + 1))
                            dve.wait_ge(y2_ready, met(n + 1))
                            own.done(dve.tensor_tensor(y1[:], PY[:], y2[:], ALU.add))
                            dve.wait_ge(zs_ready, met(n + 1))
                            dve.wait_ge(ygT_made, met(n))
                            dve.wait_ge(ss_ready, met(n))
                            dve.tensor_tensor(yg[:], y1[:], zs[:], ALU.mult).then_inc(yg_ready, 1)
                            if c:
                                dve.wait_ge(state_ready, met(n))
                                own.done(dve.tensor_tensor(heads(state[:]), heads(state[:]), over(dec[:, 2, at(c, NH)]), ALU.mult))
                                dve.wait_ge(st_made, met(n + 1))
                                dve.tensor_tensor(state[:], PD[1][:], state[:], ALU.add).then_inc(state_ready, 1)
                            else:
                                dve.wait_ge(st_made, met(n + 1))
                                dve.tensor_copy(state[:], PD[1][:]).then_inc(state_ready, 1)
                        if c:
                            if c < QB:
                                conv(own, b, 1, 2 * c - 2)
                            if more and c == CH:
                                conv(own, b + 1, 0, NG - 2)
                            hidden(c - 1, 2)
                            hidden(c - 1, 3)
                            if c < QB:
                                conv(own, b, 1, 2 * c - 1)
                            if more and QB < c < CH:
                                conv(own, b + 1, 0, c - QB - 1)
                            if more and c == CH:
                                conv(own, b + 1, 0, NG - 1)
                        if c < CH:
                            dve.wait_ge(o_made, met(n + 1))
                            dve.wait_ge(rms_ready, met(n + 1))
                            dve.wait_ge(u_in[c % 2], met((b * (CH // 2) + c // 2 + 1) * 16))
                            dve.scalar_tensor_tensor(res[:], PY[:, 0:DM], rms[:], ut[:, c % 2], ALU.mult,
                                                     ALU.add).then_inc(res_ready, 1)
                            dve.wait_ge(res_ready, met(n + 1))
                            own.done(dve.bn_stats(bst[:], res[:]), apart=True)
                            own.done(dve.bn_aggr(mv[:], bst[:]))
                            dve.tensor_scalar(vare[:], mv[:, 1:2], EPS, None, ALU.add).then_inc(var_ready, 1)
                            dve.wait_ge(std_ready, met(n + 1))
                            dve.wait_ge(scattered[c % 2], primed((b * (CH // 2) + c // 2) * 16 * TOPK))
                            dve.tensor_scalar(x1[:, c % 2, 0:DM], res[:], mv[:, 0:1], rstd[:], ALU.subtract,
                                              ALU.mult).then_inc(x1_ready, 1)
                            own.done(dve.tensor_scalar(x1[:, c % 2, YROW:ODD], x1[:, c % 2, YROW:ODD],
                                                       float(2 * P * TOPK), None, ALU.add))
                        if c:
                            dve.wait_ge(dn_made, met(n))
                            dve.wait_ge(x1_ready, met(n))
                            dve.wait_ge(acc_out[(c - 1) % 2], met((b * (CH // 2) + (c - 1) // 2) * 16))
                            dve.scalar_tensor_tensor(acc[:, (c - 1) % 2], PO[:, 0:DM], sg[:, 1:2], x1[:, (c - 1) % 2, 0:DM],
                                                     ALU.mult, ALU.add).then_inc(acc_ready, 1)
                    if more:
                        assert own.n == DVE_TURN, own.n

                front = Steps(dve, dve_own, 2)
                u_lo(0, 0)
                u_lo(0, 1)
                for g in range(NG):
                    conv(front, 0, 0, g)
                    if g == 1:
                        dt_values(front, 0)
                        softplus(front, 0)
                weigh_inputs(0)
                assert 2 + front.n == DVE_BASE, front.n
                turns(dve, turn)
                dve.wait_ge(scattered[0], primed(NC // 2 * TOPK * 16))
                dve.wait_ge(scattered[1], primed(NC // 2 * TOPK * 16))


def experts(nc, kept, up, down):
    pX, pU, pH, pO = (kept.banks[2 * j:2 * j + 2] for j in range(4))
    with ExitStack() as ctx:
        def sb(name, shape, dt=F32):
            return ctx.enter_context(nc.sbuf_tensor(name, shape, dt))

        def sem(name):
            return ctx.enter_context(nc.semaphore(name))

        UP, DOWN = KD * 2 * FI, 2 * DM
        STAGE = 3
        W = UP + DOWN
        we = sb("we", [P, 2, NE * W], F32R)
        raw = sb("raw_e", [P, STAGE, W])

        def split13(e):
            return we[:, 0, e * W:e * W + UP], we[:, 1, e * W:e * W + UP], raw[:, e % STAGE, 0:UP]

        def split2(e):
            return we[0:HF, 0, e * W + UP:(e + 1) * W], we[0:HF, 1, e * W + UP:(e + 1) * W], raw[0:HF, e % STAGE, UP:W]

        free = sb("free", [P, NE], I32)
        cnt = sb("cnt", [P, NE])
        cnti = sb("cnti", [P, NE], I32)
        tiles = sb("tiles", [P, NE])
        ones_e = sb("ones_e", [P, NE])
        ends = sb("ends", [P, NE])
        jump = sb("jump", [P, NE])
        tile_no = sb("tile_no", [P, TILES])
        past = sb("past", [P, TILES, NE])
        expert = sb("expert", [P, TILES])
        jumped = sb("jumped", [P, TILES])
        row = sb("row", [P, TILES])
        table = sb("table", [P, 2, TILES], I32)
        xr = sb("xr", [P, RING, XW])
        hit = sb("hit", [P, RING, TOPK])
        nth = sb("nth", [P, TOPK])
        pair = sb("pair", [P, RING, 2, TOPK])
        chosen = sb("chosen", [P, RING, 2])
        y_row = sb("y_row", [P, RING], I32)
        xT = sb("xT", [P, 2, 2, KD * P], F32R)
        gs = sb("gse", [P, 2, FI])
        hb = sb("hbe", [P, 2, FI])
        hT = sb("hTe", [HF, 2, 2, 2 * P], F32R)
        yo = sb("yo", [P, 2, DM])

        raw_in = [sem(f"raw_in{j}") for j in range(STAGE)]
        hi13_ready = sem("hi13_ready")
        hi2_ready = sem("hi2_ready")
        lo13_ready = sem("lo13_ready")
        lo2_ready = sem("lo2_ready")
        nums = sem("nums")
        own_sem = sem("layout_own")
        free_ready = sem("free_ready")
        padded = sem("padded")
        table_ready = sem("table_ready")
        x_in = [sem(f"x_in{j}") for j in range(RING)]
        picked = sem("picked")
        xT_made = sem("xT_made_e")
        xhi_ready = sem("xhi_ready")
        xlo_ready = sem("xlo_ready")
        u_made = sem("u_made")
        gs_ready = sem("gs_ready_e")
        h_ready = sem("h_ready_e")
        hT_made = sem("hT_made_e")
        hhi_ready = sem("hhi_ready")
        hlo_ready = sem("hlo_ready")
        d_made = sem("d_made")
        yo_ready = sem("yo_ready")
        scattered = [sem("scattered0_e"), sem("scattered1_e")]
        LAYOUT = 11

        def loads(turn, k):
            return (turn * (TURN // RING) + k // RING + 1) * 16

        def turns(eng, step):
            for k in range(TURN):
                step(k, k, 0, True)
            with eng.Fori(1, TILES // TURN) as i:
                for k in range(TURN):
                    step(TURN * i + k, k, i, False)

        with nc.Block() as block:
            @block.sync
            def _(sp):
                for e in range(NE):
                    if e >= STAGE:
                        sp.wait_ge(lo13_ready, e - STAGE + 1)
                        sp.wait_ge(lo2_ready, e - STAGE + 1)
                    sp.dma_start(raw[:, e % STAGE, 0:UP], up[:, e].rearrange("p k n -> p (k n)")).then_inc(raw_in[e % STAGE], 16)
                    sp.dma_start(raw[0:HF, e % STAGE, UP:W], down[:, e].rearrange("p k n -> p (k n)")).then_inc(raw_in[e % STAGE], 16)
                    sp.wait_ge(free_ready, 1)
                    at_row = sp.value_load(free[0:1, e:e + 1], min_val=0, max_val=NE * REGION - P)
                    sp.dma_start(kept.x_rows[bass.ds(at_row, P), :], kept.padrow[:]).then_inc(padded, 16)
                sp.wait_ge(table_ready, 2)
                sp.wait_ge(padded, NE * 16)

                def load(t, k, turn, first):
                    at_row = sp.value_load(table[0:1, 1, bass.ds(t, 1)], min_val=0, max_val=NE * REGION)
                    if not (first and k < RING):
                        sp.wait_ge(xT_made, t - RING + 1)
                        sp.wait_ge(picked, t - RING + 1)
                    sp.dma_start(xr[:, k % RING], kept.x_rows[bass.ds(at_row, P), :]).then_inc(x_in[k % RING], 16)

                turns(sp, load)

            @block.gpsimd
            def _(pool):
                pool.iota(tile_no[:], [[1, TILES]], base=0, channel_multiplier=0,
                          allow_small_or_imprecise_dtypes=True).then_inc(nums, 1)
                pool.memset(ones_e[:], 1.0).then_inc(nums, 1)
                pool.iota(nth[:], [[1, TOPK]], base=0, channel_multiplier=0,
                          allow_small_or_imprecise_dtypes=True).then_inc(nums, 1)
                prime(pool, kept, scattered)
                for e in range(NE):
                    pool.wait_ge(raw_in[e % STAGE], (e // STAGE + 1) * 32)
                    pool.wait_ge(hi2_ready, e + 1)
                    hi, lo, whole = split2(e)
                    pool.tensor_tensor(lo, whole, hi, ALU.subtract).then_inc(lo2_ready, 1)

                def scatter(t, k, turn, first):
                    r = k % RING
                    pool.wait_ge(yo_ready, t + 1)
                    waits_end(pool)
                    pool.indirect_dma_start(
                        kept.y_rows, bass.IndirectOffsetOnAxis(ap=y_row[:, r:r + 1].bitcast(U32), axis=0),
                        yo[:, k % 2], None).then_inc(scattered[k % 2], 16)

                turns(pool, scatter)
                pool.wait_ge(scattered[0], primed(TILES // 2 * 16))
                pool.wait_ge(scattered[1], primed(TILES // 2 * 16))

            @block.tensor
            def _(pe):
                pe.wait_ge(table_ready, 2)
                pe.wait_ge(lo13_ready, NE)
                pe.wait_ge(lo2_ready, NE)

                def columns_of(t):
                    return pe.value_load(table[0:1, 0, bass.ds(t, 1)], min_val=0, max_val=(NE - 1) * W)

                def product(out, x, rows, at_col, width, lo_ready, t):
                    def term(j, a, b, **flags):
                        return pe.matmul(out, x[:, a, j * P:(j + 1) * P], we[0:rows, b, bass.ds(at_col + j * width, width)], **flags)

                    for j in range(2):
                        term(j, 0, 0, start=j == 0, stop=False)
                        term(j, 0, 1, start=False, stop=False)
                    pe.wait_ge(lo_ready, t + 1)
                    term(0, 1, 0, start=False, stop=False)
                    return term(1, 1, 0, start=False, stop=True)

                def turn_rows(t, k, turn):
                    pe.wait_ge(x_in[k % RING], loads(turn, k))
                    for d in range(KD):
                        mm = pe.transpose(pX[k % 2][:, d * P:(d + 1) * P], xr[:, k % RING, d * P:(d + 1) * P], kept.ident[:])
                    mm.then_inc(xT_made, 1)

                def go_up(t, k, column):
                    pe.wait_ge(xhi_ready, t + 1)
                    product(pU[k % 2][:, 0:2 * FI], xT[:, k % 2], P, column, 2 * FI, xlo_ready, t).then_inc(u_made, 1)

                def turn_hidden(t, k):
                    pe.wait_ge(h_ready, t + 1)
                    for j in range(2):
                        mm = pe.transpose(pH[k % 2][0:HF, j * P:(j + 1) * P], hb[:, k % 2, j * HF:(j + 1) * HF], kept.ident[:])
                    mm.then_inc(hT_made, 1)

                def go_down(t, k, column, first=False):
                    pe.wait_ge(hhi_ready, t + 1)
                    if not first:
                        pe.wait_ge(yo_ready, t - 1)
                    product(pO[k % 2][:, 0:DM], hT[:, k % 2], HF, column + UP, DM, hlo_ready, t).then_inc(d_made, 1)

                turn_rows(0, 0, 0)
                at = {}
                for k in range(TURN):
                    at[k] = columns_of(k)
                    go_up(k, k, at[k])
                    if k >= 1:
                        turn_hidden(k - 1, k - 1)
                    turn_rows(k + 1, k + 1, 0)
                    if k >= 2:
                        go_down(k - 2, k - 2, at[k - 2], first=k < 4)

                def steps(turn, last):
                    at = {0: columns_of(TURN * turn)}
                    for k in range(TURN):
                        t = TURN * turn + k
                        go_up(t, k, at[k])
                        if k == 0:
                            at[-2] = columns_of(t - 2)
                        turn_hidden(t - 1, k - 1)
                        if not (last and k == TURN - 1):
                            turn_rows(t + 1, k + 1, turn)
                        if k == 0:
                            at[-1] = columns_of(t - 1)
                        go_down(t - 2, k - 2, at[k - 2])
                        if k < TURN - 1:
                            at[k + 1] = columns_of(t + 1)
                    return at

                with pe.Fori(1, TILES // TURN - 1) as turn:
                    steps(turn, False)
                at = steps(TILES // TURN - 1, True)
                turn_hidden(TILES - 1, TURN - 1)
                go_down(TILES - 2, TURN - 2, at[TURN - 2])
                go_down(TILES - 1, TURN - 1, at[TURN - 1])

            @block.scalar
            def _(act):
                def copy_rows(t, k):
                    act.wait_ge(xT_made, t + 1)
                    act.copy(xT[:, k % 2, 0], pX[k % 2][:, 0:DM]).then_inc(xhi_ready, 1)

                def copy_hidden(t, k, first=False):
                    act.wait_ge(hT_made, t + 1)
                    if not first:
                        act.wait_ge(d_made, t - 1)
                    act.copy(hT[:, k % 2, 0], pH[k % 2][0:HF, 0:2 * P]).then_inc(hhi_ready, 1)

                def gate(t, k):
                    act.wait_ge(u_made, t + 1)
                    act.activation(gs[:, k % 2], pU[k % 2][:, 0:FI], ACT.Silu).then_inc(gs_ready, 1)

                def emit(t, k, before=None):
                    act.wait_ge(picked, t + 1)
                    act.wait_ge(d_made, t + 1)
                    if before is not None:
                        act.wait_ge(scattered[k % 2], primed(before * 16))
                    act.activation(yo[:, k % 2], pO[k % 2][:, 0:DM], ACT.Copy, scale=chosen[:, k % RING, 0:1]).then_inc(yo_ready, 1)

                for e in range(NE):
                    act.wait_ge(raw_in[e % STAGE], (e // STAGE + 1) * 32)
                    for (hi, _, whole), ready in ((split13(e), hi13_ready), (split2(e), hi2_ready)):
                        act.copy(hi, whole).then_inc(ready, 1)
                copy_rows(0, 0)
                for k in range(TURN):
                    gate(k, k)
                    if k >= 1:
                        copy_hidden(k - 1, k - 1, first=k < 3)
                    copy_rows(k + 1, k + 1)
                    if k >= 2:
                        emit(k - 2, k - 2, k // 2 - 1 if k >= 4 else None)

                def steps(turn, last):
                    for k in range(TURN):
                        t = TURN * turn + k
                        gate(t, k)
                        copy_hidden(t - 1, k - 1)
                        if not (last and k == TURN - 1):
                            copy_rows(t + 1, k + 1)
                        emit(t - 2, k - 2, TURN // 2 * turn - 1 + k // 2)

                with act.Fori(1, TILES // TURN - 1) as turn:
                    steps(turn, False)
                steps(TILES // TURN - 1, True)
                copy_hidden(TILES - 1, TURN - 1)
                emit(TILES - 2, TURN - 2, TILES // 2 - 1)
                emit(TILES - 1, TURN - 1, TILES // 2 - 1)

            @block.vector
            def _(dve):
                own = Steps(dve, own_sem)
                dve.wait_ge(nums, 3)
                dve.tensor_copy(free[:], kept.place[:]).then_inc(free_ready, 1)

                def lo_weights(experts_of):
                    for e in experts_of:
                        dve.wait_ge(raw_in[e % STAGE], (e // STAGE + 1) * 32)
                        dve.wait_ge(hi13_ready, e + 1)
                        hi, lo, whole = split13(e)
                        dve.tensor_tensor(lo, whole, hi, ALU.subtract).then_inc(lo13_ready, 1)

                own.done(dve.tensor_tensor(cnt[:], kept.place[:], kept.reg0[:], ALU.subtract))
                own.done(dve.tensor_scalar(cnti[:], cnt[:], float(P - 1), None, ALU.add))
                own.done(dve.tensor_scalar(cnti[:], cnti[:], 7, None, ALU.arith_shift_right))
                own.done(dve.tensor_copy(tiles[:], cnti[:]))
                own.done(dve.tensor_tensor_scan(ends[:], ones_e[:], tiles[:], 0.0, ALU.mult, ALU.add))
                own.done(dve.tensor_scalar(jump[:], tiles[:], -float(P), float(REGION), ALU.mult, ALU.add))
                lo_weights(range(0, 2))
                own.done(dve.tensor_tensor(past[:], bc(tile_no[:], 2, [P, TILES, NE]), bc(ends[:], 1, [P, TILES, NE]), ALU.is_ge))
                lo_weights(range(2, 4))
                own.done(dve.tensor_reduce(expert[:], past[:], AX.X, ALU.add))
                lo_weights(range(4, 6))
                own.done(dve.tensor_tensor(past[:], past[:], bc(jump[:], 1, [P, TILES, NE]), ALU.mult))
                lo_weights(range(6, 8))
                own.done(dve.tensor_reduce(jumped[:], past[:], AX.X, ALU.add))
                own.done(dve.scalar_tensor_tensor(row[:], tile_no[:], float(P), jumped[:], ALU.mult, ALU.add))
                dve.tensor_scalar(table[:, 0], expert[:], float(NE - 1), float(W), ALU.min, ALU.mult).then_inc(table_ready, 1)
                dve.tensor_scalar(table[:, 1], row[:], float(NE * REGION), None, ALU.min).then_inc(table_ready, 1)
                assert own.n == LAYOUT, own.n
                lo_weights(range(8, NE))

                def lo_rows(t, k):
                    dve.wait_ge(xhi_ready, t + 1)
                    dve.tensor_tensor(xT[:, k % 2, 1], pX[k % 2][:, 0:DM], xT[:, k % 2, 0], ALU.subtract).then_inc(xlo_ready, 1)

                def lo_hidden(t, k):
                    dve.wait_ge(hhi_ready, t + 1)
                    dve.tensor_tensor(hT[:, k % 2, 1], pH[k % 2][0:HF, 0:2 * P], hT[:, k % 2, 0], ALU.subtract).then_inc(hlo_ready, 1)

                def pick(t, k, turn, n):
                    r = k % RING
                    dve.wait_ge(x_in[r], loads(turn, k))
                    dve.tensor_tensor(hit[:, r], xr[:, r, DM + TOPK:DM + 2 * TOPK],
                                      expert[:, bass.ds(t, 1)].to_broadcast([P, TOPK]), ALU.is_equal).then_inc(own_sem, 1)
                    dve.wait_ge(own_sem, n + 1)
                    dve.tensor_tensor(pair[:, r, 0], hit[:, r], xr[:, r, DM:DM + TOPK], ALU.mult)
                    dve.tensor_tensor(pair[:, r, 1], hit[:, r], nth[:], ALU.mult).then_inc(own_sem, 1)
                    dve.wait_ge(own_sem, n + 2)
                    dve.tensor_reduce(chosen[:, r], pair[:, r], AX.X, ALU.add).then_inc(own_sem, 1)
                    dve.wait_ge(own_sem, n + 3)
                    if k % 2 == 0:
                        dve.tensor_tensor(y_row[:, r:r + 1], xr[:, r, YROW:ODD], chosen[:, r, 1:2], ALU.add).then_inc(picked, 1)
                    else:
                        dve.scalar_tensor_tensor(y_row[:, r:r + 1], xr[:, r, YROW:ODD], chosen[:, r, 1:2], xr[:, r, ODD:XW],
                                                 ALU.add, ALU.add).then_inc(picked, 1)

                def hide(t, k):
                    dve.wait_ge(gs_ready, t + 1)
                    dve.tensor_tensor(hb[:, k % 2], gs[:, k % 2], pU[k % 2][:, FI:2 * FI], ALU.mult).then_inc(h_ready, 1)

                lo_rows(0, 0)
                for k in range(TURN):
                    hide(k, k)
                    if k >= 1:
                        lo_hidden(k - 1, k - 1)
                    lo_rows(k + 1, k + 1)
                    pick(k, k, 0, LAYOUT + 3 * k)

                def steps(turn, last):
                    for k in range(TURN):
                        t = TURN * turn + k
                        hide(t, k)
                        lo_hidden(t - 1, k - 1)
                        if not (last and k == TURN - 1):
                            lo_rows(t + 1, k + 1)
                        pick(t, k, turn, LAYOUT + 3 * t)

                with dve.Fori(1, TILES // TURN - 1) as turn:
                    steps(turn, False)
                steps(TILES // TURN - 1, True)
                lo_hidden(TILES - 1, TURN - 1)


def combine(nc, kept, out):
    TB = 4
    NB = NC // TB
    with ExitStack() as ctx:
        def sb(name, shape, dt=F32):
            return ctx.enter_context(nc.sbuf_tensor(name, shape, dt))

        def sem(name):
            return ctx.enter_context(nc.semaphore(name))

        IN = 3
        ys = sb("ys", [P, IN, TB, TOPK, DM])
        xb = sb("xb", [P, IN, TB, DM])
        sm = sb("sm", [P, 2, TB, DM])
        bst = sb("bst_c", [P, 2, TB, 6])
        mv = sb("mv_c", [P, 2, TB, 2])
        vare = sb("vare_c", [P, 2, TB])
        rstd = sb("rstd_c", [P, 2, TB])
        shift = sb("shift", [P, 2, TB])
        res = sb("res_c", [P, 2, TB, DM])

        ys_in = [sem(f"ys_in{j}") for j in range(IN)]
        xb_in = [sem(f"xb_in{j}") for j in range(IN)]
        pairs_ready = sem("pairs_ready")
        four_ready = sem("four_ready")
        sum_ready = sem("sum_ready")
        stats_ready = sem("stats_ready")
        var_ready = sem("var_ready_c")
        std_ready = sem("std_ready_c")
        shift_ready = sem("shift_ready")
        res_ready = sem("res_ready_c")
        written = [sem("written0"), sem("written1")]

        def block_rows(t, i, each):
            n = TB * P * each
            return t[i * n:(i + 1) * n, :].rearrange("(p j) d -> p j d", p=P)

        with nc.Block() as block:
            @block.sync
            def _(sp):
                for i in range(NB):
                    if i >= IN:
                        sp.wait_ge(sum_ready, i - IN + 1)
                    sp.dma_start(ys[:, i % IN].rearrange("p t k d -> p (t k) d"),
                                 block_rows(kept.y_rows, i, TOPK)).then_inc(ys_in[i % IN], 16)
                    sp.dma_start(xb[:, i % IN], block_rows(kept.base, i, 1)).then_inc(xb_in[i % IN], 16)
                for j in range(2):
                    sp.wait_ge(written[j], NB // 2 * 16)

            @block.vector
            def _(dve):
                def add_four(i):
                    y = ys[:, i % IN]
                    dve.wait_ge(ys_in[i % IN], (i // IN + 1) * 16)
                    dve.tensor_tensor(y[:, :, 0:2], y[:, :, 0:2], y[:, :, 2:4], ALU.add).then_inc(pairs_ready, 1)
                    dve.wait_ge(pairs_ready, i + 1)
                    dve.tensor_tensor(y[:, :, 0], y[:, :, 0], y[:, :, 1], ALU.add).then_inc(four_ready, 1)

                def stats(i):
                    dve.wait_ge(sum_ready, i + 1)
                    for j in range(TB):
                        s = dve.bn_stats(bst[:, i % 2, j], sm[:, i % 2, j])
                    s.then_inc(stats_ready, 1)
                    dve.wait_ge(stats_ready, 2 * i + 1)
                    for j in range(TB):
                        s = dve.bn_aggr(mv[:, i % 2, j], bst[:, i % 2, j])
                    s.then_inc(stats_ready, 1)
                    dve.wait_ge(stats_ready, 2 * i + 2)
                    dve.tensor_scalar(vare[:, i % 2], mv[:, i % 2, :, 1], EPS, None, ALU.add).then_inc(var_ready, 1)

                def finish(i):
                    dve.wait_ge(std_ready, i + 1)
                    if i >= 2:
                        dve.wait_ge(res_ready, i - 1)
                    dve.scalar_tensor_tensor(shift[:, i % 2], mv[:, i % 2, :, 0], -1.0, rstd[:, i % 2], ALU.mult,
                                             ALU.mult).then_inc(shift_ready, 1)

                for i in range(NB):
                    add_four(i)
                    if i:
                        stats(i - 1)
                        finish(i - 1)
                stats(NB - 1)
                finish(NB - 1)

            @block.gpsimd
            def _(pool):
                for i in range(NB):
                    pool.wait_ge(four_ready, i + 1)
                    pool.wait_ge(xb_in[i % IN], (i // IN + 1) * 16)
                    if i >= 2:
                        pool.wait_ge(res_ready, i - 1)
                    pool.tensor_tensor(sm[:, i % 2], ys[:, i % IN, :, 0], xb[:, i % IN], ALU.add).then_inc(sum_ready, 1)
                    pool.wait_ge(var_ready, i + 1)
                    pool.tensor_tensor(rstd[:, i % 2], vare[:, i % 2], kept.half[:].to_broadcast([P, TB]),
                                       ALU.pow).then_inc(std_ready, 1)

            @block.scalar
            def _(act):
                for i in range(NB):
                    act.wait_ge(shift_ready, i + 1)
                    if i >= 2:
                        act.wait_ge(written[i % 2], i // 2 * 16)
                    for j in range(TB):
                        r = act.activation(res[:, i % 2, j], sm[:, i % 2, j], ACT.Identity, bias=shift[:, i % 2, j:j + 1],
                                           scale=rstd[:, i % 2, j:j + 1])
                    r.then_inc(res_ready, 1)
                    act.wait_ge(res_ready, i + 1)
                    act.dma_start(block_rows(out, i, 1), res[:, i % 2]).then_inc(written[i % 2], 16)


def kernel(**inputs):
    import numpy as np
    from concourse import bacc
    from concourse.bass_utils import run_bass_kernel_spmd

    a = {k: np.asarray(v) for k, v in inputs.items()}

    def halves(w, p):
        return w.T.reshape(w.shape[1] // p, p, w.shape[0]).transpose(1, 0, 2)

    tokens = BATCH * SEQ
    u = a["L0_attn_u"].reshape(tokens, DM)
    f = NSL * FI
    sgu = a["L0_ffn_shared_gate_up_w"]
    ups = [*a["L0_ffn_w13"]] + [np.concatenate([sgu[s * FI:(s + 1) * FI], sgu[f + s * FI:f + (s + 1) * FI]]) for s in range(NSL)]
    downs = [*a["L0_ffn_w2"]] + [a["L0_ffn_shared_down_w"][:, s * FI:(s + 1) * FI] for s in range(NSL)]
    laid = {
        "uT": halves(u, P),
        "u": u,
        "w_in": halves(a["L0_attn_W_in"], P),
        "conv_w": a["L0_attn_conv_w"].reshape(NG, P, TAPS).transpose(1, 0, 2),
        "conv_b": a["L0_attn_conv_b"].reshape(NG, P).T,
        "dt_bias": np.broadcast_to(a["L0_attn_dt_bias"], (P, NH)),
        "a_log": np.broadcast_to(a["L0_attn_A_log"], (P, NH)),
        "d_skip": np.broadcast_to(a["L0_attn_D"], (P, NH)),
        "norm_w": a["L0_attn_norm_w"].reshape(KI, P).T,
        "w_out": halves(a["L0_attn_W_out"], P),
        "gate": halves(np.concatenate([a["L0_ffn_gate_w"], a["L0_ffn_sgate_w"], np.zeros((GATES - NE - 1, DM), np.float32)]), P),
        "up": np.stack([halves(w, P) for w in ups], axis=1),
        "down": np.stack([halves(w, HF) for w in downs], axis=1),
    }
    nc = bacc.Bacc("TRN2", target_bir_lowering=False, num_devices=1)
    arrays = {f"in_{k}": np.ascontiguousarray(v) for k, v in laid.items()}
    args = [nc.dram_tensor(k, v.shape, F32, kind="ExternalInput").ap() for k, v in arrays.items()]
    out = nc.dram_tensor("out_dram", (tokens, DM), F32, kind="ExternalOutput").ap()
    build(nc, *args, out)
    r = run_bass_kernel_spmd(nc, [arrays], core_ids=[0])
    return r.results[0]["out_dram"].reshape(BATCH, SEQ, DM)
```
